# Optimizing a Trainium2 kernel written in Bass

```python
import numpy as np
import jax
import jax.numpy as jnp

def _softmax(x, axis=-1):
    return jax.nn.softmax(x, axis=axis)

def _gelu(x):
    return jax.nn.gelu(x, approximate=True)

def _silu(x):
    return jax.nn.silu(x)

def _sigmoid(x):
    return jax.nn.sigmoid(x)

def _layernorm(x, axis=-1, eps=1e-05):
    m = jnp.mean(x, axis=axis, keepdims=True)
    v = jnp.var(x, axis=axis, keepdims=True)
    return (x - m) / jnp.sqrt(v + eps)

def _scatter_add(tgt, idx, src, axis=0):
    return tgt.at[idx].add(src)

def _segment_sum(src, seg, n):
    return jax.ops.segment_sum(src, seg, n)
kernel_name = 'mk_flamingo_gated_d4_seqx_r4_97d81c'

def setup_inputs(seed: int=0):
    np.random.seed(seed)
    _w = jnp.asarray

    def _rec_inputs():
        import jax
        import jax.numpy as jnp
        _rk = jax.random.key(seed)
        x = 7.22e-05 + 1 * jax.random.normal(jax.random.fold_in(_rk, 1), (16, 112, 256), jnp.float32)
        _lenS = 112 - jax.random.randint(jax.random.fold_in(_rk, 7), (16,), 0, max(1, 112 // 4) + 1, jnp.int32)
        _lenS2 = 375 - jax.random.randint(jax.random.fold_in(_rk, 8), (16,), 0, max(1, 375 // 4) + 1, jnp.int32)
        _ctx_1024P = jax.random.normal(jax.random.fold_in(_rk, 11), (16, 16, 256), jnp.float32)
        _ctx_1024c = jax.random.dirichlet(jax.random.fold_in(_rk, 511), 0.3 * jnp.ones((16,), jnp.float32), (16, 375))
        _ctx_1024t = jnp.einsum('bsk,bkd->bsd', _ctx_1024c, _ctx_1024P)
        _ctx_1024t = _ctx_1024t * jax.lax.rsqrt(jnp.mean(jnp.square(_ctx_1024t)) + 1e-12) * 0.953939
        ctx_1024 = 4.13588e-05 + 0.999923 * (_ctx_1024t + 0.3 * jax.random.normal(jax.random.fold_in(_rk, 611), (16, 375, 256), jnp.float32))
        _validS = jnp.arange(112)[None, :] < _lenS[:, None]
        _validS2 = jnp.arange(375)[None, :] < _lenS2[:, None]
        _causal = jnp.tril(jnp.ones((112, 112), dtype=bool))
        mask_1x1xSxS_fk0 = jnp.where(jnp.broadcast_to(_validS[0:1, None, None, :], (1, 1, 112, 112)), 0.0, 1.0).astype(jnp.float32)
        mask_Bx1x1xS_ff1 = jnp.where(jnp.ones((16, 1, 1, 112), dtype=bool), 1.0, 0.0).astype(jnp.float32)
        mask_Bx1xSxS2_if1 = jnp.where(jnp.ones((16, 1, 112, 375), dtype=bool), 1, 0).astype(jnp.int32)
        mask_BxS2_if1 = jnp.where(jnp.ones((16, 375), dtype=bool), 1, 0).astype(jnp.int32)
        _g = jax.random.normal(jax.random.fold_in(_rk, 9001), (2, 4), jnp.float32)
        _g = jnp.sign(_g) * jnp.maximum(jnp.abs(_g), 1.0) + (_g == 0) * 1.0
        g_xattn = _g[0]
        g_ffn = _g[1]
        return (x, ctx_1024, mask_1x1xSxS_fk0, mask_Bx1x1xS_ff1, mask_Bx1xSxS2_if1, mask_BxS2_if1, g_xattn, g_ffn)
    x, ctx_1024, mask_1x1xSxS_fk0, mask_Bx1x1xS_ff1, mask_Bx1xSxS2_if1, mask_BxS2_if1, g_xattn, g_ffn = _rec_inputs()

    def _L0_xattn_setup():
        import jax, jax.numpy as jnp
        import numpy as np
        D_MODEL = 256
        NUM_HEADS = 16
        D_K = D_MODEL // NUM_HEADS

        def _split_heads(x):
            B, S, _ = x.shape
            return x.reshape(B, S, NUM_HEADS, D_K).transpose(0, 2, 1, 3)
        key = jax.random.key(seed)
        ks = jax.random.split(key, 11)
        B, S = (4, 512)
        s = 1.0 / np.sqrt(D_MODEL)
        return {'query': jax.random.normal(ks[0], (B, S, D_MODEL), jnp.float32), 'key': jax.random.normal(ks[1], (B, S, D_MODEL), jnp.float32), 'value': jax.random.normal(ks[2], (B, S, D_MODEL), jnp.float32), 'Wq': jax.random.normal(ks[3], (D_MODEL, D_MODEL), jnp.float32) * s, 'bq': jnp.zeros((D_MODEL,), jnp.float32), 'Wk': jax.random.normal(ks[4], (D_MODEL, D_MODEL), jnp.float32) * s, 'bk': jnp.zeros((D_MODEL,), jnp.float32), 'Wv': jax.random.normal(ks[5], (D_MODEL, D_MODEL), jnp.float32) * s, 'bv': jnp.zeros((D_MODEL,), jnp.float32), 'Wo': jax.random.normal(ks[6], (D_MODEL, D_MODEL), jnp.float32) * s, 'bo': jnp.zeros((D_MODEL,), jnp.float32)}
    _L0_xattn_all = _L0_xattn_setup()
    _L0_xattn_in = {k: v for k, v in _L0_xattn_all.items() if k in ('Wq', 'bq', 'Wk', 'bk', 'Wv', 'bv', 'Wo', 'bo')}
    del _L0_xattn_all

    def _L0_ffn_setup():
        import jax, jax.numpy as jnp
        import numpy as np
        D_MODEL = 256
        D_FF = 704
        N_EXPERTS = 8
        key = jax.random.key(seed)
        k_in, k1, k2, k3 = jax.random.split(key, 4)
        scale = 0.02
        inputs = jax.random.normal(k_in, (4, N_EXPERTS * 512, D_MODEL), dtype=jnp.float32)
        w1 = jax.random.normal(k1, (N_EXPERTS, D_MODEL, D_FF), dtype=jnp.float32) * scale
        w3 = jax.random.normal(k3, (N_EXPERTS, D_MODEL, D_FF), dtype=jnp.float32) * scale
        w2 = jax.random.normal(k2, (N_EXPERTS, D_FF, D_MODEL), dtype=jnp.float32) * scale
        return {'inputs': inputs, 'w1': w1, 'w3': w3, 'w2': w2}
    _L0_ffn_all = _L0_ffn_setup()
    _L0_ffn_in = {k: v for k, v in _L0_ffn_all.items() if k in ('w1', 'w3', 'w2')}
    del _L0_ffn_all

    def _L1_xattn_setup():
        import jax, jax.numpy as jnp
        import numpy as np
        import math
        B, T, S, C, H = (2, 512, 512, 256, 16)
        D = C // H

        def _proj_heads(x, W, b):
            y = x @ W.T + b
            Bv, L, _ = y.shape
            return y.reshape(Bv, L, H, D).transpose(0, 2, 1, 3)
        key = jax.random.key(seed)
        ks = jax.random.split(key, 12)
        s = 1.0 / math.sqrt(C)
        inp = {'query': jax.random.normal(ks[0], (B, T, C), jnp.float32), 'key': jax.random.normal(ks[1], (B, S, C), jnp.float32), 'value': jax.random.normal(ks[2], (B, S, C), jnp.float32), 'Wq': jax.random.normal(ks[3], (C, C), jnp.float32) * s, 'bq': jax.random.normal(ks[4], (C,), jnp.float32) * s, 'Wk': jax.random.normal(ks[5], (C, C), jnp.float32) * s, 'bk': jax.random.normal(ks[6], (C,), jnp.float32) * s, 'Wv': jax.random.normal(ks[7], (C, C), jnp.float32) * s, 'bv': jax.random.normal(ks[8], (C,), jnp.float32) * s, 'Wo': jax.random.normal(ks[9], (C, C), jnp.float32) * s, 'bo': jax.random.normal(ks[10], (C,), jnp.float32) * s, 'query_chunk_size': 256}
        return inp
    _L1_xattn_all = _L1_xattn_setup()
    _L1_xattn_in = {k: v for k, v in _L1_xattn_all.items() if k in ('Wq', 'bq', 'Wk', 'bk', 'Wv', 'bv', 'Wo', 'bo')}
    del _L1_xattn_all

    def _L1_ffn_setup():
        import jax, jax.numpy as jnp
        import numpy as np
        E = 8
        TOPK = 2
        SCALE = 2.0
        key = jax.random.key(seed)
        ks = jax.random.split(key, 12)
        B, S, D, F, R = (2, 128, 256, 1024, 16)
        w = lambda k, shp: jax.random.normal(k, shp, dtype=jnp.float32) * 0.02
        return {'hidden_states': jax.random.normal(ks[0], (B, S, D), dtype=jnp.float32), 'gate_w': w(ks[1], (E, D)), 'w_gate': w(ks[2], (F, D)), 'w_up': w(ks[3], (F, D)), 'w_down': w(ks[4], (D, F)), 'A1': w(ks[5], (E, R, D)), 'B1': w(ks[6], (E, F, R)), 'A3': w(ks[7], (E, R, D)), 'B3': w(ks[8], (E, F, R)), 'A2': w(ks[9], (E, R, F)), 'B2': w(ks[10], (E, D, R))}
    _L1_ffn_all = _L1_ffn_setup()
    _L1_ffn_in = {k: v for k, v in _L1_ffn_all.items() if k in ('gate_w', 'w_gate', 'w_up', 'w_down', 'A1', 'B1', 'A3', 'B3', 'A2', 'B2')}
    del _L1_ffn_all

    def _L2_xattn_setup():
        import jax, jax.numpy as jnp
        import numpy as np
        B, S, D, H, DFF = (4, 512, 256, 16, 1024)
        DEPTH = D // H
        EPS = 1e-06

        def _ln(x, g, b):
            m = jnp.mean(x, axis=-1, keepdims=True)
            v = jnp.mean(jnp.square(x - m), axis=-1, keepdims=True)
            return (x - m) * jax.lax.rsqrt(v + EPS) * g + b

        def _mha(q_in, k_in, v_in, wq, bq, wk, bk, wv, bv, wo, bo, mask=None):
            b = q_in.shape[0]

            def heads(t):
                return t.reshape(b, -1, H, DEPTH).transpose(0, 2, 1, 3)
            q = heads(q_in @ wq + bq)
            k = heads(k_in @ wk + bk)
            v = heads(v_in @ wv + bv)
            scores = jnp.einsum('bhqd,bhkd->bhqk', q, k) / jnp.sqrt(jnp.float32(DEPTH))
            if mask is not None:
                scores = scores + mask * -1000000000.0
            attn = jax.nn.softmax(scores, axis=-1)
            out = jnp.einsum('bhqk,bhkd->bhqd', attn, v)
            out = out.transpose(0, 2, 1, 3).reshape(b, -1, D)
            return out @ wo + bo
        key = jax.random.key(seed)
        ks = jax.random.split(key, 32)

        def dense(i, fan_in, fan_out):
            w = jax.random.normal(ks[i], (fan_in, fan_out), jnp.float32) / np.sqrt(fan_in)
            return (w, jnp.zeros((fan_out,), jnp.float32))
        inp = {}
        inp['x'] = jax.random.normal(ks[0], (B, S, D), jnp.float32)
        inp['enc_output'] = jax.random.normal(ks[1], (B, S, D), jnp.float32)
        inp['attention_mask'] = jnp.tril(jnp.ones((S, S), jnp.float32))[None, None]
        inp['padding_mask'] = jnp.ones((B, 1, 1, S), jnp.float32)
        names = ['wq1', 'wk1', 'wv1', 'wo1', 'wq2', 'wk2', 'wv2', 'wo2']
        for j, n in enumerate(names):
            w, bb = dense(2 + j, D, D)
            inp[n] = w
            inp['b' + n[1:]] = bb
        inp['w_ff1'], inp['b_ff1'] = dense(10, D, DFF)
        inp['w_ff2'], inp['b_ff2'] = dense(11, DFF, D)
        for i in (1, 2, 3):
            inp[f'g{i}'] = jnp.ones((D,), jnp.float32)
            inp[f'be{i}'] = jnp.zeros((D,), jnp.float32)
        return inp
    _L2_xattn_all = _L2_xattn_setup()
    _L2_xattn_in = {k: v for k, v in _L2_xattn_all.items() if k in ('wq1', 'bq1', 'wk1', 'bk1', 'wv1', 'bv1', 'wo1', 'bo1', 'wq2', 'bq2', 'wk2', 'bk2', 'wv2', 'bv2', 'wo2', 'bo2', 'w_ff1', 'b_ff1', 'w_ff2', 'b_ff2', 'g1', 'be1', 'g2', 'be2', 'g3', 'be3')}
    del _L2_xattn_all

    def _L2_ffn_setup():
        import jax, jax.numpy as jnp
        import numpy as np
        B, T, D = (2, 512, 256)
        DCD = 1024
        RET = 128
        NEXP = 1024
        NKEYS = 64
        H = 4
        KPH = 8
        key = jax.random.key(seed)
        ks = jax.random.split(key, 10)
        s = lambda k, shape, scale: jax.random.normal(k, shape, jnp.float32) * scale
        return {'hidden_states': jax.random.normal(ks[0], (B, T, D), jnp.float32), 'Wg': s(ks[1], (D, DCD), 0.02), 'bg': jnp.zeros((DCD,), jnp.float32), 'Wu': s(ks[2], (D, DCD), 0.02), 'bu': jnp.zeros((DCD,), jnp.float32), 'Wd': s(ks[3], (DCD, D), 0.02), 'bd': jnp.zeros((D,), jnp.float32), 'Wq': s(ks[4], (D, RET * H), 0.02), 'keys': s(ks[5], (H, NKEYS, 2, RET // 2), 0.02), 'down_embed': s(ks[6], (NEXP, D), 0.02), 'up_embed': s(ks[7], (NEXP, D), 0.02)}
    _L2_ffn_all = _L2_ffn_setup()
    _L2_ffn_in = {k: v for k, v in _L2_ffn_all.items() if k in ('Wg', 'bg', 'Wu', 'bu', 'Wd', 'bd', 'Wq', 'keys', 'down_embed', 'up_embed')}
    del _L2_ffn_all

    def _L3_xattn_setup():
        import jax, jax.numpy as jnp
        import numpy as np
        import math
        D_MODEL = 256
        N_HEADS = 16
        HEAD_DIM = D_MODEL // N_HEADS
        B, S = (4, 512)
        key = jax.random.key(seed)
        ks = jax.random.split(key, 12)
        s = 1.0 / math.sqrt(D_MODEL)
        inp = {'query': jax.random.normal(ks[0], (B, S, D_MODEL), jnp.float32), 'key': jax.random.normal(ks[1], (B, S, D_MODEL), jnp.float32), 'value': jax.random.normal(ks[2], (B, S, D_MODEL), jnp.float32), 'mask': jnp.ones((B, 1, S, S), jnp.int32), 'key_padding_mask': jnp.ones((B, S), jnp.int32), 'Wq': jax.random.normal(ks[3], (D_MODEL, D_MODEL), jnp.float32) * s, 'bq': jax.random.normal(ks[4], (D_MODEL,), jnp.float32) * s, 'Wk': jax.random.normal(ks[5], (D_MODEL, D_MODEL), jnp.float32) * s, 'bk': jax.random.normal(ks[6], (D_MODEL,), jnp.float32) * s, 'Wv': jax.random.normal(ks[7], (D_MODEL, D_MODEL), jnp.float32) * s, 'bv': jax.random.normal(ks[8], (D_MODEL,), jnp.float32) * s, 'Wo': jax.random.normal(ks[9], (D_MODEL, D_MODEL), jnp.float32) * s, 'bo': jax.random.normal(ks[10], (D_MODEL,), jnp.float32) * s}
        return inp
    _L3_xattn_all = _L3_xattn_setup()
    _L3_xattn_in = {k: v for k, v in _L3_xattn_all.items() if k in ('Wq', 'bq', 'Wk', 'bk', 'Wv', 'bv', 'Wo', 'bo')}
    del _L3_xattn_all

    def _L3_ffn_setup():
        import jax, jax.numpy as jnp
        import numpy as np
        E, K = (8, 2)
        B, S, H, F = (2, 512, 256, 1024)
        EPS = 1e-12

        def _expert_ffn(xf, Wi_e, bi_e, Wg_e, bg_e, Wo_e, bo_e, g_e, b_e):
            h = jax.nn.gelu(xf @ Wi_e + bi_e, approximate=False) * jax.nn.sigmoid(xf @ Wg_e + bg_e)
            r = xf + (h @ Wo_e + bo_e)
            mu = jnp.mean(r, axis=-1, keepdims=True)
            var = jnp.mean(jnp.square(r - mu), axis=-1, keepdims=True)
            return (r - mu) * jax.lax.rsqrt(var + EPS) * g_e + b_e
        key = jax.random.key(seed)
        ks = jax.random.split(key, 8)
        s = 0.02
        return {'x': jax.random.normal(ks[0], (B, S, H), jnp.float32), 'Wr': jax.random.normal(ks[1], (H, E), jnp.float32) * s, 'br': jnp.zeros((E,), jnp.float32), 'Wi': jax.random.normal(ks[2], (E, H, F), jnp.float32) * s, 'bi': jnp.zeros((E, F), jnp.float32), 'Wg': jax.random.normal(ks[3], (E, H, F), jnp.float32) * s, 'bg': jnp.zeros((E, F), jnp.float32), 'Wo': jax.random.normal(ks[4], (E, F, H), jnp.float32) * s, 'bo': jnp.zeros((E, H), jnp.float32), 'gamma': jnp.ones((E, H), jnp.float32), 'beta': jnp.zeros((E, H), jnp.float32)}
    _L3_ffn_all = _L3_ffn_setup()
    _L3_ffn_in = {k: v for k, v in _L3_ffn_all.items() if k in ('Wr', 'br', 'Wi', 'bi', 'Wg', 'bg', 'Wo', 'bo', 'gamma', 'beta')}
    del _L3_ffn_all
    return {'x': x, 'ctx_1024': ctx_1024, 'mask_1x1xSxS_fk0': mask_1x1xSxS_fk0, 'mask_Bx1x1xS_ff1': mask_Bx1x1xS_ff1, 'mask_Bx1xSxS2_if1': mask_Bx1xSxS2_if1, 'mask_BxS2_if1': mask_BxS2_if1, 'g_xattn': g_xattn, 'g_ffn': g_ffn, 'L0_xattn_Wq': _L0_xattn_in['Wq'], 'L0_xattn_bq': _L0_xattn_in['bq'], 'L0_xattn_Wk': _L0_xattn_in['Wk'], 'L0_xattn_bk': _L0_xattn_in['bk'], 'L0_xattn_Wv': _L0_xattn_in['Wv'], 'L0_xattn_bv': _L0_xattn_in['bv'], 'L0_xattn_Wo': _L0_xattn_in['Wo'], 'L0_xattn_bo': _L0_xattn_in['bo'], 'L0_ffn_w1': _L0_ffn_in['w1'], 'L0_ffn_w3': _L0_ffn_in['w3'], 'L0_ffn_w2': _L0_ffn_in['w2'], 'L1_xattn_Wq': _L1_xattn_in['Wq'], 'L1_xattn_bq': _L1_xattn_in['bq'], 'L1_xattn_Wk': _L1_xattn_in['Wk'], 'L1_xattn_bk': _L1_xattn_in['bk'], 'L1_xattn_Wv': _L1_xattn_in['Wv'], 'L1_xattn_bv': _L1_xattn_in['bv'], 'L1_xattn_Wo': _L1_xattn_in['Wo'], 'L1_xattn_bo': _L1_xattn_in['bo'], 'L1_ffn_gate_w': _L1_ffn_in['gate_w'], 'L1_ffn_w_gate': _L1_ffn_in['w_gate'], 'L1_ffn_w_up': _L1_ffn_in['w_up'], 'L1_ffn_w_down': _L1_ffn_in['w_down'], 'L1_ffn_A1': _L1_ffn_in['A1'], 'L1_ffn_B1': _L1_ffn_in['B1'], 'L1_ffn_A3': _L1_ffn_in['A3'], 'L1_ffn_B3': _L1_ffn_in['B3'], 'L1_ffn_A2': _L1_ffn_in['A2'], 'L1_ffn_B2': _L1_ffn_in['B2'], 'L2_xattn_wq1': _L2_xattn_in['wq1'], 'L2_xattn_bq1': _L2_xattn_in['bq1'], 'L2_xattn_wk1': _L2_xattn_in['wk1'], 'L2_xattn_bk1': _L2_xattn_in['bk1'], 'L2_xattn_wv1': _L2_xattn_in['wv1'], 'L2_xattn_bv1': _L2_xattn_in['bv1'], 'L2_xattn_wo1': _L2_xattn_in['wo1'], 'L2_xattn_bo1': _L2_xattn_in['bo1'], 'L2_xattn_wq2': _L2_xattn_in['wq2'], 'L2_xattn_bq2': _L2_xattn_in['bq2'], 'L2_xattn_wk2': _L2_xattn_in['wk2'], 'L2_xattn_bk2': _L2_xattn_in['bk2'], 'L2_xattn_wv2': _L2_xattn_in['wv2'], 'L2_xattn_bv2': _L2_xattn_in['bv2'], 'L2_xattn_wo2': _L2_xattn_in['wo2'], 'L2_xattn_bo2': _L2_xattn_in['bo2'], 'L2_xattn_w_ff1': _L2_xattn_in['w_ff1'], 'L2_xattn_b_ff1': _L2_xattn_in['b_ff1'], 'L2_xattn_w_ff2': _L2_xattn_in['w_ff2'], 'L2_xattn_b_ff2': _L2_xattn_in['b_ff2'], 'L2_xattn_g1': _L2_xattn_in['g1'], 'L2_xattn_be1': _L2_xattn_in['be1'], 'L2_xattn_g2': _L2_xattn_in['g2'], 'L2_xattn_be2': _L2_xattn_in['be2'], 'L2_xattn_g3': _L2_xattn_in['g3'], 'L2_xattn_be3': _L2_xattn_in['be3'], 'L2_ffn_Wg': _L2_ffn_in['Wg'], 'L2_ffn_bg': _L2_ffn_in['bg'], 'L2_ffn_Wu': _L2_ffn_in['Wu'], 'L2_ffn_bu': _L2_ffn_in['bu'], 'L2_ffn_Wd': _L2_ffn_in['Wd'], 'L2_ffn_bd': _L2_ffn_in['bd'], 'L2_ffn_Wq': _L2_ffn_in['Wq'], 'L2_ffn_keys': _L2_ffn_in['keys'], 'L2_ffn_down_embed': _L2_ffn_in['down_embed'], 'L2_ffn_up_embed': _L2_ffn_in['up_embed'], 'L3_xattn_Wq': _L3_xattn_in['Wq'], 'L3_xattn_bq': _L3_xattn_in['bq'], 'L3_xattn_Wk': _L3_xattn_in['Wk'], 'L3_xattn_bk': _L3_xattn_in['bk'], 'L3_xattn_Wv': _L3_xattn_in['Wv'], 'L3_xattn_bv': _L3_xattn_in['bv'], 'L3_xattn_Wo': _L3_xattn_in['Wo'], 'L3_xattn_bo': _L3_xattn_in['bo'], 'L3_ffn_Wr': _L3_ffn_in['Wr'], 'L3_ffn_br': _L3_ffn_in['br'], 'L3_ffn_Wi': _L3_ffn_in['Wi'], 'L3_ffn_bi': _L3_ffn_in['bi'], 'L3_ffn_Wg': _L3_ffn_in['Wg'], 'L3_ffn_bg': _L3_ffn_in['bg'], 'L3_ffn_Wo': _L3_ffn_in['Wo'], 'L3_ffn_bo': _L3_ffn_in['bo'], 'L3_ffn_gamma': _L3_ffn_in['gamma'], 'L3_ffn_beta': _L3_ffn_in['beta']}

def reference(x, ctx_1024, mask_1x1xSxS_fk0, mask_Bx1x1xS_ff1, mask_Bx1xSxS2_if1, mask_BxS2_if1, g_xattn, g_ffn, L0_xattn_Wq, L0_xattn_bq, L0_xattn_Wk, L0_xattn_bk, L0_xattn_Wv, L0_xattn_bv, L0_xattn_Wo, L0_xattn_bo, L0_ffn_w1, L0_ffn_w3, L0_ffn_w2, L1_xattn_Wq, L1_xattn_bq, L1_xattn_Wk, L1_xattn_bk, L1_xattn_Wv, L1_xattn_bv, L1_xattn_Wo, L1_xattn_bo, L1_ffn_gate_w, L1_ffn_w_gate, L1_ffn_w_up, L1_ffn_w_down, L1_ffn_A1, L1_ffn_B1, L1_ffn_A3, L1_ffn_B3, L1_ffn_A2, L1_ffn_B2, L2_xattn_wq1, L2_xattn_bq1, L2_xattn_wk1, L2_xattn_bk1, L2_xattn_wv1, L2_xattn_bv1, L2_xattn_wo1, L2_xattn_bo1, L2_xattn_wq2, L2_xattn_bq2, L2_xattn_wk2, L2_xattn_bk2, L2_xattn_wv2, L2_xattn_bv2, L2_xattn_wo2, L2_xattn_bo2, L2_xattn_w_ff1, L2_xattn_b_ff1, L2_xattn_w_ff2, L2_xattn_b_ff2, L2_xattn_g1, L2_xattn_be1, L2_xattn_g2, L2_xattn_be2, L2_xattn_g3, L2_xattn_be3, L2_ffn_Wg, L2_ffn_bg, L2_ffn_Wu, L2_ffn_bu, L2_ffn_Wd, L2_ffn_bd, L2_ffn_Wq, L2_ffn_keys, L2_ffn_down_embed, L2_ffn_up_embed, L3_xattn_Wq, L3_xattn_bq, L3_xattn_Wk, L3_xattn_bk, L3_xattn_Wv, L3_xattn_bv, L3_xattn_Wo, L3_xattn_bo, L3_ffn_Wr, L3_ffn_br, L3_ffn_Wi, L3_ffn_bi, L3_ffn_Wg, L3_ffn_bg, L3_ffn_Wo, L3_ffn_bo, L3_ffn_gamma, L3_ffn_beta):
    import jax
    import jax.numpy as jnp

    def _L0_xattn_ref(query, key, value, Wq, bq, Wk, bk, Wv, bv, Wo, bo):
        import jax, jax.numpy as jnp
        import numpy as np
        D_MODEL = 256
        NUM_HEADS = 16
        D_K = D_MODEL // NUM_HEADS

        def _split_heads(x):
            B, S, _ = x.shape
            return x.reshape(B, S, NUM_HEADS, D_K).transpose(0, 2, 1, 3)
        B, Sq, _ = query.shape
        q = _split_heads(query @ Wq.T + bq)
        k = _split_heads(key @ Wk.T + bk)
        v = _split_heads(value @ Wv.T + bv)
        scores = jnp.einsum('bhqd,bhkd->bhqk', q, k) / jnp.sqrt(jnp.float32(D_K))
        attn = jax.nn.softmax(scores, axis=-1)
        ctx = jnp.einsum('bhqk,bhkd->bhqd', attn, v)
        ctx = ctx.transpose(0, 2, 1, 3).reshape(B, Sq, D_MODEL)
        return ctx @ Wo.T + bo

    def _L0_ffn_ref(inputs, w1, w3, w2):
        import jax, jax.numpy as jnp
        import numpy as np
        D_MODEL = 256
        D_FF = 704
        N_EXPERTS = 8
        B, T, D = inputs.shape
        E = w1.shape[0]
        C = T // E
        x = inputs.reshape(B, E, C, D)
        gate = jnp.einsum('becd,edf->becf', x, w1)
        up = jnp.einsum('becd,edf->becf', x, w3)
        h = jax.nn.silu(gate) * up
        out = jnp.einsum('becf,efd->becd', h, w2)
        return out.reshape(B, T, D)

    def _L1_xattn_ref(query, key, value, Wq, bq, Wk, bk, Wv, bv, Wo, bo, query_chunk_size):
        import jax, jax.numpy as jnp
        import numpy as np
        import math
        B, T, S, C, H = (2, 512, 512, 256, 16)
        D = C // H

        def _proj_heads(x, W, b):
            y = x @ W.T + b
            Bv, L, _ = y.shape
            return y.reshape(Bv, L, H, D).transpose(0, 2, 1, 3)
        q = _proj_heads(query, Wq, bq) * (1.0 / math.sqrt(D))
        k = _proj_heads(key, Wk, bk)
        v = _proj_heads(value, Wv, bv)
        scores = jnp.einsum('bhqd,bhkd->bhqk', q, k)
        attn = jax.nn.softmax(scores, axis=-1)
        out = jnp.einsum('bhqk,bhkd->bhqd', attn, v)
        out = out.transpose(0, 2, 1, 3).reshape(query.shape[0], query.shape[1], C)
        return out @ Wo.T + bo

    def _L1_ffn_ref(hidden_states, gate_w, w_gate, w_up, w_down, A1, B1, A3, B3, A2, B2):
        import jax, jax.numpy as jnp
        import numpy as np
        E = 8
        TOPK = 2
        SCALE = 2.0
        B, S, D = hidden_states.shape
        x = hidden_states.reshape(-1, D)
        N = x.shape[0]
        probs = jax.nn.softmax(x @ gate_w.T, axis=-1)
        vals, idx = jax.lax.top_k(probs, TOPK)
        rw = vals / jnp.sum(vals, axis=-1, keepdims=True)
        weight = jnp.zeros((N, E), x.dtype).at[jnp.arange(N)[:, None], idx].add(rw)
        common_w1 = x @ w_gate.T
        common_w3 = x @ w_up.T
        d1 = jnp.einsum('enr,efr->enf', jnp.einsum('nd,erd->enr', x, A1), B1) * SCALE
        d3 = jnp.einsum('enr,efr->enf', jnp.einsum('nd,erd->enr', x, A3), B3) * SCALE
        act = jax.nn.silu(common_w1[None] + d1) * (common_w3[None] + d3)
        out = jnp.einsum('ne,enf->nf', weight, act) @ w_down.T
        z = jnp.einsum('enf,erf->enr', act, A2)
        out = out + jnp.einsum('ne,enr,edr->nd', weight, z, B2) * SCALE
        return out.reshape(B, S, D)

    def _L2_xattn_ref(x, enc_output, attention_mask, padding_mask, wq1, bq1, wk1, bk1, wv1, bv1, wo1, bo1, wq2, bq2, wk2, bk2, wv2, bv2, wo2, bo2, w_ff1, b_ff1, w_ff2, b_ff2, g1, be1, g2, be2, g3, be3):
        import jax, jax.numpy as jnp
        import numpy as np
        B, S, D, H, DFF = (4, 512, 256, 16, 1024)
        DEPTH = D // H
        EPS = 1e-06

        def _ln(x, g, b):
            m = jnp.mean(x, axis=-1, keepdims=True)
            v = jnp.mean(jnp.square(x - m), axis=-1, keepdims=True)
            return (x - m) * jax.lax.rsqrt(v + EPS) * g + b

        def _mha(q_in, k_in, v_in, wq, bq, wk, bk, wv, bv, wo, bo, mask=None):
            b = q_in.shape[0]

            def heads(t):
                return t.reshape(b, -1, H, DEPTH).transpose(0, 2, 1, 3)
            q = heads(q_in @ wq + bq)
            k = heads(k_in @ wk + bk)
            v = heads(v_in @ wv + bv)
            scores = jnp.einsum('bhqd,bhkd->bhqk', q, k) / jnp.sqrt(jnp.float32(DEPTH))
            if mask is not None:
                scores = scores + mask * -1000000000.0
            attn = jax.nn.softmax(scores, axis=-1)
            out = jnp.einsum('bhqk,bhkd->bhqd', attn, v)
            out = out.transpose(0, 2, 1, 3).reshape(b, -1, D)
            return out @ wo + bo
        inv_mask = 1.0 - attention_mask * padding_mask
        attn_out = _mha(x, x, x, wq1, bq1, wk1, bk1, wv1, bv1, wo1, bo1, inv_mask)
        h1 = _ln(x + attn_out, g1, be1)
        cross = _mha(h1, enc_output, enc_output, wq2, bq2, wk2, bk2, wv2, bv2, wo2, bo2, None)
        h2 = _ln(h1 + cross, g2, be2)
        ff = jax.nn.relu(h2 @ w_ff1 + b_ff1) @ w_ff2 + b_ff2
        return _ln(h2 + ff, g3, be3)

    def _L2_ffn_ref(hidden_states, Wg, bg, Wu, bu, Wd, bd, Wq, keys, down_embed, up_embed):
        import jax, jax.numpy as jnp
        import numpy as np
        B, T, D = (2, 512, 256)
        DCD = 1024
        RET = 128
        NEXP = 1024
        NKEYS = 64
        H = 4
        KPH = 8
        b, t, d = hidden_states.shape
        q = (hidden_states @ Wq).reshape(b, t, 2, H, RET // 2)
        sim = jnp.einsum('btphn,hkpn->pbthk', q, keys)
        sc, ix = jax.lax.top_k(sim, KPH)
        sx, sy = (sc[0], sc[1])
        ixx, ixy = (ix[0], ix[1])
        all_sc = (sx[..., :, None] + sy[..., None, :]).reshape(b, t, H, KPH * KPH)
        all_ix = (ixx[..., :, None] * NKEYS + ixy[..., None, :]).reshape(b, t, H, KPH * KPH)
        scores, pk = jax.lax.top_k(all_sc, KPH)
        idx = jnp.take_along_axis(all_ix, pk, axis=-1)
        de = down_embed[idx]
        ue = up_embed[idx]
        w = jnp.einsum('btd,bthkd->bthk', hidden_states, de)
        w = jax.nn.silu(w) * jax.nn.softmax(scores, axis=-1)
        experts_states = jnp.einsum('bthk,bthkd->btd', w, ue)
        mlp = jax.nn.silu(hidden_states @ Wg + bg) * (hidden_states @ Wu + bu) @ Wd + bd
        return mlp + experts_states

    def _L3_xattn_ref(query, key, value, mask, key_padding_mask, Wq, bq, Wk, bk, Wv, bv, Wo, bo):
        import jax, jax.numpy as jnp
        import numpy as np
        import math
        D_MODEL = 256
        N_HEADS = 16
        HEAD_DIM = D_MODEL // N_HEADS
        B, S = (4, 512)
        b = query.shape[0]
        q = query @ Wq.T + bq
        k = key @ Wk.T + bk
        v = value @ Wv.T + bv

        def split_heads(x):
            return x.reshape(b, -1, N_HEADS, HEAD_DIM).transpose(0, 2, 1, 3)
        q, k, v = (split_heads(q), split_heads(k), split_heads(v))
        scale = math.log(D_MODEL) / math.sqrt(HEAD_DIM)
        energy = jnp.einsum('bhqd,bhkd->bhqk', q, k) * scale
        neg_inf = jnp.float32(-jnp.inf)
        energy = jnp.where(mask == 0, neg_inf, energy)
        kpm = key_padding_mask[:, None, None, :]
        energy = jnp.where(kpm == 0, neg_inf, energy)
        attention = jax.nn.softmax(energy, axis=-1)
        out = jnp.einsum('bhqk,bhkd->bhqd', attention, v)
        out = out.transpose(0, 2, 1, 3).reshape(b, -1, D_MODEL)
        return out @ Wo.T + bo

    def _L3_ffn_ref(x, Wr, br, Wi, bi, Wg, bg, Wo, bo, gamma, beta):
        import jax, jax.numpy as jnp
        import numpy as np
        E, K = (8, 2)
        B, S, H, F = (2, 512, 256, 1024)
        EPS = 1e-12

        def _expert_ffn(xf, Wi_e, bi_e, Wg_e, bg_e, Wo_e, bo_e, g_e, b_e):
            h = jax.nn.gelu(xf @ Wi_e + bi_e, approximate=False) * jax.nn.sigmoid(xf @ Wg_e + bg_e)
            r = xf + (h @ Wo_e + bo_e)
            mu = jnp.mean(r, axis=-1, keepdims=True)
            var = jnp.mean(jnp.square(r - mu), axis=-1, keepdims=True)
            return (r - mu) * jax.lax.rsqrt(var + EPS) * g_e + b_e
        b, s, h = x.shape
        T = b * s
        xf = x.reshape(T, h)
        probs = jax.nn.softmax(xf @ Wr + br, axis=-1)
        topw, topi = jax.lax.top_k(probs, K)
        topw = topw / jnp.sum(topw, axis=-1, keepdims=True)
        c = jnp.zeros((T, E), x.dtype).at[jnp.arange(T)[:, None], topi].set(topw)
        y = jax.vmap(_expert_ffn, in_axes=(None, 0, 0, 0, 0, 0, 0, 0, 0))(xf, Wi, bi, Wg, bg, Wo, bo, gamma, beta)
        out = jnp.einsum('te,eth->th', c, y)
        return out.reshape(b, s, h)
    x = x + jnp.tanh(g_xattn[0]) * _L0_xattn_ref(_layernorm(x, axis=-1), ctx_1024, ctx_1024, L0_xattn_Wq, L0_xattn_bq, L0_xattn_Wk, L0_xattn_bk, L0_xattn_Wv, L0_xattn_bv, L0_xattn_Wo, L0_xattn_bo)
    x = x + jnp.tanh(g_ffn[0]) * _L0_ffn_ref(_layernorm(x, axis=-1), L0_ffn_w1, L0_ffn_w3, L0_ffn_w2)
    x = x + jnp.tanh(g_xattn[1]) * _L1_xattn_ref(_layernorm(x, axis=-1), ctx_1024, ctx_1024, L1_xattn_Wq, L1_xattn_bq, L1_xattn_Wk, L1_xattn_bk, L1_xattn_Wv, L1_xattn_bv, L1_xattn_Wo, L1_xattn_bo, 256)
    x = x + jnp.tanh(g_ffn[1]) * _L1_ffn_ref(_layernorm(x, axis=-1), L1_ffn_gate_w, L1_ffn_w_gate, L1_ffn_w_up, L1_ffn_w_down, L1_ffn_A1, L1_ffn_B1, L1_ffn_A3, L1_ffn_B3, L1_ffn_A2, L1_ffn_B2)
    x = x + jnp.tanh(g_xattn[2]) * _L2_xattn_ref(_layernorm(x, axis=-1), ctx_1024, mask_1x1xSxS_fk0, mask_Bx1x1xS_ff1, L2_xattn_wq1, L2_xattn_bq1, L2_xattn_wk1, L2_xattn_bk1, L2_xattn_wv1, L2_xattn_bv1, L2_xattn_wo1, L2_xattn_bo1, L2_xattn_wq2, L2_xattn_bq2, L2_xattn_wk2, L2_xattn_bk2, L2_xattn_wv2, L2_xattn_bv2, L2_xattn_wo2, L2_xattn_bo2, L2_xattn_w_ff1, L2_xattn_b_ff1, L2_xattn_w_ff2, L2_xattn_b_ff2, L2_xattn_g1, L2_xattn_be1, L2_xattn_g2, L2_xattn_be2, L2_xattn_g3, L2_xattn_be3)
    x = x + jnp.tanh(g_ffn[2]) * _L2_ffn_ref(_layernorm(x, axis=-1), L2_ffn_Wg, L2_ffn_bg, L2_ffn_Wu, L2_ffn_bu, L2_ffn_Wd, L2_ffn_bd, L2_ffn_Wq, L2_ffn_keys, L2_ffn_down_embed, L2_ffn_up_embed)
    x = x + jnp.tanh(g_xattn[3]) * _L3_xattn_ref(_layernorm(x, axis=-1), ctx_1024, ctx_1024, mask_Bx1xSxS2_if1, mask_BxS2_if1, L3_xattn_Wq, L3_xattn_bq, L3_xattn_Wk, L3_xattn_bk, L3_xattn_Wv, L3_xattn_bv, L3_xattn_Wo, L3_xattn_bo)
    x = x + jnp.tanh(g_ffn[3]) * _L3_ffn_ref(_layernorm(x, axis=-1), L3_ffn_Wr, L3_ffn_br, L3_ffn_Wi, L3_ffn_bi, L3_ffn_Wg, L3_ffn_bg, L3_ffn_Wo, L3_ffn_bo, L3_ffn_gamma, L3_ffn_beta)
    return x

_drawn_inputs = setup_inputs


def setup_inputs(seed=0):
    import zlib

    import numpy as np

    out = dict(_drawn_inputs(seed))
    spreads = {'L0_xattn_bq': (0.0, 0.412),
     'L0_xattn_bk': (0.0, 2.0),
     'L0_xattn_bv': (0.0, 0.1),
     'L0_xattn_bo': (0.0, 0.1),
     'L2_xattn_bq1': (0.0, 2.0),
     'L2_xattn_bk1': (0.0, 2.0),
     'L2_xattn_bv1': (0.0, 2.0),
     'L2_xattn_bo1': (0.0, 2.0),
     'L2_xattn_bq2': (0.0, 2.0),
     'L2_xattn_bk2': (0.0, 2.0),
     'L2_xattn_bv2': (0.0, 2.0),
     'L2_xattn_bo2': (0.0, 2.0),
     'L2_xattn_b_ff1': (0.0, 2.0),
     'L2_xattn_b_ff2': (0.0, 2.0),
     'L2_xattn_g1': (1.0, 0.6),
     'L2_xattn_be1': (0.0, 0.8),
     'L2_xattn_g2': (1.0, 0.6),
     'L2_xattn_be2': (0.0, 2.0),
     'L2_xattn_g3': (1.0, 0.6),
     'L2_xattn_be3': (0.0, 0.8),
     'L2_ffn_bg': (0.0, 2.0),
     'L2_ffn_bu': (0.0, 2.0),
     'L2_ffn_bd': (0.0, 2.0),
     'L3_ffn_br': (0.0, 2.0),
     'L3_ffn_bi': (0.0, 2.0),
     'L3_ffn_bg': (0.0, 2.0),
     'L3_ffn_bo': (0.0, 2.0),
     'L3_ffn_gamma': (1.0, 0.6),
     'L3_ffn_beta': (0.0, 2.0)}
    factors = {'g_ffn': 26.96,
     'L0_ffn_w1': 2.835,
     'L0_ffn_w3': 2.775,
     'L0_ffn_w2': 2.76,
     'L1_xattn_bq': 4.163,
     'L1_xattn_bk': 200.0,
     'L1_ffn_gate_w': 8.0,
     'L1_ffn_A1': 8.0,
     'L1_ffn_B1': 8.0,
     'L1_ffn_A3': 8.0,
     'L1_ffn_B3': 8.0,
     'L1_ffn_A2': 8.0,
     'L1_ffn_B2': 8.0,
     'L2_ffn_Wq': 64.0,
     'L2_ffn_keys': 64.0,
     'L2_ffn_down_embed': 33.501,
     'L2_ffn_up_embed': 29.452,
     'L3_xattn_bk': 200.0,
     'L3_ffn_Wi': 69.117,
     'L3_ffn_Wg': 200.0,
     'L3_ffn_Wo': 38.345,
     'L2_xattn_wq1': 8.0,
     'L2_xattn_wk1': 8.0,
     'L2_xattn_wv1': 8.0,
     'L2_xattn_wo1': 8.0,
     'L2_xattn_wq2': 8.0,
     'L2_xattn_wk2': 8.0,
     'L2_xattn_wv2': 6.161,
     'L2_xattn_wo2': 6.061,
     'L2_xattn_w_ff1': 5.883,
     'L2_xattn_w_ff2': 4.899,
     'L2_ffn_Wg': 8.0,
     'L2_ffn_Wu': 8.0,
     'L2_ffn_Wd': 8.0,
     'L3_xattn_Wq': 3.239,
     'L3_xattn_bq': 8.0,
     'L3_xattn_Wk': 3.231,
     'L3_xattn_Wv': 2.825,
     'L3_xattn_bv': 25.774,
     'L3_xattn_Wo': 2.792,
     'L3_xattn_bo': 64.0,
     'L3_ffn_Wr': 4.269}
    for name, (base, spread) in spreads.items():
        noise = np.random.default_rng([zlib.crc32(name.encode()), seed]).standard_normal(out[name].shape)
        drawn = base * np.exp(spread * noise) if base else spread * noise
        out[name] = jnp.asarray(drawn.astype(out[name].dtype))
    for name, factor in factors.items():
        out[name] = (out[name] * factor).astype(out[name].dtype)
    return out
```

```python
from contextlib import ExitStack

import concourse.bass as bass
import numpy as np
from concourse import mybir

ACT = mybir.ActivationFunctionType
ALU = mybir.AluOpType
F32 = mybir.dt.float32
BF16 = mybir.dt.bfloat16
I32 = mybir.dt.int32
AX = mybir.AxisListType

B, T, D = 16, 112, 256
S2 = 375
KC, KN = 3, 125
H, DH = 16, 16
DC = D // 128
G, GB = 4, 4
GT = GB * T
PARTS = 3
VW = DH + 1
NEG = -1.0e30
K_PART = (0, 0, 1, 0, 2, 1)
Q_PART = (0, 1, 0, 2, 0, 1)
SROWS = DH * len(K_PART)
AROWS = SROWS + 2
E = 8
F0 = 704
F0_ROWS = (128, 128, 128, 128, 96, 96)
F0_AT = (0, 128, 256, 384, 512, 608)
F = 1024
FC = F // 128
ER = 128
PH, PK = 4, 64
NEXP = 1024
PI = NEXP // PK
ATTN = 5
KV_SET = (0, 1, 3, 4)


class Region:

    def __init__(self, tensor, words):
        self.tensor, self.words, self.at = tensor, words, 0

    def clear(self):
        self.at = 0

    def take(self, parts, *dims, dtype=F32):
        count = 1
        for d in dims:
            count *= d
        words = (count + 1) // 2 if dtype == BF16 else count
        words += words % 2
        assert self.at + words <= self.words, (self.at, words)
        view = self.tensor[0:parts, self.at : self.at + words]
        self.at += words
        if dtype != F32:
            view = view.bitcast(dtype)
        view = view[:, 0:count]
        if len(dims) == 1:
            return view
        names = "abcdef"[: len(dims)]
        return view.rearrange(f"p ({' '.join(names)}) -> p {' '.join(names)}", **dict(zip(names, dims)))


def at_least(eng, sem, value):
    if not (isinstance(value, int) and value <= 0):
        eng.wait_ge(sem, value)


def batches(eng, step):
    step(0, 0, 0)
    step(1, 1, 0)
    with eng.Fori(1, B // 2) as i:
        step(i * 2, 0, i)
        step(i * 2 + 1, 1, i)


def build(nc, a):
    ctx = ExitStack()
    with ctx:
        def sb(name, shape, dt=F32):
            return ctx.enter_context(nc.sbuf_tensor(name, shape, dt))

        def sem(name):
            return ctx.enter_context(nc.semaphore(name))

        x = sb("x", [T, B, D])
        h = sb("h", [T, B, D])
        xn_t = sb("xn_t", [128, DC, B * T])
        ident = sb("ident", [128, 128])
        ident16 = sb("ident16", [T, T], BF16)
        neg16 = sb("neg16", [T, GB, T], BF16)
        gates = sb("gates", [128, 8])
        one = sb("one", [128, 1])
        idle = sb("idle", [128, 1])
        ln_raw = sb("ln_raw", [T, B, 6])
        ln_tmp = sb("ln_tmp", [T, 5, B])
        ln_mean = sb("ln_mean", [T, B])
        ln_rstd = sb("ln_rstd", [T, B])
        half = sb("half", [T, B])
        xn2 = [sb(f"xn2_{r}", [T, D]) for r in range(2)]
        attn_cols = sb("attn_cols", [128, ATTN, 4])
        attn_rows = sb("attn_rows", [128, 2, D])
        A_WORDS, W_WORDS, L_WORDS = 22528, 12288, 2048
        arena = Region(sb("arena", [128, A_WORDS]), A_WORDS)
        wreg = Region(sb("wreg", [128, W_WORDS]), W_WORDS)
        wlow = Region(sb("wlow", [128, L_WORDS]), L_WORDS)
        ps = ctx.enter_context(nc.psum_tensor("ps", [128, 8, 512], F32))

        key_parts = nc.dram_tensor("key_parts", (4, B, PARTS, D, S2), BF16, kind="Internal").ap()
        values = nc.dram_tensor("values", (4, B, KN, KC * H * VW), F32, kind="Internal").ap()
        query_parts = nc.dram_tensor("query_parts", (2, PARTS, D, B * T), BF16, kind="Internal").ap()

        block = ctx.enter_context(nc.Block())
        programs = {"sync": [], "gpsimd": [], "scalar": [], "vector": [], "tensor": []}

        stage_done = sem("stage_done")
        stages = [0]

        def stage(sync=None, gpsimd=None, scalar=None, vector=None, tensor=None):
            stages[0] += 1
            meet = 5 * stages[0]
            for name, program in (("sync", sync), ("gpsimd", gpsimd), ("scalar", scalar), ("vector", vector), ("tensor", tensor)):
                def whole(eng, program=program):
                    if program is not None:
                        program(eng)
                    eng.drain().then_inc(stage_done, 1)
                    eng.wait_ge(stage_done, meet)
                programs[name].append(whole)

        loaded = sem("loaded")
        loads = [0]

        def expect(transfers):
            loads[0] += 16 * transfers
            return loads[0]

        in_ready = expect(4)
        const_made = sem("const_made")
        gate_in = arena.take(128, 8)

        def start_sync(sp):
            sp.dma_start(x[:, :, :], a["x"].rearrange("b t d -> t b d")).then_inc(loaded, 16)
            sp.dma_start(gate_in[:, 0:4], a["g_xattn"].partition_broadcast(128)).then_inc(loaded, 16)
            sp.dma_start(gate_in[:, 4:8], a["g_ffn"].partition_broadcast(128)).then_inc(loaded, 16)
            sp.dma_start(attn_cols[:, :, :], a["attn_cols"].rearrange("l p c -> p l c")).then_inc(loaded, 16)
            sp.wait_ge(loaded, in_ready)

        def start_gpsimd(pool):
            pool.memset(ident[:, :], 0.0).then_inc(const_made, 1)
            pool.memset(ident16[:, :], 0.0).then_inc(const_made, 1)
            pool.memset(neg16[:, :, :], 0.0).then_inc(const_made, 1)
            pool.memset(half[:, :], -0.5)
            pool.memset(one[:, :], 1.0)
            pool.wait_ge(const_made, 3)
            pool.affine_select(out=ident[:, :], in_=ident[:, :], compare_op=ALU.not_equal, fill=1.0, base=0,
                               pattern=[[-1, 128]], channel_multiplier=1)
            pool.affine_select(out=ident16[:, :], in_=ident16[:, :], compare_op=ALU.not_equal, fill=1.0, base=0,
                               pattern=[[-1, T]], channel_multiplier=1)
            pool.affine_select(out=neg16[:, :, :], in_=neg16[:, :, :], compare_op=ALU.not_equal, fill=NEG, base=0,
                               pattern=[[0, GB], [-1, T]], channel_multiplier=1)

        def start_scalar(act):
            act.wait_ge(loaded, in_ready)
            act.activation(gates[:, :], gate_in, ACT.Tanh)

        stage(sync=start_sync, gpsimd=start_gpsimd, scalar=start_scalar)

        kv_ctx = [sem("kv_ctx0"), sem("kv_ctx1")]
        kv_ones = sem("kv_ones")
        kv_k, kv_v = sem("kv_k"), sem("kv_v")
        kv_hi, kv_res, kv_mid, kv_lo = sem("kv_hi"), sem("kv_res"), sem("kv_mid"), sem("kv_lo")
        kv_vout = sem("kv_vout")
        kv_kst, kv_vst = [sem("kv_kst0"), sem("kv_kst1")], [sem("kv_vst0"), sem("kv_vst1")]

        def context_stage():
            arena.clear()
            wreg.clear()
            NKV = len(KV_SET)
            weights_ready = expect(2 * NKV)
            ctx_t = [arena.take(128, DC, S2) for _ in range(2)]
            parts = [arena.take(128, DC, PARTS, S2, dtype=BF16) for _ in range(2)]
            rest = [arena.take(128, DC, S2) for _ in range(2)]
            vout = [arena.take(KN, KC, H, VW) for _ in range(2)]
            bv = arena.take(128, NKV, D)
            w = wreg.take(128, NKV, 2, DC, D)

            def sync(sp):
                for i, s in enumerate(KV_SET):
                    sp.dma_start(w[:, i], a["attn_w"][s, :, 1:3]).then_inc(loaded, 16)
                    sp.dma_start(bv[:, i, :], a["attn_rows"][s, 0].partition_broadcast(128)).then_inc(loaded, 16)
                sp.dma_start(ctx_t[0], a["ctx_t"][0]).then_inc(kv_ctx[0], 16)
                sp.dma_start(ctx_t[1], a["ctx_t"][1]).then_inc(kv_ctx[1], 16)

                def step(b, u, pair):
                    for i in range(NKV):
                        n = b * NKV + i
                        sp.wait_ge(kv_lo, n * 2 + 2)
                        for t in range(DC):
                            sp.dma_start(key_parts[i, b, :, t * 128:(t + 1) * 128, :].rearrange("q p k -> p q k"),
                                         parts[i % 2][:, t]).then_inc(kv_kst[i % 2], 16)
                        sp.wait_ge(kv_vout, n * 2 + 2)
                        sp.dma_start(values[i, b], vout[i % 2].rearrange("p c h w -> p (c h w)")).then_inc(kv_vst[i % 2], 16)

                def more(b, u):
                    step(b, u, None)
                    sp.wait_ge(kv_v, (b * NKV + NKV) * 2)
                    sp.dma_start(ctx_t[u], a["ctx_t"][b + 2]).then_inc(kv_ctx[u], 16)

                with sp.Fori(0, B // 2 - 1) as i:
                    more(i * 2, 0)
                    more(i * 2 + 1, 1)
                step(B - 2, 0, None)
                step(B - 1, 1, None)
                for q in range(2):
                    sp.wait_ge(kv_kst[q], 16 * DC * B * NKV // 2)
                    sp.wait_ge(kv_vst[q], 16 * B * NKV // 2)

            def tensor(pe):
                pe.wait_ge(loaded, weights_ready)

                def step(b, u, pair):
                    pe.wait_ge(kv_ctx[u], pair * 16 + 16)
                    for i in range(NKV):
                        n = b * NKV + i
                        at_least(pe, kv_res, (n - 1) * 2)
                        for t in range(DC):
                            for c in range(DC):
                                mm = pe.matmul(ps[:, 2 * (i % 2) + t, 0:S2], w[:, i, 0, c, t * 128:(t + 1) * 128],
                                               ctx_t[u][:, c, :], start=(c == 0), stop=(c == DC - 1))
                            mm.then_inc(kv_k, 1)
                        at_least(pe, kv_vout, (n - 1) * 2)
                        for k in range(KC):
                            for c in range(DC):
                                mm = pe.matmul(ps[0:KN, 4 + 2 * (i % 2) + k // 2, (k % 2) * D:(k % 2 + 1) * D],
                                               ctx_t[u][:, c, k * KN:(k + 1) * KN], w[:, i, 1, c, :],
                                               start=(c == 0), stop=(c == DC - 1))
                            if k > 0:
                                mm.then_inc(kv_v, 1)

                batches(pe, step)

            def scalar(act):
                def step(b, u, pair):
                    for i, s in enumerate(KV_SET):
                        n = b * NKV + i
                        at_least(act, kv_kst[i % 2], (b * (NKV // 2) + i // 2) * (16 * DC))
                        for t in range(DC):
                            act.wait_ge(kv_k, n * 2 + t + 1)
                            act.activation(parts[i % 2][:, t, 0, :], ps[:, 2 * (i % 2) + t, 0:S2], ACT.Identity,
                                           bias=attn_cols[:, s, 2 + t:3 + t]).then_inc(kv_hi, 1)
                        for t in range(DC):
                            act.wait_ge(kv_res, n * 2 + t + 1)
                            act.activation(parts[i % 2][:, t, 1, :], rest[i % 2][:, t, :], ACT.Copy).then_inc(kv_mid, 1)

                batches(act, step)

            def vector(dve):
                for q in range(2):
                    dve.memset(vout[q], 1.0).then_inc(kv_ones, 1)
                dve.wait_ge(kv_ones, 2)
                dve.wait_ge(loaded, weights_ready)

                def step(b, u, pair):
                    for i, s in enumerate(KV_SET):
                        n = b * NKV + i
                        at_least(dve, kv_lo, (n - 1) * 2)
                        for t in range(DC):
                            dve.wait_ge(kv_hi, n * 2 + t + 1)
                            dve.scalar_tensor_tensor(rest[i % 2][:, t, :], ps[:, 2 * (i % 2) + t, 0:S2],
                                                     attn_cols[:, s, 2 + t:3 + t], parts[i % 2][:, t, 0, :],
                                                     ALU.add, ALU.subtract).then_inc(kv_res, 1)
                        at_least(dve, kv_vst[i % 2], (b * (NKV // 2) + i // 2) * 16)
                        for k in range(2):
                            n_k = 2 - k
                            dve.wait_ge(kv_v, n * 2 + k + 1)
                            dve.tensor_tensor(vout[i % 2][:, 2 * k:2 * k + n_k, :, 0:DH],
                                              ps[0:KN, 4 + 2 * (i % 2) + k, 0:n_k * D].rearrange("p (c h e) -> p c h e", c=n_k, h=H),
                                              bv[0:KN, i, :].rearrange("p (h e) -> p h e", h=H).unsqueeze(1).broadcast_to([KN, n_k, H, DH]),
                                              ALU.add).then_inc(kv_vout, 1)

                batches(dve, step)

            def gpsimd(pool):
                def step(b, u, pair):
                    for i in range(NKV):
                        n = b * NKV + i
                        for t in range(DC):
                            pool.wait_ge(kv_mid, n * 2 + t + 1)
                            pool.tensor_tensor(parts[i % 2][:, t, 2, :], rest[i % 2][:, t, :], parts[i % 2][:, t, 1, :],
                                               ALU.subtract).then_inc(kv_lo, 1)

                batches(pool, step)

            stage(sync, gpsimd, scalar, vector, tensor)

        context_stage()

        ln_stat, ln_step, ln_ready = sem("ln_stat"), sem("ln_step"), sem("ln_ready")
        ln_normed, ln_scaled, ln_turned, ln_kept, ln_stored = (sem("ln_normed"), sem("ln_scaled"), sem("ln_turned"),
                                                               sem("ln_kept"), sem("ln_stored"))
        ln_evac = sem("ln_evac")
        ln_count = {"call": 0, "gain": 0, "turn": 0, "store": 0}

        def norm_stage(src, eps, gain=None, keep=None, turn=True, add_gate=None):
            m, mg = ln_count["call"], ln_count["gain"]
            t0, s0 = ln_count["turn"] * B, ln_count["store"] * B
            stores = keep is not None or add_gate is not None
            ln_count["call"] += 1
            ln_count["gain"] += gain is not None
            ln_count["turn"] += turn
            ln_count["store"] += stores
            arena.clear()
            rows = arena.take(128, 2, D)
            scaled = [arena.take(T, D) for _ in range(2)]
            n0 = m * B
            g0 = mg * B
            gain_ready = expect(2) if gain is not None else 0

            def sync(sp):
                if gain is not None:
                    for r in range(2):
                        sp.dma_start(rows[:, r, :], a["ln_rows"][gain + r].partition_broadcast(128)).then_inc(loaded, 16)
                    sp.wait_ge(loaded, gain_ready)

            def vector(dve):
                with dve.Fori(0, B) as b:
                    dve.bn_stats(ln_raw[:, b, :], src[:, b, :]).then_inc(ln_stat, 1)
                dve.wait_ge(ln_stat, n0 + B)
                k = 6 * m
                dve.tensor_tensor(ln_tmp[:, 0, :], ln_raw[:, :, 1], ln_raw[:, :, 4], ALU.add).then_inc(ln_step, 1)
                dve.tensor_tensor(ln_tmp[:, 1, :], ln_raw[:, :, 1], ln_raw[:, :, 4], ALU.subtract).then_inc(ln_step, 1)
                dve.tensor_tensor(ln_tmp[:, 2, :], ln_raw[:, :, 2], ln_raw[:, :, 5], ALU.add).then_inc(ln_step, 1)
                dve.wait_ge(ln_step, k + 3)
                dve.tensor_scalar(ln_mean[:, :], ln_tmp[:, 0, :], 0.5, None, ALU.mult).then_inc(ln_step, 1)
                dve.scalar_tensor_tensor(ln_tmp[:, 3, :], ln_tmp[:, 1, :], 0.25, ln_tmp[:, 1, :], ALU.mult, ALU.mult).then_inc(ln_step, 1)
                dve.wait_ge(ln_step, k + 5)
                dve.scalar_tensor_tensor(ln_tmp[:, 4, :], ln_tmp[:, 2, :], 1.0 / D, ln_tmp[:, 3, :], ALU.mult, ALU.add).then_inc(ln_step, 1)
                dve.wait_ge(ln_ready, 2 * (m + 1))
                if gain is not None:
                    dve.wait_ge(loaded, gain_ready)

                def step(b, u, pair):
                    n = n0 + b
                    if turn:
                        at_least(dve, ln_turned, t0 + b - 1)
                    if stores:
                        at_least(dve, ln_stored, s0 + b - 1)
                    if gain is not None:
                        at_least(dve, ln_scaled, g0 + b - 1)
                    dve.tensor_scalar(xn2[u][:, :] if gain is None else scaled[u], src[:, b, :], ln_mean[:, bass.ds(b, 1)],
                                      ln_rstd[:, bass.ds(b, 1)], ALU.subtract, ALU.mult).then_inc(ln_normed, 1)
                    if gain is not None:
                        dve.wait_ge(ln_scaled, g0 + b + 1)
                        dve.tensor_tensor(xn2[u][:, :], scaled[u], rows[0:T, 1, :], ALU.add).then_inc(ln_kept, 1)
                        if add_gate is not None:
                            dve.wait_ge(ln_kept, g0 + b + 1)
                            dve.scalar_tensor_tensor(x[:, b, :], xn2[u][:, :], gates[0:T, add_gate:add_gate + 1], x[:, b, :],
                                                     ALU.mult, ALU.add).then_inc(ln_stored, 1)

                batches(dve, step)

            def gpsimd(pool):
                pool.wait_ge(ln_step, 6 * (m + 1))
                pool.tensor_scalar(ln_tmp[:, 0, :], ln_tmp[:, 4, :], eps, None, ALU.add).then_inc(ln_ready, 1)
                pool.wait_ge(ln_ready, 2 * m + 1)
                pool.tensor_tensor(ln_rstd[:, :], ln_tmp[:, 0, :], half[:, :], ALU.pow).then_inc(ln_ready, 1)
                if gain is not None:
                    pool.wait_ge(loaded, gain_ready)

                def step(b, u, pair):
                    n = n0 + b
                    if gain is not None:
                        pool.wait_ge(ln_normed, n + 1)
                        pool.tensor_tensor(scaled[u], scaled[u], rows[0:T, 0, :], ALU.mult).then_inc(ln_scaled, 1)
                    if keep is not None:
                        if gain is None:
                            pool.wait_ge(ln_normed, n + 1)
                        else:
                            pool.wait_ge(ln_kept, g0 + b + 1)
                        pool.tensor_copy(keep[:, b, :], xn2[u][:, :]).then_inc(ln_stored, 1)

                batches(pool, step)

            def tensor(pe):
                def step(b, u, pair):
                    n = n0 + b
                    if gain is None:
                        pe.wait_ge(ln_normed, n + 1)
                    else:
                        pe.wait_ge(ln_kept, g0 + b + 1)
                    at_least(pe, ln_evac, t0 + b - 1)
                    for c in range(DC):
                        mm = pe.transpose(ps[:, u, c * T:(c + 1) * T], xn2[u][:, c * 128:(c + 1) * 128], ident[0:T, 0:T])
                    mm.then_inc(ln_turned, 1)

                batches(pe, step)

            def scalar(act):
                def step(b, u, pair):
                    act.wait_ge(ln_turned, t0 + b + 1)
                    act.activation(xn_t[:, :, bass.ds(b * T, T)], ps[:, u, 0:DC * T].rearrange("p (c t) -> p c t", c=DC),
                                   ACT.Copy).then_inc(ln_evac, 1)

                batches(act, step)

            stage(sync, gpsimd, scalar if turn else None, vector, tensor if turn else None)


        q_made, q_hi, q_res, q_mid, q_lo = sem("q_made"), sem("q_hi"), sem("q_res"), sem("q_mid"), sem("q_lo")
        q_stored = [sem("q_stored0"), sem("q_stored1")]
        q_count = {"tile": 0, "store": 0}

        def query_stage(s, kinds):
            arena.clear()
            wlow.clear()
            w = wlow.take(128, 4, DC, D)
            parts = [arena.take(128, PARTS, GT, dtype=BF16) for _ in range(2)]
            rest = [arena.take(128, GT) for _ in range(2)]
            weights_ready = expect(3)
            q0, st0 = q_count["tile"], q_count["store"]
            TILES = DC * kinds
            q_count["tile"] += G * TILES
            q_count["store"] += G * TILES // 2

            def sync(sp):
                sp.dma_start(w, a["attn_w"][s]).then_inc(loaded, 16)
                for r in range(2):
                    sp.dma_start(attn_rows[:, r, :], a["attn_rows"][s, r].partition_broadcast(128)).then_inc(loaded, 16)
                with sp.Fori(0, G) as g:
                    for j in range(TILES):
                        sp.wait_ge(q_lo, q0 + g * TILES + j + 1)
                        sp.dma_start(query_parts[j // DC, :, (j % DC) * 128:(j % DC + 1) * 128, bass.ds(g * GT, GT)].rearrange("q p n -> p q n"),
                                     parts[j % 2]).then_inc(q_stored[j % 2], 16)
                for r in range(2):
                    sp.wait_ge(q_stored[r], 16 * (st0 + G * TILES // 2))
                sp.wait_ge(loaded, weights_ready)

            def groups(eng, step):
                step(0)
                with eng.Fori(1, G) as g:
                    step(g)

            def tensor(pe):
                pe.wait_ge(loaded, weights_ready)

                def step(g):
                    for j in range(TILES):
                        at_least(pe, q_res, q0 + g * TILES + j - 1)
                        for c in range(DC):
                            mm = pe.matmul(ps[:, j % 2, 0:GT], w[:, j // DC, c, (j % DC) * 128:(j % DC + 1) * 128],
                                           xn_t[:, c, bass.ds(g * GT, GT)], start=(c == 0), stop=(c == DC - 1))
                        mm.then_inc(q_made, 1)

                groups(pe, step)

            def scalar(act):
                def step(g):
                    for j in range(TILES):
                        n = q0 + g * TILES + j
                        at_least(act, q_stored[j % 2], (st0 + g * (TILES // 2) + j // 2) * 16)
                        act.wait_ge(q_made, n + 1)
                        act.activation(parts[j % 2][:, 0, :], ps[:, j % 2, 0:GT], ACT.Identity,
                                       bias=attn_cols[:, s, j:j + 1]).then_inc(q_hi, 1)
                        act.wait_ge(q_res, n + 1)
                        act.activation(parts[j % 2][:, 1, :], rest[j % 2], ACT.Copy).then_inc(q_mid, 1)

                groups(act, step)

            def vector(dve):
                def step(g):
                    for j in range(TILES):
                        n = q0 + g * TILES + j
                        at_least(dve, q_lo, n - 1)
                        dve.wait_ge(q_hi, n + 1)
                        dve.scalar_tensor_tensor(rest[j % 2], ps[:, j % 2, 0:GT], attn_cols[:, s, j:j + 1], parts[j % 2][:, 0, :],
                                                 ALU.add, ALU.subtract).then_inc(q_res, 1)

                groups(dve, step)

            def gpsimd(pool):
                def step(g):
                    for j in range(TILES):
                        n = q0 + g * TILES + j
                        pool.wait_ge(q_mid, n + 1)
                        pool.tensor_tensor(parts[j % 2][:, 2, :], rest[j % 2], parts[j % 2][:, 1, :], ALU.subtract).then_inc(q_lo, 1)

                groups(pool, step)

            stage(sync, gpsimd, scalar, vector, tensor)
            return w

        o_copied = sem("o_copied")
        o_turned = sem("o_turned")
        o_recip, o_normed = sem("o_recip"), sem("o_normed")
        o_turned2, o_copied2 = sem("o_turned2"), sem("o_copied2")
        o_made, o_added = sem("o_made"), sem("o_added")
        MISC, SUMS = 7, 6

        class Output:

            def __init__(self, w, dest, gate):
                self.w, self.dest, self.gate = w, dest, gate
                self.sums = [arena.take(128, 4, T) for _ in range(3)]
                self.normed = [arena.take(T, D) for _ in range(3)]
                self.turned = [arena.take(128, DC, T) for _ in range(3)]
                self.recip = arena.take(T, H)
            def turn_back(self, pe, n, r):
                at_least(pe, o_added, n)
                pe.wait_ge(o_copied, n + 1)
                for j in range(4):
                    mm = pe.transpose(ps[0:T, MISC, j * 128:(j + 1) * 128], self.sums[r][:, j, :], ident[:, :])
                mm.then_inc(o_turned, 1)

            def turn(self, pe, n, r):
                pe.wait_ge(o_normed, n + 1)
                for c in range(DC):
                    mm = pe.transpose(ps[:, MISC, c * T:(c + 1) * T], self.normed[r][:, c * 128:(c + 1) * 128], ident[0:T, 0:T])
                mm.then_inc(o_turned2, 1)

            def project(self, pe, n, r):
                pe.wait_ge(o_copied2, n + 1)
                for c in range(DC):
                    mm = pe.matmul(ps[0:T, MISC, 0:D], self.turned[r][:, c, :], self.w[:, 3, c, :], start=(c == 0), stop=(c == DC - 1))
                mm.then_inc(o_made, 1)

            def copy_turned(self, act, n, r):
                act.wait_ge(o_turned2, n + 1)
                act.activation(self.turned[r], ps[:, MISC, 0:DC * T].rearrange("p (c t) -> p c t", c=DC), ACT.Copy).then_inc(o_copied2, 1)

            def copy_sums(self, act, n, r):
                act.activation(self.sums[r], ps[:, SUMS, 0:4 * T].rearrange("p (j t) -> p j t", j=4), ACT.Copy).then_inc(o_copied, 1)

            def normalise(self, dve, n, r):
                back = ps[0:T, MISC, :].rearrange("p (h w) -> p h w", w=32)
                dve.wait_ge(o_turned, n + 1)
                dve.reciprocal(self.recip, back[:, :, DH]).then_inc(o_recip, 1)
                dve.wait_ge(o_recip, n + 1)
                dve.tensor_tensor(self.normed[r].rearrange("p (h e) -> p h e", h=H), back[:, :, 0:DH],
                                  self.recip.unsqueeze(2).broadcast_to([T, H, DH]), ALU.mult).then_inc(o_normed, 1)

            def add(self, dve, n, b):
                dve.wait_ge(o_made, n + 1)
                dve.scalar_tensor_tensor(self.dest[:, b, :], ps[0:T, MISC, 0:D], self.gate, self.dest[:, b, :],
                                         ALU.mult, ALU.add).then_inc(o_added, 1)

        bias_scaled, bias_added = sem("bias_scaled"), sem("bias_added")
        bias_count = [0]

        def bias_stage(dest, gate, row, load=None):
            k = bias_count[0]
            bias_count[0] += 1
            arena.clear()
            scaled = arena.take(T, D)
            row_ready = expect(1) if load is not None else 0

            def sync(sp):
                if load is not None:
                    sp.dma_start(row, load.partition_broadcast(T)).then_inc(loaded, 16)
                    sp.wait_ge(loaded, row_ready)

            def vector(dve):
                if load is not None:
                    dve.wait_ge(loaded, row_ready)
                dve.tensor_scalar(scaled, row, gate, None, ALU.mult).then_inc(bias_scaled, 1)
                dve.wait_ge(bias_scaled, k + 1)
                for q in range(2):
                    dve.tensor_tensor(dest[:, q * 8:q * 8 + 8, :], dest[:, q * 8:q * 8 + 8, :],
                                      scaled.unsqueeze(1).broadcast_to([T, 8, D]), ALU.add).then_inc(bias_added, 1)

            stage(sync=sync, vector=vector)

        at_loaded = [sem(f"at_loaded{r}") for r in range(3)]
        at_maxrow = [sem(f"at_maxrow{r}") for r in range(3)]
        at_ones = sem("at_ones")
        at_pair, at_max = sem("at_pair"), sem("at_max")
        at_clamped, at_mturn, at_mhi, at_mmid = sem("at_clamped"), sem("at_mturn"), sem("at_mhi"), sem("at_mmid")
        at_scores, at_probs, at_pv = sem("at_scores"), sem("at_probs"), sem("at_pv")
        at_mask, at_pen0, at_pen = [sem(f"at_mask{r}") for r in range(3)], sem("at_pen0"), sem("at_pen")
        at_count = {"call": 0, "mask": 0}
        out_count = [0]
        STEPS, PAIRS = 12, H // 2

        def cross_stage(kv, w, scale, dest, gate, masked=False):
            arena.clear()
            wreg.clear()
            n0, o0, p0 = at_count["call"] * B, out_count[0] * B, at_count["mask"] * B
            call = at_count["call"]
            at_count["call"] += 1
            at_count["mask"] += masked
            out_count[0] += 1
            keys = [wreg.take(AROWS, H, S2, dtype=BF16) for _ in range(3)]
            queries = [wreg.take(AROWS, H, T, dtype=BF16) for _ in range(3)]
            vals = [arena.take(KN, KC, H, VW) for _ in range(3)]
            probs = [arena.take(KN, GT) for _ in range(3)]
            out = Output(w, dest, gate)
            negmax = [arena.take(T, H) for _ in range(3)]
            negmax_c = [arena.take(T, H) for _ in range(3)]
            maxrow = [arena.take(H, 2, T, dtype=BF16) for _ in range(3)]
            if masked:
                mask_in = [arena.take(T, S2, dtype=I32) for _ in range(3)]
                pad_in = [arena.take(T, S2, dtype=I32) for _ in range(3)]
                pen = [arena.take(T, S2, dtype=BF16) for _ in range(3)]

            def schedule(eng, step):
                step(0, 0)
                with eng.Fori(0, 4) as i:
                    for q in range(3):
                        step(i * 3 + 1 + q, (1 + q) % 3)
                for b in range(13, B):
                    step(b, b % 3)

            def has_next(b):
                return not isinstance(b, int) or b < B - 1

            def has_prev(b):
                return not isinstance(b, int) or b > 0

            LOADS = 2 * len(K_PART) + 1

            def base(r):
                return (6 if r == 0 else 5) * call

            def sync(sp):
                def load(b, r):
                    for j in range(len(K_PART)):
                        sp.dma_start(keys[r][DH * j:DH * j + DH, :, :],
                                     key_parts[kv, b, K_PART[j], :, :].rearrange("(h d) k -> d h k", d=DH)).then_inc(at_loaded[r], 16)
                        sp.dma_start(queries[r][DH * j:DH * j + DH, :, :],
                                     query_parts[0, Q_PART[j], :, bass.ds(b * T, T)].rearrange("(h d) k -> d h k", d=DH)).then_inc(at_loaded[r], 16)
                    sp.dma_start(vals[r].rearrange("p c h w -> p (c h w)"), values[kv, b]).then_inc(at_loaded[r], 16)
                    if masked:
                        sp.dma_start(mask_in[r], a["mask"][b]).then_inc(at_mask[r], 16)
                        sp.dma_start(pad_in[r], a["pad"][b].partition_broadcast(T)).then_inc(at_mask[r], 16)

                def rows(b, r):
                    sp.wait_ge(at_mmid, n0 + b + 1)
                    for q in range(2):
                        sp.dma_start(queries[r][SROWS + q:SROWS + q + 1, :, :], maxrow[r][:, q, :]).then_inc(at_maxrow[r], 16)

                load(0, 0)
                load(1, 1)
                rows(0, 0)

                def step(b, r):
                    if not isinstance(b, int) or b < B - 2:
                        at_least(sp, at_pv, (n0 + b) * STEPS if has_prev(b) else 0)
                        load(b + 2, (r + 2) % 3)
                    if has_next(b):
                        rows(b + 1, (r + 1) % 3)

                schedule(sp, step)

            def tensor(pe):
                def pair(b, r, p):
                    k = (n0 + b) * PAIRS + p
                    at_least(pe, at_max, k - 1)
                    for e in range(2):
                        hd = 2 * p + e
                        mm = pe.matmul(ps[0:T, 2 * (p % 2) + e, 0:S2], queries[r][0:SROWS, hd, :], keys[r][0:SROWS, hd, :],
                                       start=True, stop=not masked)
                        if masked:
                            mm = pe.matmul(ps[0:T, 2 * (p % 2) + e, 0:S2], neg16[:, 0, :], pen[r], start=False, stop=True)
                    mm.then_inc(at_pair, 1)

                def maxima(b, r):
                    pe.wait_ge(at_clamped, n0 + b + 1)
                    pe.transpose(ps[0:H, MISC, 0:T], negmax_c[r], ident[0:T, 0:T]).then_inc(at_mturn, 1)

                def scores(b, r, k):
                    m = (n0 + b) * STEPS + k
                    at_least(pe, at_probs, m - 1)
                    bank, c = 4 + k % 2, k % KC
                    if masked:
                        pe.matmul(ps[0:KN, bank, 0:GT], pen[r][:, c * KN:(c + 1) * KN], neg16[:, :, :], start=True, stop=False)
                    for g in range(4):
                        hd = 4 * (k // KC) + g
                        mm = pe.matmul(ps[0:KN, bank, g * T:(g + 1) * T], keys[r][:, hd, c * KN:(c + 1) * KN], queries[r][:, hd, :],
                                       start=not masked, stop=not masked or g == 3)
                    mm.then_inc(at_scores, 1)

                def weigh(b, r, k):
                    m = (n0 + b) * STEPS + k
                    pe.wait_ge(at_probs, m + 1)
                    j, c = k // KC, k % KC
                    for g in range(4):
                        mm = pe.matmul(ps[32 * g:32 * g + VW, SUMS, j * T:(j + 1) * T], vals[r][:, c, 4 * j + g, :],
                                       probs[k % 3][:, g * T:(g + 1) * T], start=(c == 0), stop=(c == KC - 1))
                    mm.then_inc(at_pv, 1)

                def arrived(b, r, q):
                    pe.wait_ge(at_loaded[r], (q + 1) * (16 * LOADS))
                    if masked:
                        pe.wait_ge(at_pen, p0 + b + 1)

                pe.wait_ge(at_ones, 3 * (call + 1))
                arrived(0, 0, base(0))
                for p in range(PAIRS):
                    pair(0, 0, p)
                maxima(0, 0)

                def step(b, r, turn, turn_next):
                    n = n0 + b
                    last = o0 + b - 1
                    pe.wait_ge(at_maxrow[r], (turn + 1) * 32)
                    for k in range(STEPS):
                        scores(b, r, k)
                        if k == 1:
                            at_least(pe, o_copied, o0 + b)
                        if k > 0:
                            weigh(b, r, k - 1)
                        if k < PAIRS and has_next(b):
                            if k == 0:
                                arrived(b + 1, (r + 1) % 3, turn_next)
                            pair(b + 1, (r + 1) % 3, k)
                        if has_prev(b):
                            if k == 1:
                                at_least(pe, at_mmid, n + 1)
                                out.turn_back(pe, last, (r + 2) % 3)
                            if k == 3:
                                out.turn(pe, last, (r + 2) % 3)
                            if k == 6:
                                out.project(pe, last, (r + 2) % 3)
                        if k == 9 and has_next(b):
                            at_least(pe, o_added, o0 + b)
                            maxima(b + 1, (r + 1) % 3)
                    weigh(b, r, STEPS - 1)

                spread(pe, step)
                last = o0 + B - 1
                out.turn_back(pe, last, (B - 1) % 3)
                out.turn(pe, last, (B - 1) % 3)
                out.project(pe, last, (B - 1) % 3)

            def spread(eng, step):
                def static(b):
                    step(b, b % 3, base(b % 3) + b // 3, base((b + 1) % 3) + (b + 1) // 3)

                static(0)
                with eng.Fori(0, 4) as i:
                    for q in range(3):
                        r, r1 = (1 + q) % 3, (2 + q) % 3
                        step(i * 3 + 1 + q, r, i + base(r) + (1 + q) // 3, i + base(r1) + (2 + q) // 3)
                for b in range(13, B):
                    static(b)

            def scalar(act):
                act.activation(idle[:, :], one[:, :], ACT.Exp)

                def step(b, r):
                    for k in range(STEPS):
                        m = (n0 + b) * STEPS + k
                        at_least(act, at_pv, m - 2)
                        act.wait_ge(at_scores, m + 1)
                        act.activation(probs[k % 3], ps[0:KN, 4 + k % 2, 0:GT], ACT.Exp, scale=scale).then_inc(at_probs, 1)
                        if k == 4 and has_prev(b):
                            out.copy_turned(act, o0 + b - 1, (r + 2) % 3)
                    act.wait_ge(at_pv, (n0 + b + 1) * STEPS)
                    out.copy_sums(act, o0 + b, r)

                schedule(act, step)
                out.copy_turned(act, o0 + B - 1, (B - 1) % 3)

            def vector(dve):
                dve.memset(ps[:, SUMS, :], 0.0)
                for r in range(3):
                    dve.memset(keys[r][SROWS:AROWS, :, :], 1.0).then_inc(at_ones, 1)

                def reduce_pair(b, r, p):
                    k = (n0 + b) * PAIRS + p
                    dve.wait_ge(at_pair, k + 1)
                    dve.tensor_reduce(negmax[r][:, 2 * p:2 * p + 2], ps[0:T, 2 * (p % 2):2 * (p % 2) + 2, 0:S2], AX.X, ALU.max,
                                      negate=True).then_inc(at_max, 1)

                def clamp(b, r):
                    dve.wait_ge(at_max, (n0 + b + 1) * PAIRS)
                    dve.tensor_scalar(negmax_c[r], negmax[r], 0.1 * -NEG, None, ALU.min).then_inc(at_clamped, 1)

                def split_rows(b, r):
                    n = n0 + b
                    dve.wait_ge(at_mturn, n + 1)
                    dve.tensor_copy(maxrow[r][:, 0, :], ps[0:H, MISC, 0:T]).then_inc(at_mhi, 1)
                    dve.wait_ge(at_mhi, n + 1)
                    dve.tensor_tensor(maxrow[r][:, 1, :], ps[0:H, MISC, 0:T], maxrow[r][:, 0, :], ALU.subtract).then_inc(at_mmid, 1)

                def penalty(b, r, turn):
                    dve.wait_ge(at_mask[r], (turn + 1) * 32)
                    at_least(dve, at_pv, (n0 + b - 2) * STEPS)
                    dve.tensor_scalar(mask_in[r].bitcast(F32), mask_in[r], 0, None, ALU.is_equal).then_inc(at_pen0, 1)
                    dve.wait_ge(at_pen0, p0 + b + 1)
                    dve.scalar_tensor_tensor(pen[r], pad_in[r], 0, mask_in[r].bitcast(F32), ALU.is_equal, ALU.add).then_inc(at_pen, 1)

                if masked:
                    penalty(0, 0, 0)
                    penalty(1, 1, 0)
                for p in range(PAIRS):
                    reduce_pair(0, 0, p)
                clamp(0, 0)
                split_rows(0, 0)

                def step(b, r, turn, turn_next):
                    r1, last = (r + 1) % 3, o0 + b - 1
                    for p in range(PAIRS):
                        if has_next(b):
                            reduce_pair(b + 1, r1, p)
                        if p == 1 and has_prev(b):
                            out.normalise(dve, last, (r + 2) % 3)
                        if p == 6 and has_prev(b):
                            out.add(dve, last, b - 1)
                        if p == 6 and masked and (not isinstance(b, int) or b < B - 2):
                            penalty(b + 2, (r + 2) % 3, turn - base(r) + (r + 2) // 3)
                    if has_next(b):
                        clamp(b + 1, r1)
                        split_rows(b + 1, r1)

                spread(dve, step)
                out.normalise(dve, o0 + B - 1, (B - 1) % 3)
                out.add(dve, o0 + B - 1, B - 1)

            stage(sync, None, scalar, vector, tensor)

        se_inv = sem("se_inv")
        se_loaded = [sem("se_loaded0"), sem("se_loaded1")]
        se_group, se_v, se_vout, se_ones = sem("se_group"), sem("se_v"), sem("se_vout"), sem("se_ones")
        se_scores, se_masked, se_max, se_shifted = sem("se_scores"), sem("se_masked"), sem("se_max"), sem("se_shifted")
        se_probs, se_pturn, se_pcopied, se_pv = sem("se_probs"), sem("se_pturn"), sem("se_pcopied"), sem("se_pv")

        def self_stage(s, w, scale, dest, gate):
            arena.clear()
            wreg.clear()
            masks_ready = expect(2)
            o0 = out_count[0] * B
            out_count[0] += 1
            keys = [wreg.take(SROWS, H, T, dtype=BF16) for _ in range(2)]
            queries = [wreg.take(SROWS, H, T, dtype=BF16) for _ in range(2)]
            group_t = wreg.take(128, DC, GT)
            am = wreg.take(T, T)
            pm = arena.take(T, B, T)
            out = Output(w, dest, gate)
            vals = [arena.take(T, H, VW) for _ in range(2)]
            masked = [arena.take(T, 4, T) for _ in range(2)]
            probs = [arena.take(T, 4, T) for _ in range(2)]
            probs_t = [arena.take(T, 4, T) for _ in range(2)]
            negmax = arena.take(T, H)
            LOADS = 2 * len(K_PART)
            Q4 = 4

            def sync(sp):
                sp.dma_start(am, a["am"][0, 0]).then_inc(loaded, 16)
                sp.dma_start(pm, a["pm"].rearrange("b o u k -> (o u) b k").squeeze(0).partition_broadcast(T)).then_inc(loaded, 16)

                def load(b, u):
                    for j in range(len(K_PART)):
                        for kind, dst, part in ((1, keys, K_PART[j]), (0, queries, Q_PART[j])):
                            sp.dma_start(dst[u][DH * j:DH * j + DH, :, :],
                                         query_parts[kind, part, :, bass.ds(b * T, T)].rearrange("(h d) k -> d h k", d=DH)).then_inc(se_loaded[u], 16)

                load(0, 0)
                load(1, 1)
                with sp.Fori(1, B // 2) as i:
                    for u in range(2):
                        sp.wait_ge(se_scores, (i * 2 + u - 1) * 4)
                        load(i * 2 + u, u)
                sp.wait_ge(loaded, masks_ready)

            def gpsimd(pool):
                pool.wait_ge(loaded, masks_ready)
                pool.tensor_tensor(pm, pm, am.unsqueeze(1).broadcast_to([T, B, T]), ALU.mult).then_inc(se_inv, 1)
                pool.wait_ge(se_inv, 1)
                pool.tensor_scalar(pm, pm, -1.0, 1.0, ALU.mult, ALU.add).then_inc(se_inv, 1)
                pool.wait_ge(se_inv, 2)
                pool.tensor_scalar(pm, pm, -1.0e9, None, ALU.mult).then_inc(se_inv, 1)

            def tensor(pe):
                def scores(b, u, k):
                    m = b * 4 + k
                    at_least(pe, se_masked, m - 1)
                    for g in range(Q4):
                        hd = 4 * k + g
                        mm = pe.matmul(ps[0:T, k % 2, g * T:(g + 1) * T], queries[u][:, hd, :], keys[u][:, hd, :], start=True, stop=True)
                    mm.then_inc(se_scores, 1)

                def turn(b, k):
                    m = b * 4 + k
                    pe.wait_ge(se_probs, m + 1)
                    at_least(pe, se_pcopied, m - 1)
                    for g in range(Q4):
                        mm = pe.transpose(ps[0:T, 2 + k % 2, g * T:(g + 1) * T], probs[k % 2][:, g, :], ident[0:T, 0:T])
                    mm.then_inc(se_pturn, 1)

                def weigh(b, u, k):
                    m = b * 4 + k
                    pe.wait_ge(se_pcopied, m + 1)
                    if k == 0:
                        pe.wait_ge(se_vout, b + 1)
                        at_least(pe, o_copied, o0 + b)
                    for g in range(Q4):
                        mm = pe.matmul(ps[32 * g:32 * g + VW, SUMS, k * T:(k + 1) * T], vals[u][:, 4 * k + g, :],
                                       probs_t[k % 2][:, g, :], start=True, stop=True)
                    mm.then_inc(se_pv, 1)

                pe.wait_ge(se_ones, 3)

                def step(g):
                    for q in range(GB):
                        u = q % 2
                        b = g * GB + q
                        if q == 0:
                            pe.wait_ge(se_group, g + 1)
                        pe.wait_ge(se_loaded[u], (g * 2 + q // 2 + 1) * (16 * LOADS))
                        scores(b, u, 0)
                        scores(b, u, 1)
                        for c in range(DC):
                            mm = pe.matmul(ps[0:T, 4, 0:D], group_t[:, c, q * T:(q + 1) * T], w[:, 2, c, :], start=(c == 0), stop=(c == DC - 1))
                        mm.then_inc(se_v, 1)
                        turn(b, 0)
                        scores(b, u, 2)
                        turn(b, 1)
                        scores(b, u, 3)
                        weigh(b, u, 0)
                        turn(b, 2)
                        weigh(b, u, 1)
                        turn(b, 3)
                        weigh(b, u, 2)
                        weigh(b, u, 3)
                        n = o0 + b
                        out.turn_back(pe, n, u)
                        out.turn(pe, n, u)
                        out.project(pe, n, u)

                first(pe, step)

            def scalar(act):
                act.activation(idle[:, :], one[:, :], ACT.Exp)

                def step(g):
                    for q in range(GB):
                        u, b = q % 2, g * GB + q
                        for k in range(4):
                            m = b * 4 + k
                            act.wait_ge(se_shifted, m + 1)
                            at_least(act, se_pturn, m - 1)
                            act.activation(probs[k % 2], masked[k % 2], ACT.Exp).then_inc(se_probs, 1)
                            if k > 0:
                                copy(act, b, k - 1)
                        copy(act, b, 3)
                        act.wait_ge(se_pv, b * 4 + 4)
                        out.copy_sums(act, o0 + b, u)
                        out.copy_turned(act, o0 + b, u)

                def copy(act, b, k):
                    m = b * 4 + k
                    act.wait_ge(se_pturn, m + 1)
                    at_least(act, se_pv, m - 1)
                    act.activation(probs_t[k % 2], ps[0:T, 2 + k % 2, 0:GT].rearrange("p (g t) -> p g t", g=4), ACT.Copy).then_inc(se_pcopied, 1)

                first(act, step)

            def first(eng, step):
                step(0)
                with eng.Fori(1, G) as g:
                    step(g)

            def vector(dve):
                dve.memset(ps[:, SUMS, :], 0.0).then_inc(se_ones, 1)
                for u in range(2):
                    dve.memset(vals[u], 1.0).then_inc(se_ones, 1)
                dve.wait_ge(se_inv, 3)

                def step(g):
                    at_least(dve, se_v, g * GB)
                    dve.tensor_copy(group_t, xn_t[:, :, bass.ds(g * GT, GT)]).then_inc(se_group, 1)
                    for q in range(GB):
                        u, b = q % 2, g * GB + q
                        n = o0 + b
                        dve.wait_ge(se_v, b + 1)
                        at_least(dve, se_pv, (b - 1) * 4)
                        dve.tensor_tensor(vals[u][:, :, 0:DH], ps[0:T, 4, 0:D].rearrange("p (h e) -> p h e", h=H),
                                          attn_rows[0:T, 0, :].rearrange("p (h e) -> p h e", h=H), ALU.add).then_inc(se_vout, 1)
                        for k in range(4):
                            m = b * 4 + k
                            dve.wait_ge(se_scores, m + 1)
                            at_least(dve, se_probs, m - 1)
                            dve.scalar_tensor_tensor(masked[k % 2], ps[0:T, k % 2, 0:GT].rearrange("p (g t) -> p g t", g=4), scale,
                                                     pm[:, bass.ds(b, 1), :].broadcast_to([T, 4, T]), ALU.mult, ALU.add).then_inc(se_masked, 1)
                            dve.wait_ge(se_masked, m + 1)
                            dve.tensor_reduce(negmax[:, 4 * k:4 * k + 4], masked[k % 2], AX.X, ALU.max).then_inc(se_max, 1)
                            dve.wait_ge(se_max, m + 1)
                            dve.tensor_tensor(masked[k % 2], masked[k % 2], negmax[:, 4 * k:4 * k + 4].unsqueeze(2).broadcast_to([T, 4, T]),
                                              ALU.subtract).then_inc(se_shifted, 1)
                        out.normalise(dve, n, u)
                        out.add(dve, n, b)

                first(dve, step)

            stage(sync, gpsimd, scalar, vector, tensor)

        def groups(eng, step):
            step(0)
            with eng.Fori(1, G) as g:
                step(g)

        expert_w = [sem("expert_w0"), sem("expert_w1")]
        e0_h, e0_gate, e0_act, e0_out, e0_kept = sem("e0_h"), sem("e0_gate"), sem("e0_act"), sem("e0_out"), sem("e0_kept")
        e0_turned, e0_added = sem("e0_turned"), sem("e0_added")

        def position_experts_stage(gate):
            arena.clear()
            wreg.clear()
            TE = T // E
            NT = B * TE
            NF = len(F0_ROWS)
            w1 = [wreg.take(128, DC, F0) for _ in range(2)]
            w3 = [wreg.take(128, DC, F0) for _ in range(2)]
            w2 = [wreg.take(128, NF, D) for _ in range(2)]
            hid = [arena.take(128, NF, NT) for _ in range(2)]
            silu = [arena.take(128, NT) for _ in range(2)]
            out_t = arena.take(128, DC, B * T)
            stage_in = [arena.take(128, DC, NT) for _ in range(2)]
            rows = F0_ROWS

            def experts(eng, step):
                step(0, 0, 0)
                step(1, 1, 0)
                with eng.Fori(1, E // 2) as i:
                    step(i * 2, 0, i)
                    step(i * 2 + 1, 1, i)

            def sync(sp):
                def step(e, u, i):
                    at_least(sp, e0_out, (e - 1) * DC)
                    sp.dma_start(w1[u], a["e0_w1"][e]).then_inc(expert_w[u], 16)
                    sp.dma_start(w3[u], a["e0_w3"][e]).then_inc(expert_w[u], 16)
                    sp.dma_start(w2[u][:, 0:4, :], a["e0_w2"][e]).then_inc(expert_w[u], 16)
                    sp.dma_start(w2[u][0:96, 4:6, :], a["e0_w2r"][e]).then_inc(expert_w[u], 16)

                experts(sp, step)
                for u in range(2):
                    sp.wait_ge(expert_w[u], 64 * E // 2)

            def tensor(pe):
                def step(e, u, i):
                    pe.wait_ge(expert_w[u], (i + 1) * 64)
                    for f in range(NF):
                        k = e * NF + f
                        at_least(pe, e0_act, k - 1)
                        for q, w in ((0, w1[u]), (1, w3[u])):
                            for c in range(DC):
                                mm = pe.matmul(ps[0:rows[f], f % 2, q * NT:(q + 1) * NT], w[:, c, F0_AT[f]:F0_AT[f] + rows[f]],
                                               xn_t[:, c, :].rearrange("p (b t) -> p b t", t=T)[:, :, bass.ds(e * TE, TE)],
                                               start=(c == 0), stop=(c == DC - 1))
                        mm.then_inc(e0_h, 1)
                    for c in range(DC):
                        at_least(pe, e0_kept, e * DC + c - 1)
                        for f in range(NF):
                            if c == 0:
                                pe.wait_ge(e0_act, e * NF + f + 1)
                            mm = pe.matmul(ps[:, 2 + c, 0:NT], w2[u][0:rows[f], f, c * 128:(c + 1) * 128], hid[u][0:rows[f], f, :],
                                           start=(f == 0), stop=(f == NF - 1))
                        mm.then_inc(e0_out, 1)

                experts(pe, step)
                for b in range(B):
                    at_least(pe, e0_added, b - 1)
                    if b == 0:
                        pe.wait_ge(e0_kept, E * DC)
                    for c in range(DC):
                        mm = pe.transpose(ps[0:T, 4 + b % 2, c * 128:(c + 1) * 128], out_t[:, c, b * T:(b + 1) * T], ident[:, :])
                    mm.then_inc(e0_turned, 1)

            def scalar(act):
                act.activation(idle[:, :], one[:, :], ACT.Silu)

                def step(e, u, i):
                    for f in range(NF):
                        k = e * NF + f
                        act.wait_ge(e0_h, k + 1)
                        at_least(act, e0_act, k - 1)
                        act.activation(silu[f % 2][0:rows[f], :], ps[0:rows[f], f % 2, 0:NT], ACT.Silu).then_inc(e0_gate, 1)
                    for c in range(DC):
                        act.wait_ge(e0_out, e * DC + c + 1)
                        act.activation(out_t[:, c, :].rearrange("p (b t) -> p b t", t=T)[:, :, bass.ds(e * TE, TE)],
                                       ps[:, 2 + c, 0:NT].rearrange("p (b t) -> p b t", t=TE), ACT.Copy).then_inc(e0_kept, 1)

                experts(act, step)

            def vector(dve):
                def step(e, u, i):
                    for f in range(NF):
                        k = e * NF + f
                        dve.wait_ge(e0_gate, k + 1)
                        if f == 0:
                            at_least(dve, e0_out, (e - 1) * DC)
                        dve.tensor_tensor(hid[u][0:rows[f], f, :], silu[f % 2][0:rows[f], :], ps[0:rows[f], f % 2, NT:2 * NT],
                                          ALU.mult).then_inc(e0_act, 1)

                experts(dve, step)
                for b in range(B):
                    dve.wait_ge(e0_turned, b + 1)
                    dve.scalar_tensor_tensor(x[:, b, :], ps[0:T, 4 + b % 2, 0:D], gates[0:T, gate:gate + 1], x[:, b, :],
                                             ALU.mult, ALU.add).then_inc(e0_added, 1)

            stage(sync, None, scalar, vector, tensor)

        rt_in, rt_logits, rt_step, rt_exp = sem("rt_in"), sem("rt_logits"), sem("rt_step"), sem("rt_exp")
        rt_count = {"call": 0, "step": 0}

        class TopTwo:

            def __init__(self, router, bias=None):
                self.n = rt_count["call"]
                rt_count["call"] += 1
                self.router, self.bias = router, bias
                self.logits, self.rank, self.equal = (arena.take(T, B, E) for _ in range(3))
                self.best, self.found, self.second, self.gap, self.grown = (arena.take(T, B) for _ in range(5))
                self.onehot = [arena.take(T, B, E) for _ in range(2)]
                self.weight = [arena.take(T, B) for _ in range(2)]
                self.steps = rt_count["step"]

            def make_ranks(self, pool):
                for e in range(E):
                    pool.memset(self.rank[:, :, e], float(E - e)).then_inc(rt_in, 1)

            def logits_pe(self, pe):
                for b in range(B):
                    for c in range(DC):
                        mm = pe.matmul(ps[0:T, 0, b * E:(b + 1) * E], xn_t[:, c, b * T:(b + 1) * T], self.router[:, c, :],
                                       start=(c == 0), stop=(c == DC - 1))
                mm.then_inc(rt_logits, 1)

            def exp_act(self, act):
                act.wait_ge(rt_step, self.gap_step)
                act.activation(self.grown, self.gap, ACT.Exp).then_inc(rt_exp, 1)

            def plan(self):
                self.gap_step = self.steps + 14
                rt_count["step"] = self.steps + 17

            def choose(self, dve):
                def link(ins):
                    self.steps += 1
                    ins.then_inc(rt_step, 1)
                    dve.wait_ge(rt_step, self.steps)

                def over(v):
                    return v.unsqueeze(2).broadcast_to([T, B, E])

                dve.wait_ge(rt_in, E * (self.n + 1))
                dve.wait_ge(rt_logits, self.n + 1)
                logits = ps[0:T, 0, 0:B * E].rearrange("p (b e) -> p b e", e=E)
                if self.bias is None:
                    link(dve.tensor_copy(self.logits, logits))
                else:
                    link(dve.tensor_tensor(self.logits, logits, self.bias.unsqueeze(1).broadcast_to([T, B, E]), ALU.add))
                for k, top in ((0, self.best), (1, self.second)):
                    link(dve.tensor_reduce(top, self.logits, AX.X, ALU.max))
                    link(dve.tensor_tensor(self.equal, self.logits, over(top), ALU.is_equal))
                    link(dve.tensor_tensor(self.equal, self.equal, self.rank, ALU.mult))
                    link(dve.tensor_reduce(self.found, self.equal, AX.X, ALU.max))
                    link(dve.tensor_tensor(self.onehot[k], self.equal, over(self.found), ALU.is_equal))
                    if k == 0:
                        link(dve.scalar_tensor_tensor(self.logits, self.onehot[0], NEG, self.logits, ALU.mult, ALU.add))
                    else:
                        link(dve.tensor_tensor(self.gap, self.second, self.best, ALU.subtract))
                link(dve.tensor_copy(self.found, self.gap))
                dve.wait_ge(rt_exp, self.n + 1)
                link(dve.tensor_scalar(self.found, self.grown, 1.0, None, ALU.add))
                link(dve.reciprocal(self.weight[0], self.found))
                link(dve.tensor_tensor(self.weight[1], self.grown, self.weight[0], ALU.mult))

        e1_mask, e1_maskt, e1_maskc = sem("e1_mask"), sem("e1_maskt"), sem("e1_maskc")
        e1_low, e1_lowc, e1_lowm, e1_hid = sem("e1_low"), sem("e1_lowc"), sem("e1_lowm"), sem("e1_hid")
        e1_gate, e1_act, e1_z, e1_zm, e1_out, e1_added = (sem("e1_gate"), sem("e1_act"), sem("e1_z"), sem("e1_zm"),
                                                          sem("e1_out"), sem("e1_added"))

        def lora_experts_stage(gate):
            arena.clear()
            wreg.clear()
            wlow.clear()
            LORA_SCALE = 2.0
            wg, wu = wreg.take(128, DC, F), wreg.take(128, DC, F)
            wd = wreg.take(128, FC, D)
            a1, a3 = wreg.take(128, DC, ER), wreg.take(128, DC, ER)
            b1, b3 = wreg.take(128, F), wreg.take(128, F)
            a2 = wreg.take(128, FC, ER)
            b2 = wreg.take(128, D)
            router = wreg.take(128, DC, E)
            top = TopTwo(router)
            top.plan()
            wide = [arena.take(T, E, ER // E, dtype=BF16) for _ in range(2)]
            mask_t = arena.take(128, 2, B * T, dtype=BF16)
            weight = arena.take(T, 2, B)
            low = arena.take(128, 2, GT)
            lowm = [[arena.take(128, GT) for _ in range(2)] for _ in range(2)]
            act_t = [arena.take(128, FC, GT) for _ in range(2)]
            silu = [arena.take(128, GT) for _ in range(2)]
            zm = [arena.take(128, GT) for _ in range(2)]
            weights_ready = expect(10)
            order = [(0, 0)]
            for f in range(1, FC):
                order += [(f, 0), (f - 1, 1)]
            order.append((FC - 1, 1))
            when = {fk: n for n, fk in enumerate(order)}

            def sync(sp):
                for dst, name in ((router, "e1_router"), (a1, "e1_a1"), (a3, "e1_a3"), (wg, "e1_gate"), (wu, "e1_up"), (b1, "e1_b1"),
                                  (b3, "e1_b3"), (wd, "e1_down"), (a2, "e1_a2"), (b2, "e1_b2")):
                    sp.dma_start(dst, a[name]).then_inc(loaded, 16)
                sp.wait_ge(loaded, weights_ready)

            def gpsimd(pool):
                top.make_ranks(pool)

            def tensor(pe):
                pe.wait_ge(loaded, weights_ready)
                top.logits_pe(pe)
                for b in range(B):
                    for k in range(2):
                        m = b * 2 + k
                        pe.wait_ge(e1_mask, m + 1)
                        if b % GB == 0 and b >= 2 * GB:
                            pe.wait_ge(e1_maskc, (b // GB - 1) * 2)
                        mm = pe.matmul(ps[:, 2 + 2 * (b // GB % 2) + k, (b % GB) * T:(b % GB + 1) * T], wide[k].rearrange("p e r -> p (e r)"),
                                       ident16[:, :], start=True, stop=True)
                        mm.then_inc(e1_maskt, 1)
                pe.wait_ge(e1_maskc, 2 * G)

                def hidden(g, f, k):
                    for q, (w, bq) in enumerate(((wg, b1), (wu, b3))):
                        dst = ps[:, 2 + 2 * (f % 3) + q, 0:GT]
                        if k == 0:
                            for c in range(DC):
                                pe.matmul(dst, w[:, c, f * 128:(f + 1) * 128], xn_t[:, c, bass.ds(g * GT, GT)],
                                          start=(c == 0), stop=False)
                        mm = pe.matmul(dst, bq[:, f * 128:(f + 1) * 128], lowm[q][k], start=False, stop=True, skip_group_check=k == 1)
                    mm.then_inc(e1_hid, 1)

                def step(g):
                    at_least(pe, e1_zm, g * 2)
                    for q, w in ((0, a1), (1, a3)):
                        for c in range(DC):
                            mm = pe.matmul(ps[:, q, 0:GT], w[:, c, :], xn_t[:, c, bass.ds(g * GT, GT)], start=(c == 0), stop=(c == DC - 1))
                        mm.then_inc(e1_low, 1)
                    at_least(pe, e1_added, g * GB * 2)
                    pe.wait_ge(e1_lowm, (g + 1) * 6)
                    for f in range(FC + 1):
                        if f < FC:
                            if f >= 3:
                                pe.wait_ge(e1_act, g * (FC * 2) + when[f - 3, 1] + 1)
                            hidden(g, f, 0)
                        if f > 0:
                            pe.wait_ge(e1_act, g * (FC * 2) + when[f - 1, 0] + 1)
                            hidden(g, f - 1, 1)
                    for k in range(2):
                        for f in range(FC):
                            pe.wait_ge(e1_act, g * (FC * 2) + when[f, k] + 1)
                            mm = pe.matmul(ps[:, k, 0:GT], a2[:, f, :], act_t[k][:, f, :], start=(f == 0), stop=(f == FC - 1))
                        mm.then_inc(e1_z, 1)
                    pe.wait_ge(e1_act, (g + 1) * (FC * 2))
                    for q in range(GB):
                        for k in range(2):
                            if q * 2 + k >= 6:
                                pe.wait_ge(e1_added, g * (GB * 2) + q * 2 + k - 5)
                            dst = ps[0:T, 2 + (q * 2 + k) % 6, 0:D]
                            for f in range(FC):
                                pe.matmul(dst, act_t[k][:, f, q * T:(q + 1) * T], wd[:, f, :], start=(f == 0), stop=False)
                            pe.wait_ge(e1_zm, g * 2 + k + 1)
                            pe.matmul(dst, zm[k][:, q * T:(q + 1) * T], b2, start=False, stop=True).then_inc(e1_out, 1)

                groups(pe, step)

            def scalar(act):
                top.exp_act(act)
                act.activation(idle[:, :], one[:, :], ACT.Silu)
                for g in range(G):
                    for k in range(2):
                        act.wait_ge(e1_maskt, (g * GB + GB - 1) * 2 + k + 1)
                        act.activation(mask_t[:, k, g * GT:(g + 1) * GT], ps[:, 2 + 2 * (g % 2) + k, 0:GT], ACT.Copy).then_inc(e1_maskc, 1)

                def step(g):
                    for q in range(2):
                        act.wait_ge(e1_low, g * 2 + q + 1)
                        at_least(act, e1_lowm, g * 6)
                        act.activation(low[:, q, :], ps[:, q, 0:GT], ACT.Copy).then_inc(e1_lowc, 1)
                    for n, (f, k) in enumerate(order):
                        m = g * (FC * 2) + n
                        act.wait_ge(e1_hid, m + 1)
                        at_least(act, e1_act, m - 1)
                        act.activation(silu[n % 2], ps[:, 2 + 2 * (f % 3), 0:GT], ACT.Silu).then_inc(e1_gate, 1)

                groups(act, step)

            def vector(dve):
                top.choose(dve)
                for k in range(2):
                    dve.tensor_scalar(weight[:, k, :], top.weight[k], gates[0:T, gate:gate + 1], None, ALU.mult)
                for b in range(B):
                    for k in range(2):
                        m = b * 2 + k
                        at_least(dve, e1_maskt, m - 1)
                        dve.tensor_scalar(wide[k], top.onehot[k][:, b, :].unsqueeze(2).broadcast_to([T, E, ER // E]), LORA_SCALE, None,
                                          ALU.mult).then_inc(e1_mask, 1)

                def step(g):
                    cols = bass.ds(g * GT, GT)
                    at_least(dve, e1_z, g * 2)
                    if isinstance(g, int):
                        dve.wait_ge(e1_maskc, 2 * G)
                    for q in range(2):
                        dve.wait_ge(e1_lowc, g * 2 + q + 1)
                        for k in range(2):
                            dve.tensor_tensor(lowm[q][k], low[:, q, :], mask_t[:, k, cols], ALU.mult).then_inc(e1_lowm, 1)
                        dve.wait_ge(e1_lowm, g * 6 + q * 3 + 2)
                        dve.tensor_tensor(lowm[q][1], lowm[q][1], lowm[q][0], ALU.subtract).then_inc(e1_lowm, 1)
                    at_least(dve, e1_out, g * (GB * 2))
                    for n, (f, k) in enumerate(order):
                        dve.wait_ge(e1_gate, g * (FC * 2) + n + 1)
                        dve.tensor_tensor(act_t[k][:, f, :], silu[n % 2], ps[:, 3 + 2 * (f % 3), 0:GT], ALU.mult).then_inc(e1_act, 1)
                    for k in range(2):
                        dve.wait_ge(e1_z, g * 2 + k + 1)
                        dve.tensor_tensor(zm[k], ps[:, k, 0:GT], mask_t[:, k, cols], ALU.mult).then_inc(e1_zm, 1)
                    for q in range(GB):
                        b = g * GB + q
                        for k in range(2):
                            m = g * (GB * 2) + q * 2 + k
                            dve.wait_ge(e1_out, m + 1)
                            at_least(dve, e1_added, m)
                            dve.scalar_tensor_tensor(x[:, b, :], ps[0:T, 2 + (q * 2 + k) % 6, 0:D], weight[:, k, bass.ds(b, 1)], x[:, b, :],
                                                     ALU.mult, ALU.add).then_inc(e1_added, 1)

                groups(dve, step)

            stage(sync, gpsimd, scalar, vector, tensor)

        r_h, r_act, r_out, r_added = sem("r_h"), sem("r_act"), sem("r_out"), sem("r_added")

        def relu_stage():
            arena.clear()
            wreg.clear()
            w1, w2 = wreg.take(128, DC, F), wreg.take(128, FC, D)
            b1 = wreg.take(128, FC)
            weights_ready = expect(3)
            hid = [arena.take(128, FC, GT) for _ in range(2)]

            def sync(sp):
                for dst, name in ((w1, "r_w1"), (b1, "r_b1"), (w2, "r_w2")):
                    sp.dma_start(dst, a[name]).then_inc(loaded, 16)
                sp.wait_ge(loaded, weights_ready)

            def pairs(eng, step):
                step(0, 0)
                step(1, 1)
                with eng.Fori(1, G // 2) as i:
                    step(i * 2, 0)
                    step(i * 2 + 1, 1)

            def tensor(pe):
                pe.wait_ge(loaded, weights_ready)

                def step(g, u):
                    for f in range(FC):
                        n = g * FC + f
                        at_least(pe, r_act, n - 1)
                        for c in range(DC):
                            mm = pe.matmul(ps[:, f % 2, 0:GT], w1[:, c, f * 128:(f + 1) * 128], xn_t[:, c, bass.ds(g * GT, GT)],
                                           start=(c == 0), stop=(c == DC - 1))
                        mm.then_inc(r_h, 1)
                    pe.wait_ge(r_act, (g + 1) * FC)
                    for q in range(GB):
                        at_least(pe, r_added, g * GB + q - 1)
                        for f in range(FC):
                            mm = pe.matmul(ps[0:T, 2 + q % 2, 0:D], hid[u][:, f, q * T:(q + 1) * T], w2[:, f, :], start=(f == 0), stop=(f == FC - 1))
                        mm.then_inc(r_out, 1)

                pairs(pe, step)

            def scalar(act):
                act.wait_ge(loaded, weights_ready)

                def step(g, u):
                    at_least(act, r_out, (g - 1) * GB)
                    for f in range(FC):
                        act.wait_ge(r_h, g * FC + f + 1)
                        act.activation(hid[u][:, f, :], ps[:, f % 2, 0:GT], ACT.Relu, bias=b1[:, f:f + 1]).then_inc(r_act, 1)

                pairs(act, step)

            def vector(dve):
                def step(g, u):
                    for q in range(GB):
                        b = g * GB + q
                        dve.wait_ge(r_out, b + 1)
                        dve.tensor_tensor(h[:, b, :], h[:, b, :], ps[0:T, 2 + q % 2, 0:D], ALU.add).then_inc(r_added, 1)

                pairs(dve, step)

            stage(sync, None, scalar, vector, tensor)

        pk_zero, pk_group, pk_q, pk_qc = sem("pk_zero"), sem("pk_group"), sem("pk_q"), sem("pk_qc")
        pk_h, pk_gate, pk_act = sem("pk_h"), sem("pk_gate"), sem("pk_act")
        pk_emb, pk_silu, pk_sim, pk_simc = sem("pk_emb"), sem("pk_silu"), sem("pk_sim"), sem("pk_simc")
        pk_step, pk_gexp, pk_sum, pk_dexp, pk_kept = (sem("pk_step"), sem("pk_gexp"), sem("pk_sum"),
                                                              sem("pk_dexp"), sem("pk_kept"))
        pk_top = sem("pk_top")
        pk_mixed, pk_turned, pk_turnc, pk_out, pk_added = (sem("pk_mixed"), sem("pk_turned"), sem("pk_turnc"), sem("pk_out"), sem("pk_added"))

        def product_key_stage(gate):
            arena.clear()
            wreg.clear()
            wlow.clear()
            wg, wu = wreg.take(128, DC, F), wreg.take(128, DC, F)
            wd = wreg.take(128, FC, D)
            wq = wreg.take(128, DC, 2 * PH * PK)
            keys = wreg.take(128, 4, 2 * PK)
            de, ue = wreg.take(128, DC, NEXP), wreg.take(128, NEXP // 128, D)
            bcols = wreg.take(128, 2, FC)
            group_t = arena.take(128, DC, GT)
            q_t = arena.take(128, 4, GT)
            hid = arena.take(128, FC, GT)
            silu = [arena.take(128, GT) for _ in range(2)]
            act_e = [arena.take(T, NEXP) for _ in range(GB)]
            sims = [arena.take(T, 2 * PH, PK) for _ in range(GB)]
            sums = [arena.take(T, PI, PK) for _ in range(2)]
            exps = [arena.take(T, PI, PK) for _ in range(2)]
            mix = arena.take(T, NEXP)
            mix_t = arena.take(128, NEXP // 128, T)
            K = 8
            best = arena.take(T, 2 * PH, K)
            index = arena.take(T, PH, K, dtype=mybir.dt.uint32)
            beyond = arena.take(T, PH, K)
            grid, shifted, chosen = (arena.take(T, PH, K, K) for _ in range(3))
            top = arena.take(T, PH, K)
            negmax, total, share, clamped = (arena.take(T, PH) for _ in range(4))
            rowsum = arena.take(T, PH, K)
            rowclamp = arena.take(T, PH, K)
            last = arena.take(T, 2)
            weights_ready = expect(9)
            LINKS, SHIFTED = 16, 5

            def sync(sp):
                for dst, name in ((wq, "p_q"), (wg, "p_gate"), (wu, "p_up"), (bcols, "p_bcols"), (de, "p_down_e"), (wd, "p_down"), (ue, "p_up_e")):
                    sp.dma_start(dst, a[name]).then_inc(loaded, 16)
                sp.wait_ge(pk_zero, 1)
                for q in range(2):
                    sp.dma_start(keys[64 * q:64 * q + 64, :, 64 * q:64 * q + 64], a["p_keys"][64 * q:64 * q + 64]).then_inc(loaded, 16)
                sp.wait_ge(loaded, weights_ready)

            def tensor(pe):
                pe.wait_ge(loaded, weights_ready)

                def step(g):
                    pe.wait_ge(pk_group, g + 1)
                    for c in range(4):
                        if c < 2:
                            at_least(pe, pk_act, g * FC)
                        else:
                            pe.wait_ge(pk_qc, g * 4 + c - 1)
                        for d in range(DC):
                            mm = pe.matmul(ps[:, c % 2, 0:GT], wq[:, d, c * 128:(c + 1) * 128], group_t[:, d, :], start=(d == 0), stop=(d == DC - 1))
                        mm.then_inc(pk_q, 1)
                    pe.wait_ge(pk_qc, (g + 1) * 4)
                    at_least(pe, pk_turnc, g * GB * 2)
                    for f in range(FC):
                        at_least(pe, pk_act, g * FC + f - 1)
                        for q, w in ((0, wg), (1, wu)):
                            for d in range(DC):
                                mm = pe.matmul(ps[:, 2 * (f % 2) + q, 0:GT], w[:, d, f * 128:(f + 1) * 128], group_t[:, d, :],
                                               start=(d == 0), stop=(d == DC - 1))
                        mm.then_inc(pk_h, 1)
                    for q in range(GB):
                        n = g * GB + q
                        at_least(pe, pk_silu, n)
                        for e in range(2):
                            for d in range(DC):
                                mm = pe.matmul(ps[0:T, 4 + e, :], group_t[:, d, q * T:(q + 1) * T], de[:, d, e * 512:(e + 1) * 512],
                                               start=(d == 0), stop=(d == DC - 1))
                        mm.then_inc(pk_emb, 1)
                        at_least(pe, pk_simc, n)
                        for c in range(4):
                            mm = pe.matmul(ps[0:T, 6, c * 128:(c + 1) * 128], q_t[:, c, q * T:(q + 1) * T], keys[:, c, :], start=True, stop=True)
                        mm.then_inc(pk_sim, 1)
                    pe.wait_ge(pk_act, (g + 1) * FC)
                    for q in range(GB):
                        n = g * GB + q
                        at_least(pe, pk_added, n)
                        for f in range(FC):
                            pe.matmul(ps[0:T, 7, 0:D], hid[:, f, q * T:(q + 1) * T], wd[:, f, :], start=(f == 0), stop=False)
                        pe.wait_ge(pk_mixed, n + 1)
                        at_least(pe, pk_turnc, n * 2)
                        for k in range(NEXP // 128):
                            mm = pe.transpose(ps[:, 2 + k // 4, (k % 4) * T:(k % 4 + 1) * T], mix[:, k * 128:(k + 1) * 128], ident[0:T, 0:T])
                        mm.then_inc(pk_turned, 1)
                        pe.wait_ge(pk_turnc, n * 2 + 2)
                        for k in range(NEXP // 128):
                            mm = pe.matmul(ps[0:T, 7, 0:D], mix_t[:, k, :], ue[:, k, :], start=False, stop=(k == NEXP // 128 - 1))
                        mm.then_inc(pk_out, 1)

                groups(pe, step)

            def scalar(act):
                act.wait_ge(loaded, weights_ready)

                def turned(n):
                    act.wait_ge(pk_turned, n + 1)
                    at_least(act, pk_out, n)
                    for k in range(2):
                        act.activation(mix_t[:, 4 * k:4 * k + 4, :], ps[:, 2 + k, 0:4 * T].rearrange("p (k t) -> p k t", k=4),
                                       ACT.Copy).then_inc(pk_turnc, 1)

                def step(g):
                    at_least(act, pk_sim, g * GB)
                    for c in range(4):
                        act.wait_ge(pk_q, g * 4 + c + 1)
                        act.activation(q_t[:, c, :], ps[:, c % 2, 0:GT], ACT.Copy).then_inc(pk_qc, 1)
                    for f in range(FC):
                        n = g * FC + f
                        act.wait_ge(pk_h, n + 1)
                        at_least(act, pk_act, n - 1)
                        act.activation(silu[f % 2], ps[:, 2 * (f % 2), 0:GT], ACT.Silu, bias=bcols[:, 0, f:f + 1]).then_inc(pk_gate, 1)
                    for q in range(GB):
                        n = g * GB + q
                        act.wait_ge(pk_emb, n + 1)
                        at_least(act, pk_mixed, n - GB + 1)
                        act.activation(act_e[q].rearrange("p (e k) -> p e k", e=2), ps[0:T, 4:6, :], ACT.Silu).then_inc(pk_silu, 1)
                        act.wait_ge(pk_sim, n + 1)
                        at_least(act, pk_sum, (n - GB + 1) * PH)
                        act.activation(sims[q], ps[0:T, 6, :].rearrange("p (h k) -> p h k", k=PK), ACT.Copy).then_inc(pk_simc, 1)
                    for q in range(GB):
                        n = g * GB + q
                        act.wait_ge(pk_step, n * LINKS + SHIFTED)
                        act.activation(shifted, shifted, ACT.Exp).then_inc(pk_gexp, 1)
                        for hd in range(PH):
                            m = n * PH + hd
                            act.wait_ge(pk_sum, m + 1)
                            at_least(act, pk_kept, m - 1)
                            act.activation(exps[hd % 2], sums[hd % 2], ACT.Exp, bias=negmax[:, hd:hd + 1]).then_inc(pk_dexp, 1)
                        if q > 0:
                            turned(n - 1)
                    turned(g * GB + GB - 1)

                groups(act, step)

            def gpsimd(pool):
                pool.memset(keys, 0.0).then_inc(pk_zero, 1)

                def step(g):
                    at_least(pool, pk_emb, g * GB)
                    pool.tensor_copy(group_t, xn_t[:, :, bass.ds(g * GT, GT)]).then_inc(pk_group, 1)
                    for q in range(GB):
                        n = g * GB + q
                        pool.wait_ge(pk_simc, n + 1)
                        for hd in range(PH):
                            m = n * PH + hd
                            at_least(pool, pk_kept, m - 1)
                            pool.tensor_tensor(sums[hd % 2], sims[q][:, hd, 0:PI].unsqueeze(2).broadcast_to([T, PI, PK]),
                                               sims[q][:, PH + hd, :].unsqueeze(1).broadcast_to([T, PI, PK]), ALU.add).then_inc(pk_sum, 1)

                groups(pool, step)

            def vector(dve):
                dve.wait_ge(loaded, weights_ready)

                def add(n, b):
                    dve.wait_ge(pk_out, n + 1)
                    dve.scalar_tensor_tensor(x[:, b, :], ps[0:T, 7, 0:D], gates[0:T, gate:gate + 1], x[:, b, :], ALU.mult, ALU.add).then_inc(pk_added, 1)

                def mix_batch(g, q):
                    n = g * GB + q
                    done = [0]

                    def link(ins):
                        done[0] += 1
                        ins.then_inc(pk_step, 1)
                        dve.wait_ge(pk_step, n * LINKS + done[0])

                    def over(v):
                        return v.broadcast_to([T, PH, K * K])

                    def hold():
                        dve.memset(last[:, 1:2], 0.0)

                    flat = "p h i j -> p h (i j)"
                    dve.wait_ge(pk_simc, n + 1)
                    hold()
                    for s in range(2 * PH):
                        ins = dve.max(best[:, s, :], sims[q][:, s, :])
                    link(ins)
                    link(dve.tensor_tensor(grid, best[:, 0:PH, :].unsqueeze(3).broadcast_to([T, PH, K, K]),
                                           best[:, PH:2 * PH, :].unsqueeze(2).broadcast_to([T, PH, K, K]), ALU.add))
                    hold()
                    for s in range(PH):
                        ins = dve.max_index(index[:, s, :], best[:, s, :], sims[q][:, s, :])
                    for s in range(PH):
                        ins = dve.max(top[:, s, :], grid[:, s].rearrange("p i j -> p (i j)"))
                    link(ins)
                    at_least(dve, pk_dexp, n * PH)
                    link(dve.tensor_scalar(negmax, top[:, :, 0], -1.0, None, ALU.mult))
                    link(dve.tensor_tensor(shifted.rearrange(flat), grid.rearrange(flat), over(top[:, :, 0:1]), ALU.subtract))
                    link(dve.tensor_scalar(beyond, index, float(PI), None, ALU.is_ge))
                    link(dve.tensor_tensor(chosen.rearrange(flat), grid.rearrange(flat), over(top[:, :, K - 1:K]), ALU.is_ge))
                    dve.wait_ge(pk_gexp, n + 1)
                    link(dve.tensor_tensor(chosen.rearrange(flat), chosen.rearrange(flat), shifted.rearrange(flat), ALU.mult))
                    link(dve.tensor_reduce(rowsum, chosen, AX.X, ALU.add))
                    link(dve.tensor_reduce(total, rowsum, AX.X, ALU.add))
                    link(dve.reciprocal(share, total))
                    link(dve.tensor_tensor(rowclamp, rowsum, beyond, ALU.mult))
                    link(dve.tensor_reduce(clamped, rowclamp, AX.X, ALU.add))
                    link(dve.tensor_tensor(clamped, clamped, share, ALU.mult))
                    link(dve.tensor_reduce(last[:, 0:1], clamped, AX.X, ALU.add))
                    at_least(dve, pk_turned, n)
                    for hd in range(PH):
                        m = n * PH + hd
                        dve.wait_ge(pk_dexp, m + 1)
                        dve.scalar_tensor_tensor(exps[hd % 2], sums[hd % 2], top[:, hd, K - 1:K], exps[hd % 2], ALU.is_ge, ALU.mult).then_inc(pk_top, 1)
                        dve.wait_ge(pk_top, m + 1)
                        flat_e = exps[hd % 2].rearrange("p i j -> p (i j)")
                        if hd == 0:
                            dve.tensor_scalar(mix, flat_e, share[:, 0:1], None, ALU.mult).then_inc(pk_kept, 1)
                        else:
                            dve.wait_ge(pk_kept, m)
                            dve.scalar_tensor_tensor(mix, flat_e, share[:, hd:hd + 1], mix, ALU.mult, ALU.add).then_inc(pk_kept, 1)
                    dve.wait_ge(pk_kept, (n + 1) * PH)
                    link(dve.tensor_tensor(mix[:, NEXP - 1:NEXP], mix[:, NEXP - 1:NEXP], last[:, 0:1], ALU.add))
                    assert done[0] == LINKS
                    dve.wait_ge(pk_silu, n + 1)
                    dve.tensor_tensor(mix, mix, act_e[q], ALU.mult).then_inc(pk_mixed, 1)

                def step(g):
                    at_least(dve, pk_out, g * GB)
                    for f in range(FC):
                        dve.wait_ge(pk_gate, g * FC + f + 1)
                        dve.scalar_tensor_tensor(hid[:, f, :], ps[:, 2 * (f % 2) + 1, 0:GT], bcols[:, 1, f:f + 1], silu[f % 2],
                                                 ALU.add, ALU.mult).then_inc(pk_act, 1)
                    for q in range(GB):
                        mix_batch(g, q)
                        if q > 0:
                            add(g * GB + q - 1, g * GB + q - 1)
                    add(g * GB + GB - 1, g * GB + GB - 1)

                groups(dve, step)

            stage(sync, gpsimd, scalar, vector, tensor)

        m_ct, m_ctc, m_beta, m_badd = sem("m_ct"), sem("m_ctc"), sem("m_beta"), sem("m_badd")
        m_half, m_coef, m_h, m_gate, m_act, m_out = sem("m_half"), sem("m_coef"), sem("m_h"), sem("m_gate"), sem("m_act"), sem("m_out")
        m_bias, m_res, m_stat, m_aggr, m_eps_made, m_eps, m_rstd, m_scale, m_gain, m_added = (
            sem("m_bias"), sem("m_res"), sem("m_stat"), sem("m_aggr"), sem("m_eps_made"), sem("m_eps"), sem("m_rstd"), sem("m_scale"), sem("m_gain"), sem("m_added"))

        def routed_experts_stage(gate):
            arena.clear()
            wreg.clear()
            wlow.clear()
            EPS = 1e-12
            inputs_ready = expect(3)
            w0 = 64 * E // 2
            w_in = [wreg.take(128, 2, DC, F) for _ in range(2)]
            w_out = [wreg.take(128, FC, D) for _ in range(2)]
            rows = [wlow.take(T, 2, D) for _ in range(2)]
            beta = wlow.take(E, D)
            router = wlow.take(128, DC, E)
            br = arena.take(T, E)
            bcols = [arena.take(128, 2, FC) for _ in range(2)]
            half_b = [arena.take(128, FC) for _ in range(2)]
            top = TopTwo(router, br)
            top.plan()
            coef = arena.take(T, B, E)
            coef_tmp = arena.take(T, B, E)
            coef_t = [arena.take(E, T) for _ in range(2)]
            gelu = [arena.take(128, GT) for _ in range(2)]
            tanh = [arena.take(128, GT) for _ in range(2)]
            hid = [arena.take(128, FC, GT) for _ in range(2)]
            biased = [arena.take(T, D) for _ in range(GB)]
            res = [arena.take(T, D) for _ in range(GB)]
            gained = [arena.take(T, D) for _ in range(GB)]
            stats = arena.take(T, GB, 6)
            moments = arena.take(T, GB, 2)
            rstd = arena.take(T, 2, GB)
            eps = arena.take(T, GB)
            spare = arena.take(T, 2)

            def experts(eng, step):
                step(0, 0, 0)
                step(1, 1, 0)
                with eng.Fori(1, E // 2) as i:
                    step(i * 2, 0, i)
                    step(i * 2 + 1, 1, i)

            def sync(sp):
                for dst, src in ((router, a["m_router"]), (br, a["m_br"].partition_broadcast(T)), (beta, a["m_beta"])):
                    sp.dma_start(dst, src).then_inc(loaded, 16)

                def step(e, u, i):
                    at_least(sp, m_out, (e - 1) * B)
                    at_least(sp, m_gain, (e - 1) * B)
                    sp.dma_start(w_in[u], a["m_w"][e]).then_inc(expert_w[u], 16)
                    sp.dma_start(w_out[u], a["m_wo"][e]).then_inc(expert_w[u], 16)
                    sp.dma_start(bcols[u], a["m_bcols"][e]).then_inc(expert_w[u], 16)
                    sp.dma_start(rows[u], a["m_rows"][e].partition_broadcast(T)).then_inc(expert_w[u], 16)

                experts(sp, step)
                for u in range(2):
                    sp.wait_ge(expert_w[u], w0 + 64 * E // 2)

            def tensor(pe):
                pe.wait_ge(loaded, inputs_ready)
                top.logits_pe(pe)
                pe.wait_ge(m_coef, 4)
                for b in range(B):
                    at_least(pe, m_ctc, b - 1)
                    pe.transpose(ps[0:E, 1 + b % 2, 0:T], coef[:, b, :], ident[0:T, 0:T]).then_inc(m_ct, 1)
                    pe.wait_ge(m_ctc, b + 1)
                    at_least(pe, m_badd, b - 1)
                    pe.matmul(ps[0:T, 3 + b % 2, 0:D], coef_t[b % 2], beta, start=True, stop=True).then_inc(m_beta, 1)
                pe.wait_ge(m_badd, B)

                def step(e, u, i):
                    pe.wait_ge(expert_w[u], w0 + (i + 1) * 64)
                    for g in range(G):
                        for f in range(FC):
                            n = (e * G + g) * FC + f
                            at_least(pe, m_act, n - 1)
                            for q in range(2):
                                for c in range(DC):
                                    mm = pe.matmul(ps[:, 2 * (f % 2) + q, 0:GT], w_in[u][:, q, c, f * 128:(f + 1) * 128],
                                                   xn_t[:, c, g * GT:(g + 1) * GT], start=(c == 0), stop=(c == DC - 1))
                            mm.then_inc(m_h, 1)
                        pe.wait_ge(m_act, (e * G + g + 1) * FC)
                        for q in range(GB):
                            n = (e * G + g) * GB + q
                            at_least(pe, m_res, n - GB + 1)
                            for f in range(FC):
                                mm = pe.matmul(ps[0:T, 4 + q, 0:D], hid[g % 2][:, f, q * T:(q + 1) * T], w_out[u][:, f, :],
                                               start=(f == 0), stop=(f == FC - 1))
                            mm.then_inc(m_out, 1)

                experts(pe, step)

            def scalar(act):
                top.exp_act(act)
                act.activation(idle[:, :], one[:, :], ACT.Gelu)
                for b in range(B):
                    act.wait_ge(m_ct, b + 1)
                    at_least(act, m_beta, b - 1)
                    act.activation(coef_t[b % 2], ps[0:E, 1 + b % 2, 0:T], ACT.Copy).then_inc(m_ctc, 1)

                def step(e, u, i):
                    act.wait_ge(expert_w[u], w0 + (i + 1) * 64)
                    act.wait_ge(m_half, e + 1)
                    for g in range(G):
                        for f in range(FC):
                            n = (e * G + g) * FC + f
                            act.wait_ge(m_h, n + 1)
                            at_least(act, m_act, n - 1)
                            act.activation(gelu[f % 2], ps[:, 2 * (f % 2), 0:GT], ACT.Gelu, bias=bcols[u][:, 0, f:f + 1])
                            act.activation(tanh[f % 2], ps[:, 2 * (f % 2) + 1, 0:GT], ACT.Tanh, scale=0.5,
                                           bias=half_b[u][:, f:f + 1]).then_inc(m_gate, 1)

                experts(act, step)

            def vector(dve):
                dve.wait_ge(loaded, inputs_ready)
                top.choose(dve)
                weights = [w.unsqueeze(2).broadcast_to([T, B, E]) for w in top.weight]
                dve.tensor_tensor(coef, top.onehot[0], weights[0], ALU.mult).then_inc(m_coef, 1)
                dve.tensor_tensor(coef_tmp, top.onehot[1], weights[1], ALU.mult).then_inc(m_coef, 1)
                dve.wait_ge(m_coef, 2)
                dve.tensor_tensor(coef, coef, coef_tmp, ALU.add).then_inc(m_coef, 1)
                dve.wait_ge(m_coef, 3)
                dve.tensor_scalar(coef, coef, gates[0:T, gate:gate + 1], None, ALU.mult).then_inc(m_coef, 1)
                for b in range(B):
                    dve.wait_ge(m_beta, b + 1)
                    dve.tensor_tensor(x[:, b, :], x[:, b, :], ps[0:T, 3 + b % 2, 0:D], ALU.add).then_inc(m_badd, 1)

                def step(e, u, i):
                    dve.wait_ge(expert_w[u], w0 + (i + 1) * 64)
                    dve.tensor_scalar(half_b[u], bcols[u][:, 1, :], 0.5, None, ALU.mult).then_inc(m_half, 1)
                    for g in range(G):
                        k = (e * G + g) * GB
                        at_least(dve, m_out, k - GB)
                        for f in range(FC):
                            n = (e * G + g) * FC + f
                            dve.wait_ge(m_gate, n + 1)
                            dve.scalar_tensor_tensor(hid[g % 2][:, f, :], tanh[f % 2], 1.0, gelu[f % 2], ALU.add, ALU.mult).then_inc(m_act, 1)
                        for q in range(GB):
                            dve.wait_ge(m_out, k + q + 1)
                            dve.wait_ge(m_bias, k + q + 1)
                            dve.scalar_tensor_tensor(res[q], ps[0:T, 4 + q, 0:D], 0.5, biased[q], ALU.mult, ALU.add).then_inc(m_res, 1)
                        for q in range(GB):
                            dve.wait_ge(m_res, k + q + 1)
                            dve.bn_stats(stats[:, q, :], res[q]).then_inc(m_stat, 1)
                        dve.wait_ge(m_stat, k + GB)
                        dve.memset(spare, 0.0)
                        for q in range(GB):
                            dve.bn_aggr(moments[:, q, :], stats[:, q, :]).then_inc(m_aggr, 1)
                        dve.wait_ge(m_aggr, k + GB)
                        for q in range(GB):
                            dve.scalar_tensor_tensor(gained[q], res[q], moments[:, q, 0:1], rows[u][:, 1, :], ALU.subtract, ALU.mult).then_inc(m_gain, 1)
                        for q in range(GB):
                            dve.wait_ge(m_gain, k + q + 1)
                            dve.wait_ge(m_scale, e * G + g + 1)
                            b = g * GB + q
                            dve.scalar_tensor_tensor(x[:, b, :], gained[q], rstd[:, 1, q:q + 1], x[:, b, :], ALU.mult, ALU.add).then_inc(m_added, 1)

                experts(dve, step)

            def gpsimd(pool):
                top.make_ranks(pool)
                pool.memset(eps, EPS).then_inc(m_eps_made, 1)
                pool.wait_ge(m_eps_made, 1)
                pool.wait_ge(m_coef, 4)

                def step(e, u, i):
                    pool.wait_ge(expert_w[u], w0 + (i + 1) * 64)
                    for g in range(G):
                        k = (e * G + g) * GB
                        for q in range(GB):
                            at_least(pool, m_res, k + q - GB + 1)
                            pool.tensor_tensor(biased[q], h[:, g * GB + q, :], rows[u][:, 0, :], ALU.add).then_inc(m_bias, 1)
                        n = e * G + g
                        pool.wait_ge(m_aggr, k + GB)
                        at_least(pool, m_added, k)
                        pool.tensor_tensor(rstd[:, 0, :], moments[:, :, 1], eps, ALU.add).then_inc(m_eps, 1)
                        pool.wait_ge(m_eps, n + 1)
                        pool.tensor_tensor(rstd[:, 0, :], rstd[:, 0, :], half[:, 0:GB], ALU.pow).then_inc(m_rstd, 1)
                        pool.wait_ge(m_rstd, n + 1)
                        pool.tensor_tensor(rstd[:, 1, :], rstd[:, 0, :], coef[:, g * GB:(g + 1) * GB, bass.ds(e, 1)].rearrange("p b e -> p (b e)"),
                                           ALU.mult).then_inc(m_scale, 1)

                experts(pool, step)

            stage(sync, gpsimd, scalar, vector, tensor)

        stored = sem("stored")

        def end_sync(sp):
            sp.dma_start(a["out"].rearrange("b t d -> t b d"), x[:, :, :]).then_inc(stored, 16)
            sp.wait_ge(stored, 16)

        def chain():
            norm_stage(x, 1e-5)
            w = query_stage(0, 1)
            bias_stage(x, gates[0:T, 0:1], attn_rows[0:T, 1, :])
            cross_stage(0, w, 0.25, x, gates[0:T, 0:1])
            norm_stage(x, 1e-5)
            position_experts_stage(4)
            norm_stage(x, 1e-5)
            w = query_stage(1, 1)
            bias_stage(x, gates[0:T, 1:2], attn_rows[0:T, 1, :])
            cross_stage(1, w, 0.25, x, gates[0:T, 1:2])
            norm_stage(x, 1e-5)
            lora_experts_stage(5)
            norm_stage(x, 1e-5, keep=h)
            w = query_stage(2, 2)
            bias_stage(h, one[0:T, :], attn_rows[0:T, 1, :])
            self_stage(2, w, 0.25, h, one[0:T, :])
            norm_stage(h, 1e-6, gain=0, keep=h)
            w = query_stage(3, 1)
            bias_stage(h, one[0:T, :], attn_rows[0:T, 1, :])
            cross_stage(2, w, 0.25, h, one[0:T, :])
            norm_stage(h, 1e-6, gain=2, keep=h)
            bias_stage(h, one[0:T, :], attn_rows[0:T, 1, :], a["r_b2"])
            relu_stage()
            norm_stage(h, 1e-6, gain=4, turn=False, add_gate=2)
            norm_stage(x, 1e-5)
            bias_stage(x, gates[0:T, 6:7], attn_rows[0:T, 1, :], a["p_bd"])
            product_key_stage(6)
            norm_stage(x, 1e-5)
            w = query_stage(4, 1)
            bias_stage(x, gates[0:T, 3:4], attn_rows[0:T, 1, :])
            cross_stage(3, w, float(np.log(D) / np.sqrt(DH)), x, gates[0:T, 3:4], masked=True)
            norm_stage(x, 1e-5, keep=h)
            routed_experts_stage(7)

        chain()
        stage(sync=end_sync)

        @block.sync
        def _(sp):
            for program in programs["sync"]:
                program(sp)

        @block.gpsimd
        def _(pool):
            for program in programs["gpsimd"]:
                program(pool)

        @block.scalar
        def _(act):
            for program in programs["scalar"]:
                program(act)

        @block.vector
        def _(dve):
            for program in programs["vector"]:
                program(dve)

        @block.tensor
        def _(pe):
            for program in programs["tensor"]:
                program(pe)


def kernel(**inputs):
    import concourse.bacc as bacc
    from concourse.bass_utils import run_bass_kernel_spmd

    i = {k: np.asarray(v) for k, v in inputs.items()}

    def rows_first(w):
        return w.reshape(-1, 128, w.shape[-1]).transpose(1, 0, 2)

    def columns(v):
        return v.reshape(-1, 128).T

    def attn_set(names, turned):
        return np.stack([rows_first(i[n].T if turned else i[n]) for n in names], axis=1)

    sets = []
    for layer, names, turned in (("L0_xattn_", ("Wq", "Wk", "Wv", "Wo"), True), ("L1_xattn_", ("Wq", "Wk", "Wv", "Wo"), True),
                                 ("L2_xattn_", ("wq1", "wk1", "wv1", "wo1"), False), ("L2_xattn_", ("wq2", "wk2", "wv2", "wo2"), False),
                                 ("L3_xattn_", ("Wq", "Wk", "Wv", "Wo"), True)):
        sets.append(([layer + n for n in names], [layer + "b" + n[1:] for n in names], turned))
    arrays = {
        "x": i["x"],
        "g_xattn": i["g_xattn"],
        "g_ffn": i["g_ffn"],
        "ctx_t": i["ctx_1024"].transpose(0, 2, 1).reshape(B, DC, 128, S2).transpose(0, 2, 1, 3),
        "attn_w": np.stack([attn_set(w, turned) for w, _, turned in sets]),
        "attn_cols": np.stack([np.concatenate([columns(i[b[0]]), columns(i[b[1]])], axis=1) for _, b, _ in sets]),
        "attn_rows": np.stack([np.stack([i[b[2]], i[b[3]]]) for _, b, _ in sets]),
        "am": i["mask_1x1xSxS_fk0"],
        "pm": i["mask_Bx1x1xS_ff1"],
        "mask": i["mask_Bx1xSxS2_if1"].reshape(B, T, S2),
        "pad": i["mask_BxS2_if1"],
        "ln_rows": np.stack([i["L2_xattn_" + n] for n in ("g1", "be1", "g2", "be2", "g3", "be3")]),
        "e0_w1": i["L0_ffn_w1"].reshape(E, DC, 128, F0).transpose(0, 2, 1, 3),
        "e0_w3": i["L0_ffn_w3"].reshape(E, DC, 128, F0).transpose(0, 2, 1, 3),
        "e0_w2": i["L0_ffn_w2"][:, 0:512].reshape(E, 4, 128, D).transpose(0, 2, 1, 3),
        "e0_w2r": i["L0_ffn_w2"][:, 512:].reshape(E, 2, 96, D).transpose(0, 2, 1, 3),
        "e1_router": rows_first(i["L1_ffn_gate_w"].T),
        "e1_gate": rows_first(i["L1_ffn_w_gate"].T),
        "e1_up": rows_first(i["L1_ffn_w_up"].T),
        "e1_down": rows_first(i["L1_ffn_w_down"].T),
        "e1_a1": rows_first(i["L1_ffn_A1"].reshape(ER, D).T),
        "e1_a3": rows_first(i["L1_ffn_A3"].reshape(ER, D).T),
        "e1_b1": i["L1_ffn_B1"].transpose(0, 2, 1).reshape(ER, F),
        "e1_b3": i["L1_ffn_B3"].transpose(0, 2, 1).reshape(ER, F),
        "e1_a2": rows_first(i["L1_ffn_A2"].reshape(ER, F).T),
        "e1_b2": i["L1_ffn_B2"].transpose(0, 2, 1).reshape(ER, D),
        "r_w1": rows_first(i["L2_xattn_w_ff1"]),
        "r_b1": columns(i["L2_xattn_b_ff1"]),
        "r_w2": rows_first(i["L2_xattn_w_ff2"]),
        "r_b2": i["L2_xattn_b_ff2"],
        "p_gate": rows_first(i["L2_ffn_Wg"]),
        "p_up": rows_first(i["L2_ffn_Wu"]),
        "p_down": rows_first(i["L2_ffn_Wd"]),
        "p_bcols": np.stack([columns(i["L2_ffn_bg"]), columns(i["L2_ffn_bu"])], axis=1),
        "p_bd": i["L2_ffn_bd"],
        "p_q": rows_first(i["L2_ffn_Wq"]),
        "p_keys": i["L2_ffn_keys"].transpose(2, 0, 3, 1).reshape(4, 128, PK).transpose(1, 0, 2),
        "p_down_e": rows_first(i["L2_ffn_down_embed"].T),
        "p_up_e": rows_first(i["L2_ffn_up_embed"]),
        "m_router": rows_first(i["L3_ffn_Wr"]),
        "m_br": i["L3_ffn_br"],
        "m_w": np.stack([np.stack([rows_first(i["L3_ffn_Wi"][e]), rows_first(i["L3_ffn_Wg"][e])], axis=1) for e in range(E)]),
        "m_wo": np.stack([rows_first(i["L3_ffn_Wo"][e]) for e in range(E)]),
        "m_bcols": np.stack([np.stack([columns(i["L3_ffn_bi"][e]), columns(i["L3_ffn_bg"][e])], axis=1) for e in range(E)]),
        "m_rows": np.stack([i["L3_ffn_bo"], i["L3_ffn_gamma"]], axis=1),
        "m_beta": i["L3_ffn_beta"],
    }
    nc = bacc.Bacc("TRN2", target_bir_lowering=False, num_devices=1)
    feeds, views = {}, {}
    for name, array in arrays.items():
        array = np.ascontiguousarray(array)
        feeds["in_" + name] = array
        views[name] = nc.dram_tensor("in_" + name, array.shape, mybir.dt.from_np(array.dtype), kind="ExternalInput").ap()
    views["out"] = nc.dram_tensor("out", (B, T, D), F32, kind="ExternalOutput").ap()
    build(nc, views)
    result = run_bass_kernel_spmd(nc, [feeds], core_ids=[0])
    return result.results[0]["out"]
```

```python
from contextlib import ExitStack

import concourse.bass as bass
import numpy as np
from concourse import mybir

ACT = mybir.ActivationFunctionType
ALU = mybir.AluOpType
F32 = mybir.dt.float32
BF16 = mybir.dt.bfloat16
I32 = mybir.dt.int32
AX = mybir.AxisListType

B, T, D = 16, 112, 256
S2 = 375
KC, KN = 3, 125
H, DH = 16, 16
DC = D // 128
G, GB = 4, 4
GT = GB * T
PARTS = 3
VW = DH + 1
NEG = -1.0e30
K_PART = (0, 0, 1, 0, 2, 1)
Q_PART = (0, 1, 0, 2, 0, 1)
SROWS = DH * len(K_PART)
AROWS = SROWS + 2
E = 8
F0 = 704
F0_ROWS = (128, 128, 128, 128, 96, 96)
F0_AT = (0, 128, 256, 384, 512, 608)
F = 1024
FC = F // 128
ER = 128
PH, PK = 4, 64
NEXP = 1024
PI = NEXP // PK
BS = 256
BLOCKS = (2 * B * T + E * (BS - 1)) // BS
W_IN, W_OUT, W_B = 2 * DC * F, FC * D, 2 * FC
ATTN = 5
KV_SET = (0, 1, 3, 4)


class Region:

    def __init__(self, tensor, words):
        self.tensor, self.words, self.at = tensor, words, 0

    def clear(self):
        self.at = 0

    def take(self, parts, *dims, dtype=F32):
        count = 1
        for d in dims:
            count *= d
        words = (count + 1) // 2 if dtype == BF16 else count
        words += words % 2
        assert self.at + words <= self.words, (self.at, words)
        view = self.tensor[0:parts, self.at : self.at + words]
        self.at += words
        if dtype != F32:
            view = view.bitcast(dtype)
        view = view[:, 0:count]
        if len(dims) == 1:
            return view
        names = "abcdef"[: len(dims)]
        return view.rearrange(f"p ({' '.join(names)}) -> p {' '.join(names)}", **dict(zip(names, dims)))


def at_least(eng, sem, value):
    if not (isinstance(value, int) and value <= 0):
        eng.wait_ge(sem, value)


def batches(eng, step):
    step(0, 0, 0)
    step(1, 1, 0)
    with eng.Fori(1, B // 2) as i:
        step(i * 2, 0, i)
        step(i * 2 + 1, 1, i)


def build(nc, a):
    ctx = ExitStack()
    with ctx:
        def sb(name, shape, dt=F32):
            return ctx.enter_context(nc.sbuf_tensor(name, shape, dt))

        def sem(name):
            return ctx.enter_context(nc.semaphore(name))

        x = sb("x", [T, B, D])
        h = sb("h", [T, B, D])
        xn_t = sb("xn_t", [128, DC, B * T])
        ident = sb("ident", [128, 128])
        ident16 = sb("ident16", [T, T], BF16)
        neg16 = sb("neg16", [T, GB, T], BF16)
        gates = sb("gates", [128, 8])
        nought = sb("nought", [128, 2 * D])
        one = sb("one", [128, 1])
        idle = sb("idle", [128, 1])
        ln_raw = sb("ln_raw", [T, B, 6])
        ln_tmp = sb("ln_tmp", [T, 5, B])
        ln_mean = sb("ln_mean", [T, B])
        ln_rstd = sb("ln_rstd", [T, B])
        half = sb("half", [T, B])
        XN = 4
        xn2 = [sb(f"xn2_{r}", [T, D]) for r in range(XN)]
        ln_gain = sb("ln_gain", [128, 2, D])
        ln_scale = sb("ln_scale", [T, XN, D])
        attn_cols = sb("attn_cols", [128, ATTN, 4])
        attn_rows = sb("attn_rows", [128, 2, D])
        A_WORDS, W_WORDS, L_WORDS = 22528, 2 * (W_IN + W_OUT + W_B), 2048
        arena = Region(sb("arena", [128, A_WORDS]), A_WORDS)
        wreg = Region(sb("wreg", [128, W_WORDS]), W_WORDS)
        wlow = Region(sb("wlow", [128, L_WORDS]), L_WORDS)
        ps = ctx.enter_context(nc.psum_tensor("ps", [128, 8, 512], F32))

        key_parts = nc.dram_tensor("key_parts", (4, B, PARTS, D, S2), BF16, kind="Internal").ap()
        values = nc.dram_tensor("values", (4, B, KN, KC * H * VW), F32, kind="Internal").ap()
        query_parts = nc.dram_tensor("query_parts", (2, PARTS, D, B * T), BF16, kind="Internal").ap()

        sent = nc.dram_tensor("sent", (BLOCKS * BS, D), F32, kind="Internal").ap()
        returned = nc.dram_tensor("returned", (BLOCKS * BS, D), F32, kind="Internal").ap()

        block = ctx.enter_context(nc.Block())
        programs = {"sync": [], "gpsimd": [], "scalar": [], "vector": [], "tensor": []}

        stage_done = sem("stage_done")
        stages = [0]

        def stage(sync=None, gpsimd=None, scalar=None, vector=None, tensor=None, meet=True):
            stages[0] += meet
            all_done = 5 * stages[0]
            for name, program in (("sync", sync), ("gpsimd", gpsimd), ("scalar", scalar), ("vector", vector), ("tensor", tensor)):
                def whole(eng, program=program):
                    if program is not None:
                        program(eng)
                    if meet:
                        eng.drain().then_inc(stage_done, 1)
                        eng.wait_ge(stage_done, all_done)
                programs[name].append(whole)

        loaded = sem("loaded")
        loads = [0]

        def expect(transfers):
            loads[0] += 16 * transfers
            return loads[0]

        in_ready = expect(4)
        const_made = sem("const_made")
        cleared = sem("cleared")
        makes = [0]

        def expect_made(count):
            makes[0] += count
            return makes[0]

        start_made = expect_made(4)
        gate_in = arena.take(128, 8)

        def start_sync(sp):
            sp.dma_start(x[:, :, :], a["x"].rearrange("b t d -> t b d")).then_inc(loaded, 16)
            sp.dma_start(gate_in[:, 0:4], a["g_xattn"].partition_broadcast(128)).then_inc(loaded, 16)
            sp.dma_start(gate_in[:, 4:8], a["g_ffn"].partition_broadcast(128)).then_inc(loaded, 16)
            sp.dma_start(attn_cols[:, :, :], a["attn_cols"].rearrange("l p c -> p l c")).then_inc(loaded, 16)
            sp.wait_ge(loaded, in_ready)
            sp.wait_ge(const_made, start_made)
            rows_of = 2 * 128
            sp.dma_start(sent.rearrange("(j p q) d -> p j (q d)", p=128, q=2),
                         nought[:, :].unsqueeze(1).broadcast_to([128, BLOCKS * BS // rows_of, 2 * D])).then_inc(cleared, 16)

        def start_gpsimd(pool):
            pool.memset(ident[:, :], 0.0).then_inc(const_made, 1)
            pool.memset(ident16[:, :], 0.0).then_inc(const_made, 1)
            pool.memset(neg16[:, :, :], 0.0).then_inc(const_made, 1)
            pool.memset(nought[:, :], 0.0).then_inc(const_made, 1)
            pool.memset(half[:, :], -0.5)
            pool.memset(one[:, :], 1.0)
            pool.wait_ge(const_made, start_made)
            pool.affine_select(out=ident[:, :], in_=ident[:, :], compare_op=ALU.not_equal, fill=1.0, base=0,
                               pattern=[[-1, 128]], channel_multiplier=1)
            pool.affine_select(out=ident16[:, :], in_=ident16[:, :], compare_op=ALU.not_equal, fill=1.0, base=0,
                               pattern=[[-1, T]], channel_multiplier=1)
            pool.affine_select(out=neg16[:, :, :], in_=neg16[:, :, :], compare_op=ALU.not_equal, fill=NEG, base=0,
                               pattern=[[0, GB], [-1, T]], channel_multiplier=1)

        def start_scalar(act):
            act.wait_ge(loaded, in_ready)
            act.activation(gates[:, :], gate_in, ACT.Tanh)

        stage(sync=start_sync, gpsimd=start_gpsimd, scalar=start_scalar)

        kv_ctx = [sem("kv_ctx0"), sem("kv_ctx1")]
        kv_v = sem("kv_v")
        part_made, part_hi, part_res, part_mid, part_lo = sem("part_made"), sem("part_hi"), sem("part_res"), sem("part_mid"), sem("part_lo")
        kv_vout = sem("kv_vout")
        kv_kst, kv_vst = [sem("kv_kst0"), sem("kv_kst1")], [sem("kv_vst0"), sem("kv_vst1")]

        def context_stage():
            arena.clear()
            wreg.clear()
            NKV = len(KV_SET)
            weights_ready = expect(2 * NKV)
            ones_made = expect_made(2)
            ctx_t = [arena.take(128, DC, S2) for _ in range(2)]
            parts = [arena.take(128, DC, PARTS, S2, dtype=BF16) for _ in range(2)]
            rest = [arena.take(128, DC, S2) for _ in range(2)]
            vout = [arena.take(KN, KC, H, VW) for _ in range(2)]
            bv = arena.take(128, NKV, D)
            w = wreg.take(128, NKV, 2, DC, D)

            def sync(sp):
                for i, s in enumerate(KV_SET):
                    sp.dma_start(w[:, i], a["attn_w"][s, :, 1:3]).then_inc(loaded, 16)
                    sp.dma_start(bv[:, i, :], a["attn_rows"][s, 0].partition_broadcast(128)).then_inc(loaded, 16)
                sp.dma_start(ctx_t[0], a["ctx_t"][0]).then_inc(kv_ctx[0], 16)
                sp.dma_start(ctx_t[1], a["ctx_t"][1]).then_inc(kv_ctx[1], 16)

                def step(b, u, pair):
                    for i in range(NKV):
                        n = b * NKV + i
                        sp.wait_ge(part_lo, n * 2 + 2)
                        for t in range(DC):
                            sp.dma_start(key_parts[i, b, :, t * 128:(t + 1) * 128, :].rearrange("q p k -> p q k"),
                                         parts[i % 2][:, t]).then_inc(kv_kst[i % 2], 16)
                        sp.wait_ge(kv_vout, n * 2 + 2)
                        sp.dma_start(values[i, b], vout[i % 2].rearrange("p c h w -> p (c h w)")).then_inc(kv_vst[i % 2], 16)

                def more(b, u):
                    step(b, u, None)
                    sp.wait_ge(kv_v, (b * NKV + NKV) * 2)
                    sp.dma_start(ctx_t[u], a["ctx_t"][b + 2]).then_inc(kv_ctx[u], 16)

                with sp.Fori(0, B // 2 - 1) as i:
                    more(i * 2, 0)
                    more(i * 2 + 1, 1)
                step(B - 2, 0, None)
                step(B - 1, 1, None)
                for q in range(2):
                    sp.wait_ge(kv_kst[q], 16 * DC * B * NKV // 2)
                    sp.wait_ge(kv_vst[q], 16 * B * NKV // 2)

            def tensor(pe):
                pe.wait_ge(loaded, weights_ready)

                def step(b, u, pair):
                    pe.wait_ge(kv_ctx[u], pair * 16 + 16)
                    for i in range(NKV):
                        n = b * NKV + i
                        at_least(pe, part_res, (n - 1) * 2)
                        for t in range(DC):
                            for c in range(DC):
                                mm = pe.matmul(ps[:, 2 * (i % 2) + t, 0:S2], w[:, i, 0, c, t * 128:(t + 1) * 128],
                                               ctx_t[u][:, c, :], start=(c == 0), stop=(c == DC - 1))
                            mm.then_inc(part_made, 1)
                        at_least(pe, kv_vout, (n - 1) * 2)
                        for k in range(KC):
                            for c in range(DC):
                                mm = pe.matmul(ps[0:KN, 4 + 2 * (i % 2) + k // 2, (k % 2) * D:(k % 2 + 1) * D],
                                               ctx_t[u][:, c, k * KN:(k + 1) * KN], w[:, i, 1, c, :],
                                               start=(c == 0), stop=(c == DC - 1))
                            if k > 0:
                                mm.then_inc(kv_v, 1)

                batches(pe, step)

            def scalar(act):
                def step(b, u, pair):
                    for i, s in enumerate(KV_SET):
                        n = b * NKV + i
                        at_least(act, kv_kst[i % 2], (b * (NKV // 2) + i // 2) * (16 * DC))
                        for t in range(DC):
                            act.wait_ge(part_made, n * 2 + t + 1)
                            act.activation(parts[i % 2][:, t, 0, :], ps[:, 2 * (i % 2) + t, 0:S2], ACT.Identity,
                                           bias=attn_cols[:, s, 2 + t:3 + t]).then_inc(part_hi, 1)
                        for t in range(DC):
                            act.wait_ge(part_res, n * 2 + t + 1)
                            act.activation(parts[i % 2][:, t, 1, :], rest[i % 2][:, t, :], ACT.Copy).then_inc(part_mid, 1)

                batches(act, step)

            def vector(dve):
                for q in range(2):
                    dve.memset(vout[q], 1.0).then_inc(const_made, 1)
                dve.wait_ge(const_made, ones_made)
                dve.wait_ge(loaded, weights_ready)

                def step(b, u, pair):
                    for i, s in enumerate(KV_SET):
                        n = b * NKV + i
                        at_least(dve, part_lo, (n - 1) * 2)
                        for t in range(DC):
                            dve.wait_ge(part_hi, n * 2 + t + 1)
                            dve.scalar_tensor_tensor(rest[i % 2][:, t, :], ps[:, 2 * (i % 2) + t, 0:S2],
                                                     attn_cols[:, s, 2 + t:3 + t], parts[i % 2][:, t, 0, :],
                                                     ALU.add, ALU.subtract).then_inc(part_res, 1)
                        at_least(dve, kv_vst[i % 2], (b * (NKV // 2) + i // 2) * 16)
                        for k in range(2):
                            n_k = 2 - k
                            dve.wait_ge(kv_v, n * 2 + k + 1)
                            dve.tensor_tensor(vout[i % 2][:, 2 * k:2 * k + n_k, :, 0:DH],
                                              ps[0:KN, 4 + 2 * (i % 2) + k, 0:n_k * D].rearrange("p (c h e) -> p c h e", c=n_k, h=H),
                                              bv[0:KN, i, :].rearrange("p (h e) -> p h e", h=H).unsqueeze(1).broadcast_to([KN, n_k, H, DH]),
                                              ALU.add).then_inc(kv_vout, 1)

                batches(dve, step)

            def gpsimd(pool):
                def step(b, u, pair):
                    for i in range(NKV):
                        n = b * NKV + i
                        for t in range(DC):
                            pool.wait_ge(part_mid, n * 2 + t + 1)
                            pool.tensor_tensor(parts[i % 2][:, t, 2, :], rest[i % 2][:, t, :], parts[i % 2][:, t, 1, :],
                                               ALU.subtract).then_inc(part_lo, 1)

                batches(pool, step)

            stage(sync, gpsimd, scalar, vector, tensor)

        context_stage()

        ln_stat, ln_step, ln_ready = sem("ln_stat"), sem("ln_step"), sem("ln_ready")
        ln_normed, ln_scaled, ln_turned, ln_kept, ln_stored = (sem("ln_normed"), sem("ln_scaled"), sem("ln_turned"),
                                                               sem("ln_kept"), sem("ln_stored"))
        ln_evac = sem("ln_evac")
        ln_count = {"call": 0, "gain": 0, "turn": 0, "store": 0}
        ln_end = {}

        def by_four(eng, step):
            for u in range(4):
                step(u, u)
            with eng.Fori(1, B // 4) as i:
                for u in range(4):
                    step(i * 4 + u, u)

        def norm_stage(src, eps, gain=None, keep=None, turn=True, add_gate=None):
            m, mg = ln_count["call"], ln_count["gain"]
            t0, s0 = ln_count["turn"] * B, ln_count["store"] * B
            stores = keep is not None or add_gate is not None
            ln_count["call"] += 1
            ln_count["gain"] += gain is not None
            ln_count["turn"] += turn
            ln_count["store"] += stores
            rows = ln_gain
            scaled = [ln_scale[:, r, :] for r in range(XN)]
            n0 = m * B
            meet = not turn
            ln_end.update(normed=n0 + B, turned=t0 + B, stored=ln_count["store"] * B)
            g0 = mg * B
            gain_ready = expect(2) if gain is not None else 0

            def sync(sp):
                if gain is not None:
                    for r in range(2):
                        sp.dma_start(rows[:, r, :], a["ln_rows"][gain + r].partition_broadcast(128)).then_inc(loaded, 16)
                    sp.wait_ge(loaded, gain_ready)

            def vector(dve):
                with dve.Fori(0, B // 4) as i:
                    for u in range(4):
                        dve.bn_stats(ln_raw[:, i * 4 + u, :], src[:, i * 4 + u, :]).then_inc(ln_stat, 1)
                dve.wait_ge(ln_stat, n0 + B)
                k = 6 * m
                dve.tensor_tensor(ln_tmp[:, 0, :], ln_raw[:, :, 1], ln_raw[:, :, 4], ALU.add).then_inc(ln_step, 1)
                dve.tensor_tensor(ln_tmp[:, 1, :], ln_raw[:, :, 1], ln_raw[:, :, 4], ALU.subtract).then_inc(ln_step, 1)
                dve.tensor_tensor(ln_tmp[:, 2, :], ln_raw[:, :, 2], ln_raw[:, :, 5], ALU.add).then_inc(ln_step, 1)
                dve.wait_ge(ln_step, k + 3)
                dve.tensor_scalar(ln_mean[:, :], ln_tmp[:, 0, :], 0.5, None, ALU.mult).then_inc(ln_step, 1)
                dve.scalar_tensor_tensor(ln_tmp[:, 3, :], ln_tmp[:, 1, :], 0.25, ln_tmp[:, 1, :], ALU.mult, ALU.mult).then_inc(ln_step, 1)
                dve.wait_ge(ln_step, k + 5)
                dve.scalar_tensor_tensor(ln_tmp[:, 4, :], ln_tmp[:, 2, :], 1.0 / D, ln_tmp[:, 3, :], ALU.mult, ALU.add).then_inc(ln_step, 1)
                dve.wait_ge(ln_ready, 2 * (m + 1))
                if gain is not None:
                    dve.wait_ge(loaded, gain_ready)

                def step(b, u):
                    n = n0 + b
                    if turn:
                        at_least(dve, ln_turned, t0 + b - XN + 1)
                    if stores:
                        at_least(dve, ln_stored, s0 + b - XN + 1)
                    if gain is not None:
                        at_least(dve, ln_kept, g0 + b - XN + 1)
                    dve.tensor_scalar(xn2[u][:, :] if gain is None else scaled[u], src[:, b, :], ln_mean[:, bass.ds(b, 1)],
                                      ln_rstd[:, bass.ds(b, 1)], ALU.subtract, ALU.mult).then_inc(ln_normed, 1)
                    if gain is not None:
                        dve.wait_ge(ln_scaled, g0 + b + 1)
                        dve.tensor_tensor(xn2[u][:, :], scaled[u], rows[0:T, 1, :], ALU.add).then_inc(ln_kept, 1)
                        if add_gate is not None:
                            dve.wait_ge(ln_kept, g0 + b + 1)
                            dve.scalar_tensor_tensor(x[:, b, :], xn2[u][:, :], gates[0:T, add_gate:add_gate + 1], x[:, b, :],
                                                     ALU.mult, ALU.add).then_inc(ln_stored, 1)

                by_four(dve, step)

            def gpsimd(pool):
                pool.wait_ge(ln_step, 6 * (m + 1))
                pool.tensor_scalar(ln_tmp[:, 0, :], ln_tmp[:, 4, :], eps, None, ALU.add).then_inc(ln_ready, 1)
                pool.wait_ge(ln_ready, 2 * m + 1)
                pool.tensor_tensor(ln_rstd[:, :], ln_tmp[:, 0, :], half[:, :], ALU.pow).then_inc(ln_ready, 1)
                if gain is not None:
                    pool.wait_ge(loaded, gain_ready)

                def step(b, u):
                    n = n0 + b
                    if gain is not None:
                        pool.wait_ge(ln_normed, n + 1)
                        pool.tensor_tensor(scaled[u], scaled[u], rows[0:T, 0, :], ALU.mult).then_inc(ln_scaled, 1)
                    if keep is not None:
                        if gain is None:
                            pool.wait_ge(ln_normed, n + 1)
                        else:
                            pool.wait_ge(ln_kept, g0 + b + 1)
                        pool.tensor_copy(keep[:, b, :], xn2[u][:, :]).then_inc(ln_stored, 1)

                by_four(pool, step)

            def tensor(pe):
                def step(b, u):
                    n = n0 + b
                    if gain is None:
                        pe.wait_ge(ln_normed, n + 1)
                    else:
                        pe.wait_ge(ln_kept, g0 + b + 1)
                    at_least(pe, ln_evac, t0 + b - XN + 1)
                    for c in range(DC):
                        mm = pe.transpose(ps[:, u, c * T:(c + 1) * T], xn2[u][:, c * 128:(c + 1) * 128], ident[0:T, 0:T])
                    mm.then_inc(ln_turned, 1)

                by_four(pe, step)

            def scalar(act):
                def step(b, u):
                    act.wait_ge(ln_turned, t0 + b + 1)
                    act.activation(xn_t[:, :, bass.ds(b * T, T)], ps[:, u, 0:DC * T].rearrange("p (c t) -> p c t", c=DC),
                                   ACT.Copy).then_inc(ln_evac, 1)

                by_four(act, step)

            stage(sync, gpsimd, scalar if turn else None, vector, tensor if turn else None, meet=meet)


        q_stored = sem("q_stored")
        q_count = {"tile": B * len(KV_SET) * DC, "store": 0}

        def query_stage(s, kinds, dest, gate, keys_of=None):
            arena.clear()
            wlow.clear()
            w = wlow.take(128, 4, DC, D)
            TILES = DC * kinds
            parts = arena.take(128, G, TILES, PARTS, GT, dtype=BF16)
            rest = arena.take(128, G, TILES, GT)
            add_bias = bias(dest, gate, attn_rows[0:T, 1, :])
            weights_ready = expect(3)
            q0, st0 = q_count["tile"], q_count["store"]
            turned = ln_end["turned"] - B
            q_count["tile"] += G * TILES
            q_count["store"] += G * TILES

            def sync(sp):
                sp.dma_start(w, a["attn_w"][s]).then_inc(loaded, 16)
                for r in range(2):
                    sp.dma_start(attn_rows[:, r, :], a["attn_rows"][s, r].partition_broadcast(128)).then_inc(loaded, 16)
                if keys_of is not None:
                    fetch_keys(sp, keys_of)
                with sp.Fori(0, G) as g:
                    for j in range(TILES):
                        sp.wait_ge(part_lo, q0 + g * TILES + j + 1)
                        sp.dma_start(query_parts[j // DC, :, (j % DC) * 128:(j % DC + 1) * 128, bass.ds(g * GT, GT)].rearrange("q p n -> p q n"),
                                     parts[:, bass.ds(g, 1), j, :, :].rearrange("p g q n -> p (g q) n")).then_inc(q_stored, 16)
                sp.wait_ge(q_stored, 16 * (st0 + G * TILES))

            def groups(eng, step):
                step(0)
                with eng.Fori(1, G) as g:
                    step(g)

            def tensor(pe):
                pe.wait_ge(loaded, weights_ready)

                def step(g):
                    pe.wait_ge(ln_evac, turned + (g + 1) * GB)
                    for j in range(TILES):
                        at_least(pe, part_res, q0 + g * TILES + j - 1)
                        for c in range(DC):
                            mm = pe.matmul(ps[:, XN + j % 2, 0:GT], w[:, j // DC, c, (j % DC) * 128:(j % DC + 1) * 128],
                                           xn_t[:, c, bass.ds(g * GT, GT)], start=(c == 0), stop=(c == DC - 1))
                        mm.then_inc(part_made, 1)

                groups(pe, step)

            def part(g, j, q):
                return parts[:, bass.ds(g, 1), j, q, :].rearrange("p g n -> p (g n)")

            def the_rest(g, j):
                return rest[:, bass.ds(g, 1), j, :].rearrange("p g n -> p (g n)")

            def scalar(act):
                def step(g):
                    for j in range(TILES):
                        act.wait_ge(part_made, q0 + g * TILES + j + 1)
                        act.activation(part(g, j, 0), ps[:, XN + j % 2, 0:GT], ACT.Identity, bias=attn_cols[:, s, j:j + 1]).then_inc(part_hi, 1)
                        if j > 0:
                            middle(act, g, j - 1)
                    middle(act, g, TILES - 1)

                def middle(act, g, j):
                    act.wait_ge(part_res, q0 + g * TILES + j + 1)
                    act.activation(part(g, j, 1), the_rest(g, j), ACT.Copy).then_inc(part_mid, 1)

                groups(act, step)

            def vector(dve):
                dve.wait_ge(loaded, weights_ready)

                def step(g):
                    for j in range(TILES):
                        dve.wait_ge(part_hi, q0 + g * TILES + j + 1)
                        dve.scalar_tensor_tensor(the_rest(g, j), ps[:, XN + j % 2, 0:GT], attn_cols[:, s, j:j + 1], part(g, j, 0),
                                                 ALU.add, ALU.subtract).then_inc(part_res, 1)

                groups(dve, step)
                add_bias(dve)

            def gpsimd(pool):
                def step(g):
                    for j in range(TILES):
                        pool.wait_ge(part_mid, q0 + g * TILES + j + 1)
                        pool.tensor_tensor(part(g, j, 2), the_rest(g, j), part(g, j, 1), ALU.subtract).then_inc(part_lo, 1)

                groups(pool, step)

            stage(sync, gpsimd, scalar, vector, tensor)
            return w

        bias_scaled, bias_added = sem("bias_scaled"), sem("bias_added")
        bias_count = [0]

        def bias(dest, gate, row):
            k = bias_count[0]
            bias_count[0] += 1
            scaled = arena.take(T, D)
            normed, stored = ln_end["normed"], ln_end["stored"]

            def add(dve):
                dve.tensor_scalar(scaled, row, gate, None, ALU.mult).then_inc(bias_scaled, 1)
                dve.wait_ge(bias_scaled, k + 1)
                dve.wait_ge(ln_normed, normed)
                at_least(dve, ln_stored, stored)
                for q in range(2):
                    dve.tensor_tensor(dest[:, q * 8:q * 8 + 8, :], dest[:, q * 8:q * 8 + 8, :],
                                      scaled.unsqueeze(1).broadcast_to([T, 8, D]), ALU.add).then_inc(bias_added, 1)

            return add

        def bias_done():
            return 2 * bias_count[0]

        o_copied = sem("o_copied")
        o_turned = sem("o_turned")
        o_recip, o_normed = sem("o_recip"), sem("o_normed")
        o_turned2, o_copied2 = sem("o_turned2"), sem("o_copied2")
        o_made, o_added = sem("o_made"), sem("o_added")
        MISC, SUMS = 7, 6

        class Output:

            def __init__(self, w, dest, gate):
                self.w, self.dest, self.gate = w, dest, gate
                self.sums = [arena.take(128, 4, T) for _ in range(2)]
                self.normed = [arena.take(T, D) for _ in range(2)]
                self.turned = [arena.take(128, DC, T) for _ in range(2)]
                self.recip = arena.take(T, H)
            def turn_back(self, pe, n, r):
                at_least(pe, o_added, n)
                pe.wait_ge(o_copied, n + 1)
                for j in range(4):
                    mm = pe.transpose(ps[0:T, MISC, j * 128:(j + 1) * 128], self.sums[r][:, j, :], ident[:, :])
                mm.then_inc(o_turned, 1)

            def turn(self, pe, n, r):
                pe.wait_ge(o_normed, n + 1)
                for c in range(DC):
                    mm = pe.transpose(ps[:, MISC, c * T:(c + 1) * T], self.normed[r][:, c * 128:(c + 1) * 128], ident[0:T, 0:T])
                mm.then_inc(o_turned2, 1)

            def project(self, pe, n, r):
                pe.wait_ge(o_copied2, n + 1)
                for c in range(DC):
                    mm = pe.matmul(ps[0:T, MISC, 0:D], self.turned[r][:, c, :], self.w[:, 3, c, :], start=(c == 0), stop=(c == DC - 1))
                mm.then_inc(o_made, 1)

            def copy_turned(self, act, n, r):
                act.wait_ge(o_turned2, n + 1)
                act.activation(self.turned[r], ps[:, MISC, 0:DC * T].rearrange("p (c t) -> p c t", c=DC), ACT.Copy).then_inc(o_copied2, 1)

            def copy_sums(self, act, n, r):
                act.activation(self.sums[r], ps[:, SUMS, 0:4 * T].rearrange("p (j t) -> p j t", j=4), ACT.Copy).then_inc(o_copied, 1)

            def normalise(self, dve, n, r):
                back = ps[0:T, MISC, :].rearrange("p (h w) -> p h w", w=32)
                dve.wait_ge(o_turned, n + 1)
                dve.reciprocal(self.recip, back[:, :, DH]).then_inc(o_recip, 1)
                dve.wait_ge(o_recip, n + 1)
                dve.tensor_tensor(self.normed[r].rearrange("p (h e) -> p h e", h=H), back[:, :, 0:DH],
                                  self.recip.unsqueeze(2).broadcast_to([T, H, DH]), ALU.mult).then_inc(o_normed, 1)

            def add(self, dve, n, b):
                dve.wait_ge(o_made, n + 1)
                dve.scalar_tensor_tensor(self.dest[:, b, :], ps[0:T, MISC, 0:D], self.gate, self.dest[:, b, :],
                                         ALU.mult, ALU.add).then_inc(o_added, 1)

        RING = 4
        at_loaded = [sem(f"at_loaded{r}") for r in range(RING)]
        at_maxrow = [sem(f"at_maxrow{r}") for r in range(RING)]
        at_pair, at_max = sem("at_pair"), sem("at_max")
        at_clamped, at_mturn, at_mhi, at_mmid = sem("at_clamped"), sem("at_mturn"), sem("at_mhi"), sem("at_mmid")
        at_scores, at_probs, at_pv = sem("at_scores"), sem("at_probs"), sem("at_pv")
        at_mask, at_pen0, at_pen = [sem(f"at_mask{r}") for r in range(RING)], sem("at_pen0"), sem("at_pen")
        at_count = {"call": 0, "mask": 0}
        out_count = [0]
        STEPS, PAIRS = 12, H // 2
        PAIR_AT = {0: 0, 2: 1, 3: 2, 5: 3, 6: 4, 8: 5, 9: 6, 11: 7}

        def load_keys(sp, keys, kv, b, r, j):
            sp.dma_start(keys[DH * j:DH * j + DH, :, :],
                         key_parts[kv, b, K_PART[j], :, :].rearrange("(h d) k -> d h k", d=DH)).then_inc(at_loaded[r], 16)

        def low_rings():
            wreg.clear()
            keys = [wreg.take(AROWS, H, S2, dtype=BF16) for _ in range(RING - 1)]
            return keys, [wreg.take(AROWS, H, T, dtype=BF16) for _ in range(RING - 1)]

        def fetch_keys(sp, kv):
            keys, _ = low_rings()
            for b in range(RING - 1):
                for j in range(len(K_PART)):
                    load_keys(sp, keys[b], kv, b, b, j)

        def cross_stage(kv, w, scale, dest, gate, masked=False):
            arena.clear()
            call = at_count["call"]
            n0, o0, p0 = call * B, out_count[0] * B, at_count["mask"] * B
            turn0 = call * (B // RING)
            ones_made = expect_made(RING)
            at_count["call"] += 1
            at_count["mask"] += masked
            out_count[0] += 1
            keys, queries = low_rings()
            keys.append(arena.take(AROWS, H, S2, dtype=BF16))
            queries.append(arena.take(AROWS, H, T, dtype=BF16))
            vals = [arena.take(KN, KC, H, VW) for _ in range(RING)]
            probs = [arena.take(KN, GT) for _ in range(3)]
            out = Output(w, dest, gate)
            negmax = [arena.take(T, H) for _ in range(2)]
            negmax_c = [arena.take(T, H) for _ in range(2)]
            maxrow = [arena.take(H, 2, T, dtype=BF16) for _ in range(2)]
            if masked:
                mask_in = [arena.take(T, S2, dtype=I32) for _ in range(RING)]
                pad_in = [arena.take(T, S2, dtype=I32) for _ in range(RING)]
                pen = [arena.take(T, S2, dtype=BF16) for _ in range(RING)]

            def schedule(eng, step):
                def static(b):
                    step(b, lambda d: (b + d) % RING, lambda d: turn0 + (b + d) // RING)

                static(0)
                with eng.Fori(0, 3) as i:
                    for q in range(1, RING + 1):
                        step(i * RING + q, lambda d, q=q: (q + d) % RING, lambda d, q=q: i + (turn0 + (q + d) // RING))
                for b in range(13, B):
                    static(b)

            def has(b, d):
                return not isinstance(b, int) or 0 <= b + d < B

            LOADS = 2 * len(K_PART) + 1

            def sync(sp):
                def load(b, r, which, fetched=False):
                    if masked and 0 in which:
                        sp.dma_start(mask_in[r], a["mask"][b]).then_inc(at_mask[r], 16)
                        sp.dma_start(pad_in[r], a["pad"][b].partition_broadcast(T)).then_inc(at_mask[r], 16)
                    for j in which:
                        if not fetched:
                            load_keys(sp, keys[r], kv, b, r, j)
                        sp.dma_start(queries[r][DH * j:DH * j + DH, :, :],
                                     query_parts[0, Q_PART[j], :, bass.ds(b * T, T)].rearrange("(h d) k -> d h k", d=DH)).then_inc(at_loaded[r], 16)

                def load_values(b, r):
                    sp.dma_start(vals[r].rearrange("p c h w -> p (c h w)"), values[kv, b]).then_inc(at_loaded[r], 16)

                def rows(b, r):
                    sp.wait_ge(at_mmid, n0 + b + 1)
                    for q in range(2):
                        sp.dma_start(queries[r][SROWS + q:SROWS + q + 1, :, :], maxrow[r % 2][:, q, :]).then_inc(at_maxrow[r], 16)

                for b in range(RING - 1):
                    load(b, b, range(len(K_PART)), fetched=True)
                    load_values(b, b)
                rows(0, 0)

                def step(b, place, turn):
                    if has(b, 3):
                        at_least(sp, at_scores, (n0 + b) * STEPS if has(b, -1) else 0)
                        load(b + 3, place(3), range(0, 3))
                    if has(b, 1):
                        rows(b + 1, place(1))
                    if has(b, 3):
                        load(b + 3, place(3), range(3, len(K_PART)))
                        at_least(sp, at_pv, (n0 + b) * STEPS if has(b, -1) else 0)
                        load_values(b + 3, place(3))

                schedule(sp, step)

            def gpsimd(pool):
                for r in range(2):
                    pool.memset(keys[r][SROWS:AROWS, :, :], 1.0).then_inc(const_made, 1)

            def tensor(pe):
                def pair(b, r, p):
                    k = (n0 + b) * PAIRS + p
                    at_least(pe, at_max, k - 1)
                    for e in range(2):
                        hd = 2 * p + e
                        mm = pe.matmul(ps[0:T, 2 * (p % 2) + e, 0:S2], queries[r][0:SROWS, hd, :], keys[r][0:SROWS, hd, :],
                                       start=True, stop=not masked)
                        if masked:
                            mm = pe.matmul(ps[0:T, 2 * (p % 2) + e, 0:S2], neg16[:, 0, :], pen[r], start=False, stop=True)
                    mm.then_inc(at_pair, 1)

                def maxima(b, r):
                    pe.wait_ge(at_clamped, n0 + b + 1)
                    pe.transpose(ps[0:H, MISC, 0:T], negmax_c[r % 2], ident[0:T, 0:T]).then_inc(at_mturn, 1)

                def scores(b, r, k):
                    m = (n0 + b) * STEPS + k
                    at_least(pe, at_probs, m - 1)
                    bank, c = 4 + k % 2, k % KC
                    if masked:
                        pe.matmul(ps[0:KN, bank, 0:GT], pen[r][:, c * KN:(c + 1) * KN], neg16[:, :, :], start=True, stop=False)
                    for g in range(4):
                        hd = 4 * (k // KC) + g
                        mm = pe.matmul(ps[0:KN, bank, g * T:(g + 1) * T], keys[r][:, hd, c * KN:(c + 1) * KN], queries[r][:, hd, :],
                                       start=not masked, stop=not masked or g == 3)
                    mm.then_inc(at_scores, 1)

                def weigh(b, r, k):
                    m = (n0 + b) * STEPS + k
                    pe.wait_ge(at_probs, m + 1)
                    j, c = k // KC, k % KC
                    for g in range(4):
                        mm = pe.matmul(ps[32 * g:32 * g + VW, SUMS, j * T:(j + 1) * T], vals[r][:, c, 4 * j + g, :],
                                       probs[k % 3][:, g * T:(g + 1) * T], start=(c == 0), stop=(c == KC - 1))
                    mm.then_inc(at_pv, 1)

                def arrived(b, r, turn):
                    pe.wait_ge(at_loaded[r], (turn + 1) * (16 * LOADS))
                    if masked:
                        pe.wait_ge(at_pen, p0 + b + 1)

                for b in range(2):
                    arrived(b, b, turn0)
                    for p in range(PAIRS):
                        pair(b, b, p)
                    if b == 0:
                        maxima(0, 0)

                def step(b, place, turn):
                    here, prev = place(0), place(-1)
                    last = o0 + b - 1
                    pe.wait_ge(at_maxrow[here], (turn(0) + 1) * 32)
                    for k in range(STEPS):
                        scores(b, here, k)
                        if k >= 2:
                            if k == 2:
                                at_least(pe, o_copied, o0 + b)
                            weigh(b, here, k - 2)
                        elif has(b, -1):
                            weigh(b - 1, prev, STEPS - 2 + k)
                        if k in PAIR_AT and has(b, 2):
                            if k == 0:
                                arrived(b + 2, place(2), turn(2))
                            pair(b + 2, place(2), PAIR_AT[k])
                        if k == 1 and has(b, 1):
                            at_least(pe, o_added, last if has(b, -1) else o0)
                            maxima(b + 1, place(1))
                        if has(b, -1):
                            if k == 4:
                                at_least(pe, at_mmid, n0 + b + 2 if has(b, 1) else n0 + b + 1)
                                out.turn_back(pe, last, prev % 2)
                            if k == 6:
                                out.turn(pe, last, prev % 2)
                            if k == 8:
                                out.project(pe, last, prev % 2)

                pe.wait_ge(const_made, ones_made)
                schedule(pe, step)
                for k in range(STEPS - 2, STEPS):
                    weigh(B - 1, (B - 1) % RING, k)
                last = o0 + B - 1
                out.turn_back(pe, last, (B - 1) % 2)
                out.turn(pe, last, (B - 1) % 2)
                out.project(pe, last, (B - 1) % 2)

            def scalar(act):
                act.activation(idle[:, :], one[:, :], ACT.Exp)

                for r in range(2, RING):
                    act.activation(keys[r][SROWS:AROWS, :, :], one[SROWS:AROWS, :].unsqueeze(2).broadcast_to([2, H, S2]), ACT.Copy).then_inc(const_made, 1)

                def sums(b, r):
                    act.wait_ge(at_pv, (n0 + b + 1) * STEPS)
                    out.copy_sums(act, o0 + b, r % 2)

                def step(b, place, turn):
                    for k in range(STEPS):
                        m = (n0 + b) * STEPS + k
                        at_least(act, at_pv, m - 2)
                        act.wait_ge(at_scores, m + 1)
                        act.activation(probs[k % 3], ps[0:KN, 4 + k % 2, 0:GT], ACT.Exp, scale=scale).then_inc(at_probs, 1)
                        if k == 1 and has(b, -1):
                            sums(b - 1, place(-1))
                        if k == 7 and has(b, -1):
                            out.copy_turned(act, o0 + b - 1, place(-1) % 2)

                schedule(act, step)
                sums(B - 1, (B - 1) % RING)
                out.copy_turned(act, o0 + B - 1, (B - 1) % 2)

            def vector(dve):
                dve.memset(ps[:, SUMS, :], 0.0)

                def reduce_pair(b, r, p):
                    k = (n0 + b) * PAIRS + p
                    dve.wait_ge(at_pair, k + 1)
                    dve.tensor_reduce(negmax[r % 2][:, 2 * p:2 * p + 2], ps[0:T, 2 * (p % 2):2 * (p % 2) + 2, 0:S2], AX.X, ALU.max,
                                      negate=True).then_inc(at_max, 1)

                def clamp(b, r):
                    dve.wait_ge(at_max, (n0 + b + 1) * PAIRS)
                    dve.tensor_scalar(negmax_c[r % 2], negmax[r % 2], 0.1 * -NEG, None, ALU.min).then_inc(at_clamped, 1)

                def split_rows(b, r):
                    n = n0 + b
                    dve.wait_ge(at_mturn, n + 1)
                    at_least(dve, at_scores, (n - 1) * STEPS)
                    dve.tensor_copy(maxrow[r % 2][:, 0, :], ps[0:H, MISC, 0:T]).then_inc(at_mhi, 1)
                    dve.wait_ge(at_mhi, n + 1)
                    dve.tensor_tensor(maxrow[r % 2][:, 1, :], ps[0:H, MISC, 0:T], maxrow[r % 2][:, 0, :], ALU.subtract).then_inc(at_mmid, 1)

                def penalty(b, r, turn):
                    dve.wait_ge(at_mask[r], (turn - turn0 + 1) * 32)
                    at_least(dve, at_pv, (n0 + b - 3) * STEPS)
                    dve.tensor_scalar(mask_in[r].bitcast(F32), mask_in[r], 0, None, ALU.is_equal).then_inc(at_pen0, 1)
                    dve.wait_ge(at_pen0, p0 + b + 1)
                    dve.scalar_tensor_tensor(pen[r], pad_in[r], 0, mask_in[r].bitcast(F32), ALU.is_equal, ALU.add).then_inc(at_pen, 1)

                if masked:
                    for b in range(RING - 1):
                        penalty(b, b, turn0)
                for p in range(PAIRS):
                    reduce_pair(0, 0, p)
                clamp(0, 0)
                split_rows(0, 0)
                for p in range(PAIRS):
                    reduce_pair(1, 1, p)

                def step(b, place, turn):
                    last, prev = o0 + b - 1, place(-1)
                    if has(b, 1):
                        clamp(b + 1, place(1))
                    for p in range(PAIRS):
                        if has(b, 2):
                            reduce_pair(b + 2, place(2), p)
                        if p == 0 and has(b, 1):
                            split_rows(b + 1, place(1))
                        if p == 2 and has(b, -1):
                            out.normalise(dve, last, prev % 2)
                        if p == 5 and has(b, -1):
                            out.add(dve, last, b - 1)
                    if masked and has(b, 3):
                        penalty(b + 3, place(3), turn(3))

                schedule(dve, step)
                out.normalise(dve, o0 + B - 1, (B - 1) % 2)
                out.add(dve, o0 + B - 1, B - 1)

            stage(sync, gpsimd, scalar, vector, tensor)

        se_inv = sem("se_inv")
        se_loaded = [sem("se_loaded0"), sem("se_loaded1")]
        se_group, se_v, se_vout = sem("se_group"), sem("se_v"), sem("se_vout")
        se_scores, se_masked, se_max, se_shifted = sem("se_scores"), sem("se_masked"), sem("se_max"), sem("se_shifted")
        se_probs, se_pturn, se_pcopied, se_pv = sem("se_probs"), sem("se_pturn"), sem("se_pcopied"), sem("se_pv")

        def self_stage(s, w, scale, dest, gate):
            arena.clear()
            wreg.clear()
            masks_ready = expect(2)
            ones_made = expect_made(3)
            o0 = out_count[0] * B
            out_count[0] += 1
            keys = [wreg.take(SROWS, H, T, dtype=BF16) for _ in range(2)]
            queries = [wreg.take(SROWS, H, T, dtype=BF16) for _ in range(2)]
            group_t = wreg.take(128, DC, GT)
            am = wreg.take(T, T)
            pm = arena.take(T, B, T)
            out = Output(w, dest, gate)
            vals = [arena.take(T, H, VW) for _ in range(2)]
            masked = [arena.take(T, 4, T) for _ in range(2)]
            probs = [arena.take(T, 4, T) for _ in range(2)]
            probs_t = [arena.take(T, 4, T) for _ in range(2)]
            negmax = arena.take(T, H)
            LOADS = 2 * len(K_PART)
            Q4 = 4

            def sync(sp):
                sp.dma_start(am, a["am"][0, 0]).then_inc(loaded, 16)
                sp.dma_start(pm, a["pm"].rearrange("b o u k -> (o u) b k").squeeze(0).partition_broadcast(T)).then_inc(loaded, 16)

                def load(b, u):
                    for j in range(len(K_PART)):
                        for kind, dst, part in ((1, keys, K_PART[j]), (0, queries, Q_PART[j])):
                            sp.dma_start(dst[u][DH * j:DH * j + DH, :, :],
                                         query_parts[kind, part, :, bass.ds(b * T, T)].rearrange("(h d) k -> d h k", d=DH)).then_inc(se_loaded[u], 16)

                load(0, 0)
                load(1, 1)
                with sp.Fori(1, B // 2) as i:
                    for u in range(2):
                        sp.wait_ge(se_scores, (i * 2 + u - 1) * 4)
                        load(i * 2 + u, u)
                sp.wait_ge(loaded, masks_ready)

            def gpsimd(pool):
                pool.wait_ge(loaded, masks_ready)
                pool.tensor_tensor(pm, pm, am.unsqueeze(1).broadcast_to([T, B, T]), ALU.mult).then_inc(se_inv, 1)
                pool.wait_ge(se_inv, 1)
                pool.tensor_scalar(pm, pm, -1.0, 1.0, ALU.mult, ALU.add).then_inc(se_inv, 1)
                pool.wait_ge(se_inv, 2)
                pool.tensor_scalar(pm, pm, -1.0e9, None, ALU.mult).then_inc(se_inv, 1)

            def tensor(pe):
                def scores(b, u, k):
                    m = b * 4 + k
                    at_least(pe, se_masked, m - 1)
                    for g in range(Q4):
                        hd = 4 * k + g
                        mm = pe.matmul(ps[0:T, k % 2, g * T:(g + 1) * T], queries[u][:, hd, :], keys[u][:, hd, :], start=True, stop=True)
                    mm.then_inc(se_scores, 1)

                def turn(b, k):
                    m = b * 4 + k
                    pe.wait_ge(se_probs, m + 1)
                    at_least(pe, se_pcopied, m - 1)
                    for g in range(Q4):
                        mm = pe.transpose(ps[0:T, 2 + k % 2, g * T:(g + 1) * T], probs[k % 2][:, g, :], ident[0:T, 0:T])
                    mm.then_inc(se_pturn, 1)

                def weigh(b, u, k):
                    m = b * 4 + k
                    pe.wait_ge(se_pcopied, m + 1)
                    if k == 0:
                        pe.wait_ge(se_vout, b + 1)
                        at_least(pe, o_copied, o0 + b)
                    for g in range(Q4):
                        mm = pe.matmul(ps[32 * g:32 * g + VW, SUMS, k * T:(k + 1) * T], vals[u][:, 4 * k + g, :],
                                       probs_t[k % 2][:, g, :], start=True, stop=True)
                    mm.then_inc(se_pv, 1)

                pe.wait_ge(const_made, ones_made)

                def step(g):
                    for q in range(GB):
                        u = q % 2
                        b = g * GB + q
                        if q == 0:
                            pe.wait_ge(se_group, g + 1)
                        pe.wait_ge(se_loaded[u], (g * 2 + q // 2 + 1) * (16 * LOADS))
                        scores(b, u, 0)
                        scores(b, u, 1)
                        for c in range(DC):
                            mm = pe.matmul(ps[0:T, 4, 0:D], group_t[:, c, q * T:(q + 1) * T], w[:, 2, c, :], start=(c == 0), stop=(c == DC - 1))
                        mm.then_inc(se_v, 1)
                        turn(b, 0)
                        scores(b, u, 2)
                        turn(b, 1)
                        scores(b, u, 3)
                        weigh(b, u, 0)
                        turn(b, 2)
                        weigh(b, u, 1)
                        turn(b, 3)
                        weigh(b, u, 2)
                        weigh(b, u, 3)
                        n = o0 + b
                        out.turn_back(pe, n, u)
                        out.turn(pe, n, u)
                        out.project(pe, n, u)

                first(pe, step)

            def scalar(act):
                act.activation(idle[:, :], one[:, :], ACT.Exp)

                def step(g):
                    for q in range(GB):
                        u, b = q % 2, g * GB + q
                        for k in range(4):
                            m = b * 4 + k
                            act.wait_ge(se_shifted, m + 1)
                            at_least(act, se_pturn, m - 1)
                            act.activation(probs[k % 2], masked[k % 2], ACT.Exp).then_inc(se_probs, 1)
                            if k > 0:
                                copy(act, b, k - 1)
                        copy(act, b, 3)
                        act.wait_ge(se_pv, b * 4 + 4)
                        out.copy_sums(act, o0 + b, u)
                        out.copy_turned(act, o0 + b, u)

                def copy(act, b, k):
                    m = b * 4 + k
                    act.wait_ge(se_pturn, m + 1)
                    at_least(act, se_pv, m - 1)
                    act.activation(probs_t[k % 2], ps[0:T, 2 + k % 2, 0:GT].rearrange("p (g t) -> p g t", g=4), ACT.Copy).then_inc(se_pcopied, 1)

                first(act, step)

            def first(eng, step):
                step(0)
                with eng.Fori(1, G) as g:
                    step(g)

            def vector(dve):
                dve.memset(ps[:, SUMS, :], 0.0).then_inc(const_made, 1)
                for u in range(2):
                    dve.memset(vals[u], 1.0).then_inc(const_made, 1)
                dve.wait_ge(se_inv, 3)

                def step(g):
                    at_least(dve, se_v, g * GB)
                    dve.tensor_copy(group_t, xn_t[:, :, bass.ds(g * GT, GT)]).then_inc(se_group, 1)
                    for q in range(GB):
                        u, b = q % 2, g * GB + q
                        n = o0 + b
                        dve.wait_ge(se_v, b + 1)
                        at_least(dve, se_pv, (b - 1) * 4)
                        dve.tensor_tensor(vals[u][:, :, 0:DH], ps[0:T, 4, 0:D].rearrange("p (h e) -> p h e", h=H),
                                          attn_rows[0:T, 0, :].rearrange("p (h e) -> p h e", h=H), ALU.add).then_inc(se_vout, 1)
                        for k in range(4):
                            m = b * 4 + k
                            dve.wait_ge(se_scores, m + 1)
                            at_least(dve, se_probs, m - 1)
                            dve.scalar_tensor_tensor(masked[k % 2], ps[0:T, k % 2, 0:GT].rearrange("p (g t) -> p g t", g=4), scale,
                                                     pm[:, bass.ds(b, 1), :].broadcast_to([T, 4, T]), ALU.mult, ALU.add).then_inc(se_masked, 1)
                            dve.wait_ge(se_masked, m + 1)
                            dve.tensor_reduce(negmax[:, 4 * k:4 * k + 4], masked[k % 2], AX.X, ALU.max).then_inc(se_max, 1)
                            dve.wait_ge(se_max, m + 1)
                            dve.tensor_tensor(masked[k % 2], masked[k % 2], negmax[:, 4 * k:4 * k + 4].unsqueeze(2).broadcast_to([T, 4, T]),
                                              ALU.subtract).then_inc(se_shifted, 1)
                        out.normalise(dve, n, u)
                        out.add(dve, n, b)

                first(dve, step)

            stage(sync, gpsimd, scalar, vector, tensor)

        def groups(eng, step):
            step(0)
            with eng.Fori(1, G) as g:
                step(g)

        expert_w = [sem("expert_w0"), sem("expert_w1")]
        e0_h, e0_gate, e0_act, e0_out, e0_kept = sem("e0_h"), sem("e0_gate"), sem("e0_act"), sem("e0_out"), sem("e0_kept")
        e0_turned, e0_added = sem("e0_turned"), sem("e0_added")

        def position_experts_stage(gate):
            arena.clear()
            wreg.clear()
            TE = T // E
            turned = ln_end["turned"]
            NT = B * TE
            NF = len(F0_ROWS)
            w1 = [wreg.take(128, DC, F0) for _ in range(2)]
            w3 = [wreg.take(128, DC, F0) for _ in range(2)]
            w2 = [wreg.take(128, NF, D) for _ in range(2)]
            hid = [arena.take(128, NF, NT) for _ in range(2)]
            silu = [arena.take(128, NT) for _ in range(2)]
            out_t = arena.take(128, DC, B * T)
            stage_in = [arena.take(128, DC, NT) for _ in range(2)]
            rows = F0_ROWS

            def experts(eng, step):
                step(0, 0, 0)
                step(1, 1, 0)
                with eng.Fori(1, E // 2) as i:
                    step(i * 2, 0, i)
                    step(i * 2 + 1, 1, i)

            def sync(sp):
                def step(e, u, i):
                    at_least(sp, e0_out, (e - 1) * DC)
                    sp.dma_start(w1[u], a["e0_w1"][e]).then_inc(expert_w[u], 16)
                    sp.dma_start(w3[u], a["e0_w3"][e]).then_inc(expert_w[u], 16)
                    sp.dma_start(w2[u][:, 0:4, :], a["e0_w2"][e]).then_inc(expert_w[u], 16)
                    sp.dma_start(w2[u][0:96, 4:6, :], a["e0_w2r"][e]).then_inc(expert_w[u], 16)

                experts(sp, step)
                for u in range(2):
                    sp.wait_ge(expert_w[u], 64 * E // 2)

            def tensor(pe):
                pe.wait_ge(ln_evac, turned)

                def step(e, u, i):
                    pe.wait_ge(expert_w[u], (i + 1) * 64)
                    for f in range(NF):
                        k = e * NF + f
                        at_least(pe, e0_act, k - 1)
                        for q, w in ((0, w1[u]), (1, w3[u])):
                            for c in range(DC):
                                mm = pe.matmul(ps[0:rows[f], f % 2, q * NT:(q + 1) * NT], w[:, c, F0_AT[f]:F0_AT[f] + rows[f]],
                                               xn_t[:, c, :].rearrange("p (b t) -> p b t", t=T)[:, :, bass.ds(e * TE, TE)],
                                               start=(c == 0), stop=(c == DC - 1))
                        mm.then_inc(e0_h, 1)
                    for c in range(DC):
                        at_least(pe, e0_kept, e * DC + c - 1)
                        for f in range(NF):
                            if c == 0:
                                pe.wait_ge(e0_act, e * NF + f + 1)
                            mm = pe.matmul(ps[:, 2 + c, 0:NT], w2[u][0:rows[f], f, c * 128:(c + 1) * 128], hid[u][0:rows[f], f, :],
                                           start=(f == 0), stop=(f == NF - 1))
                        mm.then_inc(e0_out, 1)

                experts(pe, step)
                for b in range(B):
                    at_least(pe, e0_added, b - 1)
                    if b == 0:
                        pe.wait_ge(e0_kept, E * DC)
                    for c in range(DC):
                        mm = pe.transpose(ps[0:T, 4 + b % 2, c * 128:(c + 1) * 128], out_t[:, c, b * T:(b + 1) * T], ident[:, :])
                    mm.then_inc(e0_turned, 1)

            def scalar(act):
                act.activation(idle[:, :], one[:, :], ACT.Silu)

                def step(e, u, i):
                    for f in range(NF):
                        k = e * NF + f
                        act.wait_ge(e0_h, k + 1)
                        at_least(act, e0_act, k - 1)
                        act.activation(silu[f % 2][0:rows[f], :], ps[0:rows[f], f % 2, 0:NT], ACT.Silu).then_inc(e0_gate, 1)
                    for c in range(DC):
                        act.wait_ge(e0_out, e * DC + c + 1)
                        act.activation(out_t[:, c, :].rearrange("p (b t) -> p b t", t=T)[:, :, bass.ds(e * TE, TE)],
                                       ps[:, 2 + c, 0:NT].rearrange("p (b t) -> p b t", t=TE), ACT.Copy).then_inc(e0_kept, 1)

                experts(act, step)

            def vector(dve):
                def step(e, u, i):
                    for f in range(NF):
                        k = e * NF + f
                        dve.wait_ge(e0_gate, k + 1)
                        if f == 0:
                            at_least(dve, e0_out, (e - 1) * DC)
                        dve.tensor_tensor(hid[u][0:rows[f], f, :], silu[f % 2][0:rows[f], :], ps[0:rows[f], f % 2, NT:2 * NT],
                                          ALU.mult).then_inc(e0_act, 1)

                experts(dve, step)
                for b in range(B):
                    dve.wait_ge(e0_turned, b + 1)
                    dve.scalar_tensor_tensor(x[:, b, :], ps[0:T, 4 + b % 2, 0:D], gates[0:T, gate:gate + 1], x[:, b, :],
                                             ALU.mult, ALU.add).then_inc(e0_added, 1)

            stage(sync, None, scalar, vector, tensor)

        rt_logits, rt_step, rt_exp = sem("rt_logits"), sem("rt_step"), sem("rt_exp")
        rt_count = {"call": 0, "step": 0}

        class TopTwo:

            def __init__(self, router, bias=None):
                self.n = rt_count["call"]
                self.ranks_made = expect_made(E)
                rt_count["call"] += 1
                self.router, self.bias = router, bias
                self.turned = ln_end["turned"]
                self.logits, self.rank, self.equal = (arena.take(T, B, E) for _ in range(3))
                self.best, self.found, self.second, self.gap, self.grown = (arena.take(T, B) for _ in range(5))
                self.onehot = [arena.take(T, B, E) for _ in range(2)]
                self.weight = [arena.take(T, B) for _ in range(2)]
                self.steps = rt_count["step"]

            def make_ranks(self, pool):
                for e in range(E):
                    pool.memset(self.rank[:, :, e], float(E - e)).then_inc(const_made, 1)

            def logits_pe(self, pe):
                pe.wait_ge(ln_evac, self.turned)
                for b in range(B):
                    for c in range(DC):
                        mm = pe.matmul(ps[0:T, 0, b * E:(b + 1) * E], xn_t[:, c, b * T:(b + 1) * T], self.router[:, c, :],
                                       start=(c == 0), stop=(c == DC - 1))
                mm.then_inc(rt_logits, 1)

            def exp_act(self, act):
                act.wait_ge(rt_step, self.gap_step)
                act.activation(self.grown, self.gap, ACT.Exp).then_inc(rt_exp, 1)

            def plan(self):
                self.gap_step = self.steps + 14
                rt_count["step"] = self.steps + 17

            def choose(self, dve):
                def link(ins):
                    self.steps += 1
                    ins.then_inc(rt_step, 1)
                    dve.wait_ge(rt_step, self.steps)

                def over(v):
                    return v.unsqueeze(2).broadcast_to([T, B, E])

                dve.wait_ge(const_made, self.ranks_made)
                dve.wait_ge(rt_logits, self.n + 1)
                logits = ps[0:T, 0, 0:B * E].rearrange("p (b e) -> p b e", e=E)
                if self.bias is None:
                    link(dve.tensor_copy(self.logits, logits))
                else:
                    link(dve.tensor_tensor(self.logits, logits, self.bias.unsqueeze(1).broadcast_to([T, B, E]), ALU.add))
                for k, top in ((0, self.best), (1, self.second)):
                    link(dve.tensor_reduce(top, self.logits, AX.X, ALU.max))
                    link(dve.tensor_tensor(self.equal, self.logits, over(top), ALU.is_equal))
                    link(dve.tensor_tensor(self.equal, self.equal, self.rank, ALU.mult))
                    link(dve.tensor_reduce(self.found, self.equal, AX.X, ALU.max))
                    link(dve.tensor_tensor(self.onehot[k], self.equal, over(self.found), ALU.is_equal))
                    if k == 0:
                        link(dve.scalar_tensor_tensor(self.logits, self.onehot[0], NEG, self.logits, ALU.mult, ALU.add))
                    else:
                        link(dve.tensor_tensor(self.gap, self.second, self.best, ALU.subtract))
                link(dve.tensor_copy(self.found, self.gap))
                dve.wait_ge(rt_exp, self.n + 1)
                link(dve.tensor_scalar(self.found, self.grown, 1.0, None, ALU.add))
                link(dve.reciprocal(self.weight[0], self.found))
                link(dve.tensor_tensor(self.weight[1], self.grown, self.weight[0], ALU.mult))

        e1_mask, e1_maskt, e1_maskc = sem("e1_mask"), sem("e1_maskt"), sem("e1_maskc")
        e1_low, e1_lowc, e1_lowm, e1_hid = sem("e1_low"), sem("e1_lowc"), sem("e1_lowm"), sem("e1_hid")
        e1_gate, e1_act, e1_z, e1_zm, e1_out, e1_added = (sem("e1_gate"), sem("e1_act"), sem("e1_z"), sem("e1_zm"),
                                                          sem("e1_out"), sem("e1_added"))

        def lora_experts_stage(gate):
            arena.clear()
            wreg.clear()
            wlow.clear()
            LORA_SCALE = 2.0
            wg, wu = wreg.take(128, DC, F), wreg.take(128, DC, F)
            wd = wreg.take(128, FC, D)
            a1, a3 = wreg.take(128, DC, ER), wreg.take(128, DC, ER)
            b1, b3 = wreg.take(128, F), wreg.take(128, F)
            a2 = wreg.take(128, FC, ER)
            b2 = wreg.take(128, D)
            router = wreg.take(128, DC, E)
            top = TopTwo(router)
            top.plan()
            wide = [arena.take(T, E, ER // E, dtype=BF16) for _ in range(2)]
            mask_t = arena.take(128, 2, B * T, dtype=BF16)
            weight = arena.take(T, 2, B)
            low = arena.take(128, 2, GT)
            lowm = [[arena.take(128, GT) for _ in range(2)] for _ in range(2)]
            act_t = [arena.take(128, FC, GT) for _ in range(2)]
            silu = [arena.take(128, GT) for _ in range(2)]
            zm = [arena.take(128, GT) for _ in range(2)]
            weights_ready = expect(10)
            order = [(0, 0)]
            for f in range(1, FC):
                order += [(f, 0), (f - 1, 1)]
            order.append((FC - 1, 1))
            when = {fk: n for n, fk in enumerate(order)}

            def sync(sp):
                for dst, name in ((router, "e1_router"), (a1, "e1_a1"), (a3, "e1_a3"), (wg, "e1_gate"), (wu, "e1_up"), (b1, "e1_b1"),
                                  (b3, "e1_b3"), (wd, "e1_down"), (a2, "e1_a2"), (b2, "e1_b2")):
                    sp.dma_start(dst, a[name]).then_inc(loaded, 16)
                sp.wait_ge(loaded, weights_ready)

            def gpsimd(pool):
                top.make_ranks(pool)

            def tensor(pe):
                pe.wait_ge(loaded, weights_ready)
                top.logits_pe(pe)
                for b in range(B):
                    for k in range(2):
                        m = b * 2 + k
                        pe.wait_ge(e1_mask, m + 1)
                        if b % GB == 0 and b >= 2 * GB:
                            pe.wait_ge(e1_maskc, (b // GB - 1) * 2)
                        mm = pe.matmul(ps[:, 2 + 2 * (b // GB % 2) + k, (b % GB) * T:(b % GB + 1) * T], wide[k].rearrange("p e r -> p (e r)"),
                                       ident16[:, :], start=True, stop=True)
                        mm.then_inc(e1_maskt, 1)
                pe.wait_ge(e1_maskc, 2 * G)

                def hidden(g, f, k):
                    for q, (w, bq) in enumerate(((wg, b1), (wu, b3))):
                        dst = ps[:, 2 + 2 * (f % 3) + q, 0:GT]
                        if k == 0:
                            for c in range(DC):
                                pe.matmul(dst, w[:, c, f * 128:(f + 1) * 128], xn_t[:, c, bass.ds(g * GT, GT)],
                                          start=(c == 0), stop=False)
                        mm = pe.matmul(dst, bq[:, f * 128:(f + 1) * 128], lowm[q][k], start=False, stop=True, skip_group_check=k == 1)
                    mm.then_inc(e1_hid, 1)

                def step(g):
                    at_least(pe, e1_zm, g * 2)
                    for q, w in ((0, a1), (1, a3)):
                        for c in range(DC):
                            mm = pe.matmul(ps[:, q, 0:GT], w[:, c, :], xn_t[:, c, bass.ds(g * GT, GT)], start=(c == 0), stop=(c == DC - 1))
                        mm.then_inc(e1_low, 1)
                    at_least(pe, e1_added, g * GB * 2)
                    pe.wait_ge(e1_lowm, (g + 1) * 6)
                    for f in range(FC + 1):
                        if f < FC:
                            if f >= 3:
                                pe.wait_ge(e1_act, g * (FC * 2) + when[f - 3, 1] + 1)
                            hidden(g, f, 0)
                        if f > 0:
                            pe.wait_ge(e1_act, g * (FC * 2) + when[f - 1, 0] + 1)
                            hidden(g, f - 1, 1)
                    for k in range(2):
                        for f in range(FC):
                            pe.wait_ge(e1_act, g * (FC * 2) + when[f, k] + 1)
                            mm = pe.matmul(ps[:, k, 0:GT], a2[:, f, :], act_t[k][:, f, :], start=(f == 0), stop=(f == FC - 1))
                        mm.then_inc(e1_z, 1)
                    pe.wait_ge(e1_act, (g + 1) * (FC * 2))
                    for q in range(GB):
                        for k in range(2):
                            if q * 2 + k >= 6:
                                pe.wait_ge(e1_added, g * (GB * 2) + q * 2 + k - 5)
                            dst = ps[0:T, 2 + (q * 2 + k) % 6, 0:D]
                            for f in range(FC):
                                pe.matmul(dst, act_t[k][:, f, q * T:(q + 1) * T], wd[:, f, :], start=(f == 0), stop=False)
                            pe.wait_ge(e1_zm, g * 2 + k + 1)
                            pe.matmul(dst, zm[k][:, q * T:(q + 1) * T], b2, start=False, stop=True).then_inc(e1_out, 1)

                groups(pe, step)

            def scalar(act):
                top.exp_act(act)
                act.activation(idle[:, :], one[:, :], ACT.Silu)
                for g in range(G):
                    for k in range(2):
                        act.wait_ge(e1_maskt, (g * GB + GB - 1) * 2 + k + 1)
                        act.activation(mask_t[:, k, g * GT:(g + 1) * GT], ps[:, 2 + 2 * (g % 2) + k, 0:GT], ACT.Copy).then_inc(e1_maskc, 1)

                def step(g):
                    for q in range(2):
                        act.wait_ge(e1_low, g * 2 + q + 1)
                        at_least(act, e1_lowm, g * 6)
                        act.activation(low[:, q, :], ps[:, q, 0:GT], ACT.Copy).then_inc(e1_lowc, 1)
                    for n, (f, k) in enumerate(order):
                        m = g * (FC * 2) + n
                        act.wait_ge(e1_hid, m + 1)
                        at_least(act, e1_act, m - 1)
                        act.activation(silu[n % 2], ps[:, 2 + 2 * (f % 3), 0:GT], ACT.Silu).then_inc(e1_gate, 1)

                groups(act, step)

            def vector(dve):
                top.choose(dve)
                for k in range(2):
                    dve.tensor_scalar(weight[:, k, :], top.weight[k], gates[0:T, gate:gate + 1], None, ALU.mult)
                for b in range(B):
                    for k in range(2):
                        m = b * 2 + k
                        at_least(dve, e1_maskt, m - 1)
                        dve.tensor_scalar(wide[k], top.onehot[k][:, b, :].unsqueeze(2).broadcast_to([T, E, ER // E]), LORA_SCALE, None,
                                          ALU.mult).then_inc(e1_mask, 1)

                def step(g):
                    cols = bass.ds(g * GT, GT)
                    at_least(dve, e1_z, g * 2)
                    if isinstance(g, int):
                        dve.wait_ge(e1_maskc, 2 * G)
                    for q in range(2):
                        dve.wait_ge(e1_lowc, g * 2 + q + 1)
                        for k in range(2):
                            dve.tensor_tensor(lowm[q][k], low[:, q, :], mask_t[:, k, cols], ALU.mult).then_inc(e1_lowm, 1)
                        dve.wait_ge(e1_lowm, g * 6 + q * 3 + 2)
                        dve.tensor_tensor(lowm[q][1], lowm[q][1], lowm[q][0], ALU.subtract).then_inc(e1_lowm, 1)
                    at_least(dve, e1_out, g * (GB * 2))
                    for n, (f, k) in enumerate(order):
                        dve.wait_ge(e1_gate, g * (FC * 2) + n + 1)
                        dve.tensor_tensor(act_t[k][:, f, :], silu[n % 2], ps[:, 3 + 2 * (f % 3), 0:GT], ALU.mult).then_inc(e1_act, 1)
                    for k in range(2):
                        dve.wait_ge(e1_z, g * 2 + k + 1)
                        dve.tensor_tensor(zm[k], ps[:, k, 0:GT], mask_t[:, k, cols], ALU.mult).then_inc(e1_zm, 1)
                    for q in range(GB):
                        b = g * GB + q
                        for k in range(2):
                            m = g * (GB * 2) + q * 2 + k
                            dve.wait_ge(e1_out, m + 1)
                            at_least(dve, e1_added, m)
                            dve.scalar_tensor_tensor(x[:, b, :], ps[0:T, 2 + (q * 2 + k) % 6, 0:D], weight[:, k, bass.ds(b, 1)], x[:, b, :],
                                                     ALU.mult, ALU.add).then_inc(e1_added, 1)

                groups(dve, step)

            stage(sync, gpsimd, scalar, vector, tensor)

        r_h, r_act, r_out, r_added = sem("r_h"), sem("r_act"), sem("r_out"), sem("r_added")

        def relu_stage():
            arena.clear()
            wreg.clear()
            w1, w2 = wreg.take(128, DC, F), wreg.take(128, FC, D)
            b1 = wreg.take(128, FC)
            weights_ready = expect(4)
            hid = [arena.take(128, FC, GT) for _ in range(2)]
            row = arena.take(128, D)
            add_bias = bias(h, one[0:T, :], row[0:T, :])
            biased = bias_done()
            turned = ln_end["turned"]

            def sync(sp):
                sp.dma_start(row, a["r_b2"].partition_broadcast(128)).then_inc(loaded, 16)
                for dst, name in ((w1, "r_w1"), (b1, "r_b1"), (w2, "r_w2")):
                    sp.dma_start(dst, a[name]).then_inc(loaded, 16)
                sp.wait_ge(loaded, weights_ready)

            def pairs(eng, step):
                step(0, 0)
                step(1, 1)
                with eng.Fori(1, G // 2) as i:
                    step(i * 2, 0)
                    step(i * 2 + 1, 1)

            def tensor(pe):
                pe.wait_ge(loaded, weights_ready)
                pe.wait_ge(ln_evac, turned)

                def step(g, u):
                    for f in range(FC):
                        n = g * FC + f
                        at_least(pe, r_act, n - 1)
                        for c in range(DC):
                            mm = pe.matmul(ps[:, f % 2, 0:GT], w1[:, c, f * 128:(f + 1) * 128], xn_t[:, c, bass.ds(g * GT, GT)],
                                           start=(c == 0), stop=(c == DC - 1))
                        mm.then_inc(r_h, 1)
                    pe.wait_ge(r_act, (g + 1) * FC)
                    for q in range(GB):
                        at_least(pe, r_added, g * GB + q - 1)
                        for f in range(FC):
                            mm = pe.matmul(ps[0:T, 2 + q % 2, 0:D], hid[u][:, f, q * T:(q + 1) * T], w2[:, f, :], start=(f == 0), stop=(f == FC - 1))
                        mm.then_inc(r_out, 1)

                pairs(pe, step)

            def scalar(act):
                act.wait_ge(loaded, weights_ready)

                def step(g, u):
                    at_least(act, r_out, (g - 1) * GB)
                    for f in range(FC):
                        act.wait_ge(r_h, g * FC + f + 1)
                        act.activation(hid[u][:, f, :], ps[:, f % 2, 0:GT], ACT.Relu, bias=b1[:, f:f + 1]).then_inc(r_act, 1)

                pairs(act, step)

            def vector(dve):
                dve.wait_ge(loaded, weights_ready)
                add_bias(dve)
                dve.wait_ge(bias_added, biased)

                def step(g, u):
                    for q in range(GB):
                        b = g * GB + q
                        dve.wait_ge(r_out, b + 1)
                        dve.tensor_tensor(h[:, b, :], h[:, b, :], ps[0:T, 2 + q % 2, 0:D], ALU.add).then_inc(r_added, 1)

                pairs(dve, step)

            stage(sync, None, scalar, vector, tensor)

        pk_group, pk_q, pk_qc = sem("pk_group"), sem("pk_q"), sem("pk_qc")
        pk_h, pk_gate, pk_act = sem("pk_h"), sem("pk_gate"), sem("pk_act")
        pk_emb, pk_silu, pk_sim, pk_simc = sem("pk_emb"), sem("pk_silu"), sem("pk_sim"), sem("pk_simc")
        pk_step, pk_gexp, pk_sum, pk_dexp, pk_kept = (sem("pk_step"), sem("pk_gexp"), sem("pk_sum"),
                                                              sem("pk_dexp"), sem("pk_kept"))
        pk_top = sem("pk_top")
        pk_mixed, pk_turned, pk_turnc, pk_out, pk_added = (sem("pk_mixed"), sem("pk_turned"), sem("pk_turnc"), sem("pk_out"), sem("pk_added"))

        def product_key_stage(gate):
            arena.clear()
            wreg.clear()
            wlow.clear()
            wg, wu = wreg.take(128, DC, F), wreg.take(128, DC, F)
            wd = wreg.take(128, FC, D)
            wq = wreg.take(128, DC, 2 * PH * PK)
            keys = wreg.take(128, 4, 2 * PK)
            de, ue = wreg.take(128, DC, NEXP), wreg.take(128, NEXP // 128, D)
            bcols = wreg.take(128, 2, FC)
            group_t = arena.take(128, DC, GT)
            q_t = arena.take(128, 4, GT)
            hid = arena.take(128, FC, GT)
            silu = [arena.take(128, GT) for _ in range(2)]
            act_e = [arena.take(T, NEXP) for _ in range(GB)]
            sims = [arena.take(T, 2 * PH, PK) for _ in range(GB)]
            sums = [arena.take(T, PI, PK) for _ in range(2)]
            exps = [arena.take(T, PI, PK) for _ in range(2)]
            mix = arena.take(T, NEXP)
            mix_t = arena.take(128, NEXP // 128, T)
            K = 8
            best = arena.take(T, 2 * PH, K)
            index = arena.take(T, PH, K, dtype=mybir.dt.uint32)
            beyond = arena.take(T, PH, K)
            grid, shifted, chosen = (arena.take(T, PH, K, K) for _ in range(3))
            top = arena.take(T, PH, K)
            negmax, total, share, clamped = (arena.take(T, PH) for _ in range(4))
            rowsum = arena.take(T, PH, K)
            rowclamp = arena.take(T, PH, K)
            last = arena.take(T, 2)
            weights_ready = expect(10)
            row = arena.take(128, D)
            add_bias = bias(x, gates[0:T, gate:gate + 1], row[0:T, :])
            biased = bias_done()
            turned = ln_end["turned"]
            keys_cleared = expect_made(1)
            LINKS, SHIFTED = 16, 5

            def sync(sp):
                sp.dma_start(row, a["p_bd"].partition_broadcast(128)).then_inc(loaded, 16)
                for dst, name in ((wq, "p_q"), (wg, "p_gate"), (wu, "p_up"), (bcols, "p_bcols"), (de, "p_down_e"), (wd, "p_down"), (ue, "p_up_e")):
                    sp.dma_start(dst, a[name]).then_inc(loaded, 16)
                sp.wait_ge(const_made, keys_cleared)
                for q in range(2):
                    sp.dma_start(keys[64 * q:64 * q + 64, :, 64 * q:64 * q + 64], a["p_keys"][64 * q:64 * q + 64]).then_inc(loaded, 16)
                sp.wait_ge(loaded, weights_ready)

            def tensor(pe):
                pe.wait_ge(loaded, weights_ready)

                def step(g):
                    pe.wait_ge(pk_group, g + 1)
                    for c in range(4):
                        if c < 2:
                            at_least(pe, pk_act, g * FC)
                        else:
                            pe.wait_ge(pk_qc, g * 4 + c - 1)
                        for d in range(DC):
                            mm = pe.matmul(ps[:, c % 2, 0:GT], wq[:, d, c * 128:(c + 1) * 128], group_t[:, d, :], start=(d == 0), stop=(d == DC - 1))
                        mm.then_inc(pk_q, 1)
                    pe.wait_ge(pk_qc, (g + 1) * 4)
                    at_least(pe, pk_turnc, g * GB * 2)
                    for f in range(FC):
                        at_least(pe, pk_act, g * FC + f - 1)
                        for q, w in ((0, wg), (1, wu)):
                            for d in range(DC):
                                mm = pe.matmul(ps[:, 2 * (f % 2) + q, 0:GT], w[:, d, f * 128:(f + 1) * 128], group_t[:, d, :],
                                               start=(d == 0), stop=(d == DC - 1))
                        mm.then_inc(pk_h, 1)
                    for q in range(GB):
                        n = g * GB + q
                        at_least(pe, pk_silu, n)
                        for e in range(2):
                            for d in range(DC):
                                mm = pe.matmul(ps[0:T, 4 + e, :], group_t[:, d, q * T:(q + 1) * T], de[:, d, e * 512:(e + 1) * 512],
                                               start=(d == 0), stop=(d == DC - 1))
                        mm.then_inc(pk_emb, 1)
                        at_least(pe, pk_simc, n)
                        for c in range(4):
                            mm = pe.matmul(ps[0:T, 6, c * 128:(c + 1) * 128], q_t[:, c, q * T:(q + 1) * T], keys[:, c, :], start=True, stop=True)
                        mm.then_inc(pk_sim, 1)
                    pe.wait_ge(pk_act, (g + 1) * FC)
                    for q in range(GB):
                        n = g * GB + q
                        at_least(pe, pk_added, n)
                        for f in range(FC):
                            pe.matmul(ps[0:T, 7, 0:D], hid[:, f, q * T:(q + 1) * T], wd[:, f, :], start=(f == 0), stop=False)
                        pe.wait_ge(pk_mixed, n + 1)
                        at_least(pe, pk_turnc, n * 2)
                        for k in range(NEXP // 128):
                            mm = pe.transpose(ps[:, 2 + k // 4, (k % 4) * T:(k % 4 + 1) * T], mix[:, k * 128:(k + 1) * 128], ident[0:T, 0:T])
                        mm.then_inc(pk_turned, 1)
                        pe.wait_ge(pk_turnc, n * 2 + 2)
                        for k in range(NEXP // 128):
                            mm = pe.matmul(ps[0:T, 7, 0:D], mix_t[:, k, :], ue[:, k, :], start=False, stop=(k == NEXP // 128 - 1))
                        mm.then_inc(pk_out, 1)

                groups(pe, step)

            def scalar(act):
                act.wait_ge(loaded, weights_ready)

                def turned(n):
                    act.wait_ge(pk_turned, n + 1)
                    at_least(act, pk_out, n)
                    for k in range(2):
                        act.activation(mix_t[:, 4 * k:4 * k + 4, :], ps[:, 2 + k, 0:4 * T].rearrange("p (k t) -> p k t", k=4),
                                       ACT.Copy).then_inc(pk_turnc, 1)

                def step(g):
                    at_least(act, pk_sim, g * GB)
                    for c in range(4):
                        act.wait_ge(pk_q, g * 4 + c + 1)
                        act.activation(q_t[:, c, :], ps[:, c % 2, 0:GT], ACT.Copy).then_inc(pk_qc, 1)
                    for f in range(FC):
                        n = g * FC + f
                        act.wait_ge(pk_h, n + 1)
                        at_least(act, pk_act, n - 1)
                        act.activation(silu[f % 2], ps[:, 2 * (f % 2), 0:GT], ACT.Silu, bias=bcols[:, 0, f:f + 1]).then_inc(pk_gate, 1)
                    for q in range(GB):
                        n = g * GB + q
                        act.wait_ge(pk_emb, n + 1)
                        at_least(act, pk_mixed, n - GB + 1)
                        act.activation(act_e[q].rearrange("p (e k) -> p e k", e=2), ps[0:T, 4:6, :], ACT.Silu).then_inc(pk_silu, 1)
                        act.wait_ge(pk_sim, n + 1)
                        at_least(act, pk_sum, (n - GB + 1) * PH)
                        act.activation(sims[q], ps[0:T, 6, :].rearrange("p (h k) -> p h k", k=PK), ACT.Copy).then_inc(pk_simc, 1)
                    for q in range(GB):
                        n = g * GB + q
                        act.wait_ge(pk_step, n * LINKS + SHIFTED)
                        act.activation(shifted, shifted, ACT.Exp).then_inc(pk_gexp, 1)
                        for hd in range(PH):
                            m = n * PH + hd
                            act.wait_ge(pk_sum, m + 1)
                            at_least(act, pk_kept, m - 1)
                            act.activation(exps[hd % 2], sums[hd % 2], ACT.Exp, bias=negmax[:, hd:hd + 1]).then_inc(pk_dexp, 1)
                        if q > 0:
                            turned(n - 1)
                    turned(g * GB + GB - 1)

                groups(act, step)

            def gpsimd(pool):
                pool.memset(keys, 0.0).then_inc(const_made, 1)
                pool.wait_ge(ln_evac, turned)

                def step(g):
                    at_least(pool, pk_emb, g * GB)
                    pool.tensor_copy(group_t, xn_t[:, :, bass.ds(g * GT, GT)]).then_inc(pk_group, 1)
                    for q in range(GB):
                        n = g * GB + q
                        pool.wait_ge(pk_simc, n + 1)
                        for hd in range(PH):
                            m = n * PH + hd
                            at_least(pool, pk_kept, m - 1)
                            pool.tensor_tensor(sums[hd % 2], sims[q][:, hd, 0:PI].unsqueeze(2).broadcast_to([T, PI, PK]),
                                               sims[q][:, PH + hd, :].unsqueeze(1).broadcast_to([T, PI, PK]), ALU.add).then_inc(pk_sum, 1)

                groups(pool, step)

            def vector(dve):
                dve.wait_ge(loaded, weights_ready)
                add_bias(dve)
                dve.wait_ge(bias_added, biased)

                def add(n, b):
                    dve.wait_ge(pk_out, n + 1)
                    dve.scalar_tensor_tensor(x[:, b, :], ps[0:T, 7, 0:D], gates[0:T, gate:gate + 1], x[:, b, :], ALU.mult, ALU.add).then_inc(pk_added, 1)

                def mix_batch(g, q):
                    n = g * GB + q
                    done = [0]

                    def link(ins):
                        done[0] += 1
                        ins.then_inc(pk_step, 1)
                        dve.wait_ge(pk_step, n * LINKS + done[0])

                    def over(v):
                        return v.broadcast_to([T, PH, K * K])

                    def hold():
                        dve.memset(last[:, 1:2], 0.0)

                    flat = "p h i j -> p h (i j)"
                    dve.wait_ge(pk_simc, n + 1)
                    hold()
                    for s in range(2 * PH):
                        ins = dve.max(best[:, s, :], sims[q][:, s, :])
                    link(ins)
                    link(dve.tensor_tensor(grid, best[:, 0:PH, :].unsqueeze(3).broadcast_to([T, PH, K, K]),
                                           best[:, PH:2 * PH, :].unsqueeze(2).broadcast_to([T, PH, K, K]), ALU.add))
                    hold()
                    for s in range(PH):
                        ins = dve.max_index(index[:, s, :], best[:, s, :], sims[q][:, s, :])
                    for s in range(PH):
                        ins = dve.max(top[:, s, :], grid[:, s].rearrange("p i j -> p (i j)"))
                    link(ins)
                    at_least(dve, pk_dexp, n * PH)
                    link(dve.tensor_scalar(negmax, top[:, :, 0], -1.0, None, ALU.mult))
                    link(dve.tensor_tensor(shifted.rearrange(flat), grid.rearrange(flat), over(top[:, :, 0:1]), ALU.subtract))
                    link(dve.tensor_scalar(beyond, index, float(PI), None, ALU.is_ge))
                    link(dve.tensor_tensor(chosen.rearrange(flat), grid.rearrange(flat), over(top[:, :, K - 1:K]), ALU.is_ge))
                    dve.wait_ge(pk_gexp, n + 1)
                    link(dve.tensor_tensor(chosen.rearrange(flat), chosen.rearrange(flat), shifted.rearrange(flat), ALU.mult))
                    link(dve.tensor_reduce(rowsum, chosen, AX.X, ALU.add))
                    link(dve.tensor_reduce(total, rowsum, AX.X, ALU.add))
                    link(dve.reciprocal(share, total))
                    link(dve.tensor_tensor(rowclamp, rowsum, beyond, ALU.mult))
                    link(dve.tensor_reduce(clamped, rowclamp, AX.X, ALU.add))
                    link(dve.tensor_tensor(clamped, clamped, share, ALU.mult))
                    link(dve.tensor_reduce(last[:, 0:1], clamped, AX.X, ALU.add))
                    at_least(dve, pk_turned, n)
                    for hd in range(PH):
                        m = n * PH + hd
                        dve.wait_ge(pk_dexp, m + 1)
                        dve.scalar_tensor_tensor(exps[hd % 2], sums[hd % 2], top[:, hd, K - 1:K], exps[hd % 2], ALU.is_ge, ALU.mult).then_inc(pk_top, 1)
                        dve.wait_ge(pk_top, m + 1)
                        flat_e = exps[hd % 2].rearrange("p i j -> p (i j)")
                        if hd == 0:
                            dve.tensor_scalar(mix, flat_e, share[:, 0:1], None, ALU.mult).then_inc(pk_kept, 1)
                        else:
                            dve.wait_ge(pk_kept, m)
                            dve.scalar_tensor_tensor(mix, flat_e, share[:, hd:hd + 1], mix, ALU.mult, ALU.add).then_inc(pk_kept, 1)
                    dve.wait_ge(pk_kept, (n + 1) * PH)
                    link(dve.tensor_tensor(mix[:, NEXP - 1:NEXP], mix[:, NEXP - 1:NEXP], last[:, 0:1], ALU.add))
                    assert done[0] == LINKS
                    dve.wait_ge(pk_silu, n + 1)
                    dve.tensor_tensor(mix, mix, act_e[q], ALU.mult).then_inc(pk_mixed, 1)

                def step(g):
                    at_least(dve, pk_out, g * GB)
                    for f in range(FC):
                        dve.wait_ge(pk_gate, g * FC + f + 1)
                        dve.scalar_tensor_tensor(hid[:, f, :], ps[:, 2 * (f % 2) + 1, 0:GT], bcols[:, 1, f:f + 1], silu[f % 2],
                                                 ALU.add, ALU.mult).then_inc(pk_act, 1)
                    for q in range(GB):
                        mix_batch(g, q)
                        if q > 0:
                            add(g * GB + q - 1, g * GB + q - 1)
                    add(g * GB + GB - 1, g * GB + GB - 1)

                groups(dve, step)

            stage(sync, gpsimd, scalar, vector, tensor)

        m_prefix, m_step, m_index = sem("m_prefix"), sem("m_step"), sem("m_index")
        m_w = [sem("m_w0"), sem("m_w1")]
        m_sent, m_x, m_rows = sem("m_sent"), [sem("m_x0"), sem("m_x1")], [sem("m_rows0"), sem("m_rows1")]
        m_xt, m_xtc, m_half, m_biased = sem("m_xt"), sem("m_xtc"), sem("m_half"), sem("m_biased")
        m_h, m_gate, m_act, m_out, m_res = sem("m_h"), sem("m_gate"), sem("m_act"), sem("m_out"), sem("m_res")
        m_stat, m_aggr, m_eps, m_rstd, m_gain, m_y = sem("m_stat"), sem("m_aggr"), sem("m_eps"), sem("m_rstd"), sem("m_gain"), sem("m_y")
        m_stored, m_got, m_added = [sem("m_stored0"), sem("m_stored1")], [sem("m_got0"), sem("m_got1")], sem("m_added")

        def routed_experts_stage(gate):
            arena.clear()
            wreg.clear()
            wlow.clear()
            EPS = 1e-12
            kept = ln_end["stored"]
            inputs_ready = expect(2)
            HALVES = BS // 128
            TOP_BLOCKS = -(-(B * T) // BS)
            weights = [wreg.take(128, W_IN + W_OUT + W_B) for _ in range(2)]
            w_in = [w[:, 0:W_IN].rearrange("p (q c f) -> p q c f", q=2, c=DC) for w in weights]
            w_out = [w[:, W_IN:W_IN + W_OUT].rearrange("p (f d) -> p f d", f=FC) for w in weights]
            bcols = [w[:, W_IN + W_OUT:].rearrange("p (q f) -> p q f", q=2) for w in weights]
            router = wlow.take(128, DC, E)
            br = arena.take(T, E)
            top = TopTwo(router, br)
            top.plan()
            routing_made = expect_made(4)
            coef = arena.take(T, 2, B)
            before = arena.take(T, T)
            ones = arena.take(T, 128)
            thresholds = arena.take(128, E, TOP_BLOCKS)
            block_no = arena.take(128, BLOCKS, E)
            lane = arena.take(128, 2)
            lane_i = arena.take(128, 2, dtype=I32)
            both = arena.take(T, B, E)
            run = arena.take(128, B + 1, E)
            filled = arena.take(128, E, TOP_BLOCKS)
            blocks_of = arena.take(128, E)
            first = arena.take(128, E)
            started = arena.take(128, BLOCKS, E)
            expert = arena.take(128, BLOCKS)
            w_index = arena.take(128, BLOCKS, dtype=mybir.dt.uint32)
            row_index = arena.take(128, BLOCKS, dtype=mybir.dt.uint32)
            place = arena.take(T, B, E)
            picked = arena.take(T, B, E)
            slot = [arena.take(T, B, dtype=mybir.dt.uint32) for _ in range(2)]
            half_b = [arena.take(128, FC) for _ in range(2)]
            rows = [arena.take(128, 3 * D) for _ in range(2)]
            x_in = [arena.take(128, HALVES, D) for _ in range(2)]
            x_t = [arena.take(128, DC, BS) for _ in range(2)]
            gelu = [arena.take(128, BS) for _ in range(2)]
            tanh = [arena.take(128, BS) for _ in range(2)]
            hid = [arena.take(128, FC, BS) for _ in range(2)]
            biased = [arena.take(128, HALVES, D) for _ in range(2)]
            res = arena.take(128, HALVES, D)
            y = [arena.take(128, HALVES, D) for _ in range(2)]
            stats = arena.take(128, HALVES, 6)
            moments = arena.take(128, HALVES, 2)
            eps = arena.take(128, HALVES)
            rstd = arena.take(128, HALVES)
            exponent = arena.take(128, HALVES)
            spare = arena.take(128, 2)
            RING = 2
            got = [arena.take(T, 2 * D) for _ in range(RING)]
            SENDS = 2 * B

            def over_blocks(eng, step):
                step(0, 0, 0)
                step(1, 1, 0)
                with eng.Fori(1, BLOCKS // 2) as i:
                    step(i * 2, 0, i)
                    step(i * 2 + 1, 1, i)
                step(BLOCKS - 1, (BLOCKS - 1) % 2, BLOCKS // 2)

            def sync(sp):
                for dst, src in ((router, a["m_router"]), (br, a["m_br"].partition_broadcast(T))):
                    sp.dma_start(dst, src).then_inc(loaded, 16)

                def load(j, u):
                    sp.dma_start(x_in[u], sent[bass.ds(j * BS, BS), :].rearrange("(q p) d -> p q d", p=128)).then_inc(m_x[u], 16)

                def store(j, u):
                    sp.wait_ge(m_y, (j + 1) * HALVES)
                    sp.dma_start(returned[bass.ds(j * BS, BS), :].rearrange("(q p) d -> p q d", p=128), y[u]).then_inc(m_stored[u], 16)

                sp.wait_ge(m_sent, 16 * SENDS)
                load(0, 0)
                load(1, 1)
                with sp.Fori(0, (BLOCKS - 1) // 2 - 1) as i:
                    for u in range(2):
                        store(i * 2 + u, u)
                        load(i * 2 + u + 2, u)
                last = BLOCKS - 3
                store(last, last % 2)
                load(last + 2, last % 2)
                store(last + 1, (last + 1) % 2)
                store(last + 2, last % 2)

            def gpsimd(pool):
                top.make_ranks(pool)
                pool.memset(before, 1.0).then_inc(const_made, 1)
                pool.memset(ones, 1.0)
                pool.memset(eps, EPS)
                pool.memset(exponent, -0.5)
                for k in range(TOP_BLOCKS):
                    pool.memset(thresholds[:, :, k], float(k * BS))
                for k in range(BLOCKS):
                    pool.memset(block_no[:, k, :], float(k))
                pool.iota(lane_i, pattern=[[0, 2]], base=-128, channel_multiplier=1).then_inc(const_made, 1)
                pool.wait_ge(const_made, routing_made - 2)
                pool.tensor_copy(lane, lane_i).then_inc(const_made, 1)
                pool.affine_select(out=before, in_=before, compare_op=ALU.is_gt, fill=0.0, base=0, pattern=[[1, T]],
                                   channel_multiplier=-1).then_inc(const_made, 1)

                def gather_weights(j):
                    pool.indirect_dma_start(weights[j % 2], None, a["m_weights"], bass.IndirectOffsetOnAxis(ap=w_index[:, j:j + 1], axis=0)
                                            ).then_inc(m_w[j % 2], 16)

                def gather_rows(j):
                    pool.indirect_dma_start(rows[j % 2], None, a["m_rows"], bass.IndirectOffsetOnAxis(ap=row_index[:, j:j + 1], axis=0)
                                            ).then_inc(m_rows[j % 2], 16)

                pool.wait_ge(m_index, 1)
                for j in range(2):
                    gather_weights(j)
                    gather_rows(j)
                pool.wait_ge(m_index, 3)
                pool.wait_ge(cleared, 16)
                pool.wait_ge(ln_stored, kept)
                for k in range(2):
                    for b in range(B):
                        pool.indirect_dma_start(sent, bass.IndirectOffsetOnAxis(ap=slot[k][:, b:b + 1], axis=0), h[:, b, :], None
                                                ).then_inc(m_sent, 16)
                for j in range(BLOCKS):
                    if j + 2 < BLOCKS:
                        pool.wait_ge(m_out, j + 1)
                        gather_weights(j + 2)
                    pool.wait_ge(m_aggr, (j + 1) * HALVES)
                    at_least(pool, m_y, j * HALVES)
                    pool.tensor_tensor(rstd, moments[:, :, 1], eps, ALU.add).then_inc(m_eps, 1)
                    pool.wait_ge(m_eps, j + 1)
                    pool.tensor_tensor(rstd, rstd, exponent, ALU.pow).then_inc(m_rstd, 1)
                    if j + 2 < BLOCKS:
                        pool.wait_ge(m_y, (j + 1) * HALVES)
                        gather_rows(j + 2)
                for u in range(2):
                    pool.wait_ge(m_stored[u], 16 * ((BLOCKS + 1 - u) // 2))
                for b in range(B):
                    at_least(pool, m_added, 2 * (b - RING + 1))
                    for k in range(2):
                        pool.indirect_dma_start(got[b % RING][:, k * D:(k + 1) * D], None, returned,
                                                bass.IndirectOffsetOnAxis(ap=slot[k][:, b:b + 1], axis=0)).then_inc(m_got[b % RING], 16)

            def tensor(pe):
                pe.wait_ge(loaded, inputs_ready)
                top.logits_pe(pe)
                pe.wait_ge(const_made, routing_made)
                pe.wait_ge(m_step, 1)
                pe.matmul(ps[0:T, 1, 0:B * E], before, both.rearrange("p b e -> p (b e)"), start=True, stop=True)
                pe.matmul(ps[:, 2, 0:B * E], ones, both.rearrange("p b e -> p (b e)"), start=True, stop=True).then_inc(m_prefix, 1)

                def turn(j, u, i):
                    pe.wait_ge(m_x[u], (i + 1) * 16)
                    at_least(pe, m_xtc, j)
                    for q in range(HALVES):
                        for c in range(DC):
                            mm = pe.transpose(ps[:, 4, c * BS + q * 128:c * BS + (q + 1) * 128], x_in[u][:, q, c * 128:(c + 1) * 128], ident[:, :])
                    mm.then_inc(m_xt, 1)

                turn(0, 0, 0)

                def step(j, u, i):
                    pe.wait_ge(m_w[u], (i + 1) * 16)
                    pe.wait_ge(m_xtc, j + 1)
                    for f in range(FC):
                        at_least(pe, m_act, j * FC + f - 3)
                        for q in range(2):
                            for c in range(DC):
                                mm = pe.matmul(ps[:, f % 4, q * BS:(q + 1) * BS], w_in[u][:, q, c, f * 128:(f + 1) * 128], x_t[u][:, c, :],
                                               start=(c == 0), stop=(c == DC - 1))
                        mm.then_inc(m_h, 1)
                    if not isinstance(j, int) or j < BLOCKS - 1:
                        turn(j + 1, 1 - u, i + u)
                    at_least(pe, m_res, (j - 1) * HALVES)
                    for q in range(HALVES):
                        for f in range(FC):
                            if q == 0:
                                pe.wait_ge(m_act, j * FC + f + 1)
                            mm = pe.matmul(ps[:, 5 + u, q * D:(q + 1) * D], hid[u][:, f, q * 128:(q + 1) * 128], w_out[u][:, f, :],
                                           start=(f == 0), stop=(f == FC - 1))
                    mm.then_inc(m_out, 1)

                over_blocks(pe, step)

            def scalar(act):
                top.exp_act(act)
                act.activation(idle[:, :], one[:, :], ACT.Gelu)

                def copy(j, u):
                    act.wait_ge(m_xt, j + 1)
                    act.activation(x_t[u], ps[:, 4, 0:DC * BS].rearrange("p (c s) -> p c s", c=DC), ACT.Copy).then_inc(m_xtc, 1)

                copy(0, 0)

                def step(j, u, i):
                    act.wait_ge(m_w[u], (i + 1) * 16)
                    act.wait_ge(m_half, j + 1)
                    for f in range(FC):
                        n = j * FC + f
                        act.wait_ge(m_h, n + 1)
                        at_least(act, m_act, n - 1)
                        act.activation(gelu[f % 2], ps[:, f % 4, 0:BS], ACT.Gelu, bias=bcols[u][:, 0, f:f + 1])
                        act.activation(tanh[f % 2], ps[:, f % 4, BS:2 * BS], ACT.Tanh, scale=0.5, bias=half_b[u][:, f:f + 1]).then_inc(m_gate, 1)
                    if not isinstance(j, int) or j < BLOCKS - 1:
                        copy(j + 1, 1 - u)

                over_blocks(act, step)

            def vector(dve):
                dve.wait_ge(loaded, inputs_ready)
                top.choose(dve)
                for k in range(2):
                    dve.tensor_scalar(coef[:, k, :], top.weight[k], gates[0:T, gate:gate + 1], None, ALU.mult)
                steps = [0]

                def link(ins):
                    steps[0] += 1
                    ins.then_inc(m_step, 1)
                    dve.wait_ge(m_step, steps[0])

                link(dve.tensor_tensor(both, top.onehot[0], top.onehot[1], ALU.add))
                dve.wait_ge(const_made, routing_made)
                dve.wait_ge(m_prefix, 1)
                counts = ps[:, 2, 0:B * E].rearrange("p (b e) -> p b e", e=E)
                dve.memset(first[:, 0:1], 0.0)
                link(dve.memset(run[:, 0, :], 0.0))
                for b in range(B):
                    link(dve.tensor_tensor(run[:, b + 1, :], run[:, b, :], counts[:, b, :], ALU.add))
                link(dve.tensor_tensor(filled, run[:, B, :].unsqueeze(2).broadcast_to([128, E, TOP_BLOCKS]), thresholds, ALU.is_gt))
                link(dve.tensor_reduce(blocks_of, filled, AX.X, ALU.add))
                for e in range(1, E):
                    link(dve.tensor_tensor(first[:, e:e + 1], first[:, e - 1:e], blocks_of[:, e - 1:e], ALU.add))
                link(dve.tensor_tensor(started, block_no, first.unsqueeze(1).broadcast_to([128, BLOCKS, E]), ALU.is_ge))
                link(dve.tensor_reduce(expert, started, AX.X, ALU.add))
                dve.tensor_scalar(row_index, expert, 1.0, None, ALU.subtract)
                dve.tensor_scalar(w_index, expert, 128.0, lane[:, 0:1], ALU.mult, ALU.add).then_inc(m_index, 1)
                link(dve.tensor_tensor(place, ps[0:T, 1, 0:B * E].rearrange("p (b e) -> p b e", e=E), run[0:T, 0:B, :], ALU.add))
                link(dve.scalar_tensor_tensor(place, first[0:T, :].unsqueeze(1).broadcast_to([T, B, E]), float(BS), place, ALU.mult, ALU.add))
                for k in range(2):
                    link(dve.tensor_tensor(picked, top.onehot[k], place, ALU.mult))
                    link(dve.tensor_reduce(top.found, picked, AX.X, ALU.add))
                    dve.tensor_copy(slot[k], top.found).then_inc(m_index, 1)
                    dve.wait_ge(m_index, k + 2)

                def step(j, u, i):
                    dve.wait_ge(m_w[u], (i + 1) * 16)
                    dve.tensor_scalar(half_b[u], bcols[u][:, 1, :], 0.5, None, ALU.mult).then_inc(m_half, 1)
                    dve.wait_ge(m_rows[u], (i + 1) * 16)
                    dve.wait_ge(m_x[u], (i + 1) * 16)
                    dve.tensor_tensor(biased[u], x_in[u], rows[u][:, 0:D].unsqueeze(1).broadcast_to([128, HALVES, D]), ALU.add).then_inc(m_biased, 1)
                    at_least(dve, m_out, j - 1)
                    for f in range(FC):
                        dve.wait_ge(m_gate, j * FC + f + 1)
                        dve.scalar_tensor_tensor(hid[u][:, f, :], tanh[f % 2], 1.0, gelu[f % 2], ALU.add, ALU.mult).then_inc(m_act, 1)
                    dve.wait_ge(m_out, j + 1)
                    dve.wait_ge(m_biased, j + 1)
                    for q in range(HALVES):
                        dve.scalar_tensor_tensor(res[:, q, :], ps[:, 5 + u, q * D:(q + 1) * D], 0.5, biased[u][:, q, :],
                                                 ALU.mult, ALU.add).then_inc(m_res, 1)
                    for q in range(HALVES):
                        dve.wait_ge(m_res, j * HALVES + q + 1)
                        dve.bn_stats(stats[:, q, :], res[:, q, :]).then_inc(m_stat, 1)
                    dve.wait_ge(m_stat, (j + 1) * HALVES)
                    dve.memset(spare, 0.0)
                    for q in range(HALVES):
                        dve.bn_aggr(moments[:, q, :], stats[:, q, :]).then_inc(m_aggr, 1)
                    dve.wait_ge(m_aggr, (j + 1) * HALVES)
                    for q in range(HALVES):
                        dve.scalar_tensor_tensor(res[:, q, :], res[:, q, :], moments[:, q, 0:1], rows[u][:, D:2 * D],
                                                 ALU.subtract, ALU.mult).then_inc(m_gain, 1)
                    dve.wait_ge(m_gain, (j + 1) * HALVES)
                    dve.wait_ge(m_rstd, j + 1)
                    at_least(dve, m_stored[u], i * 16)
                    for q in range(HALVES):
                        dve.scalar_tensor_tensor(y[u][:, q, :], res[:, q, :], rstd[:, q:q + 1], rows[u][:, 2 * D:3 * D],
                                                 ALU.mult, ALU.add).then_inc(m_y, 1)

                over_blocks(dve, step)
                for b in range(B):
                    dve.wait_ge(m_got[b % RING], 32 * (b // RING + 1))
                    for k in range(2):
                        at_least(dve, m_added, 2 * b + k)
                        dve.scalar_tensor_tensor(x[:, b, :], got[b % RING][:, k * D:(k + 1) * D], coef[:, k, b:b + 1], x[:, b, :],
                                                 ALU.mult, ALU.add).then_inc(m_added, 1)

            stage(sync, gpsimd, scalar, vector, tensor)

        stored = sem("stored")

        def end_sync(sp):
            sp.dma_start(a["out"].rearrange("b t d -> t b d"), x[:, :, :]).then_inc(stored, 16)
            sp.wait_ge(stored, 16)

        def chain():
            norm_stage(x, 1e-5)
            w = query_stage(0, 1, x, gates[0:T, 0:1], keys_of=0)
            cross_stage(0, w, 0.25, x, gates[0:T, 0:1])
            norm_stage(x, 1e-5)
            position_experts_stage(4)
            norm_stage(x, 1e-5)
            w = query_stage(1, 1, x, gates[0:T, 1:2], keys_of=1)
            cross_stage(1, w, 0.25, x, gates[0:T, 1:2])
            norm_stage(x, 1e-5)
            lora_experts_stage(5)
            norm_stage(x, 1e-5, keep=h)
            w = query_stage(2, 2, h, one[0:T, :])
            self_stage(2, w, 0.25, h, one[0:T, :])
            norm_stage(h, 1e-6, gain=0, keep=h)
            w = query_stage(3, 1, h, one[0:T, :], keys_of=2)
            cross_stage(2, w, 0.25, h, one[0:T, :])
            norm_stage(h, 1e-6, gain=2, keep=h)
            relu_stage()
            norm_stage(h, 1e-6, gain=4, turn=False, add_gate=2)
            norm_stage(x, 1e-5)
            product_key_stage(6)
            norm_stage(x, 1e-5)
            w = query_stage(4, 1, x, gates[0:T, 3:4], keys_of=3)
            cross_stage(3, w, float(np.log(D) / np.sqrt(DH)), x, gates[0:T, 3:4], masked=True)
            norm_stage(x, 1e-5, keep=h)
            routed_experts_stage(7)

        chain()
        stage(sync=end_sync)

        @block.sync
        def _(sp):
            for program in programs["sync"]:
                program(sp)

        @block.gpsimd
        def _(pool):
            for program in programs["gpsimd"]:
                program(pool)

        @block.scalar
        def _(act):
            for program in programs["scalar"]:
                program(act)

        @block.vector
        def _(dve):
            for program in programs["vector"]:
                program(dve)

        @block.tensor
        def _(pe):
            for program in programs["tensor"]:
                program(pe)


def kernel(**inputs):
    import concourse.bacc as bacc
    from concourse.bass_utils import run_bass_kernel_spmd

    i = {k: np.asarray(v) for k, v in inputs.items()}

    def rows_first(w):
        return w.reshape(-1, 128, w.shape[-1]).transpose(1, 0, 2)

    def columns(v):
        return v.reshape(-1, 128).T

    def attn_set(names, turned):
        return np.stack([rows_first(i[n].T if turned else i[n]) for n in names], axis=1)

    sets = []
    for layer, names, turned in (("L0_xattn_", ("Wq", "Wk", "Wv", "Wo"), True), ("L1_xattn_", ("Wq", "Wk", "Wv", "Wo"), True),
                                 ("L2_xattn_", ("wq1", "wk1", "wv1", "wo1"), False), ("L2_xattn_", ("wq2", "wk2", "wv2", "wo2"), False),
                                 ("L3_xattn_", ("Wq", "Wk", "Wv", "Wo"), True)):
        sets.append(([layer + n for n in names], [layer + "b" + n[1:] for n in names], turned))
    arrays = {
        "x": i["x"],
        "g_xattn": i["g_xattn"],
        "g_ffn": i["g_ffn"],
        "ctx_t": i["ctx_1024"].transpose(0, 2, 1).reshape(B, DC, 128, S2).transpose(0, 2, 1, 3),
        "attn_w": np.stack([attn_set(w, turned) for w, _, turned in sets]),
        "attn_cols": np.stack([np.concatenate([columns(i[b[0]]), columns(i[b[1]])], axis=1) for _, b, _ in sets]),
        "attn_rows": np.stack([np.stack([i[b[2]], i[b[3]]]) for _, b, _ in sets]),
        "am": i["mask_1x1xSxS_fk0"],
        "pm": i["mask_Bx1x1xS_ff1"],
        "mask": i["mask_Bx1xSxS2_if1"].reshape(B, T, S2),
        "pad": i["mask_BxS2_if1"],
        "ln_rows": np.stack([i["L2_xattn_" + n] for n in ("g1", "be1", "g2", "be2", "g3", "be3")]),
        "e0_w1": i["L0_ffn_w1"].reshape(E, DC, 128, F0).transpose(0, 2, 1, 3),
        "e0_w3": i["L0_ffn_w3"].reshape(E, DC, 128, F0).transpose(0, 2, 1, 3),
        "e0_w2": i["L0_ffn_w2"][:, 0:512].reshape(E, 4, 128, D).transpose(0, 2, 1, 3),
        "e0_w2r": i["L0_ffn_w2"][:, 512:].reshape(E, 2, 96, D).transpose(0, 2, 1, 3),
        "e1_router": rows_first(i["L1_ffn_gate_w"].T),
        "e1_gate": rows_first(i["L1_ffn_w_gate"].T),
        "e1_up": rows_first(i["L1_ffn_w_up"].T),
        "e1_down": rows_first(i["L1_ffn_w_down"].T),
        "e1_a1": rows_first(i["L1_ffn_A1"].reshape(ER, D).T),
        "e1_a3": rows_first(i["L1_ffn_A3"].reshape(ER, D).T),
        "e1_b1": i["L1_ffn_B1"].transpose(0, 2, 1).reshape(ER, F),
        "e1_b3": i["L1_ffn_B3"].transpose(0, 2, 1).reshape(ER, F),
        "e1_a2": rows_first(i["L1_ffn_A2"].reshape(ER, F).T),
        "e1_b2": i["L1_ffn_B2"].transpose(0, 2, 1).reshape(ER, D),
        "r_w1": rows_first(i["L2_xattn_w_ff1"]),
        "r_b1": columns(i["L2_xattn_b_ff1"]),
        "r_w2": rows_first(i["L2_xattn_w_ff2"]),
        "r_b2": i["L2_xattn_b_ff2"],
        "p_gate": rows_first(i["L2_ffn_Wg"]),
        "p_up": rows_first(i["L2_ffn_Wu"]),
        "p_down": rows_first(i["L2_ffn_Wd"]),
        "p_bcols": np.stack([columns(i["L2_ffn_bg"]), columns(i["L2_ffn_bu"])], axis=1),
        "p_bd": i["L2_ffn_bd"],
        "p_q": rows_first(i["L2_ffn_Wq"]),
        "p_keys": i["L2_ffn_keys"].transpose(2, 0, 3, 1).reshape(4, 128, PK).transpose(1, 0, 2),
        "p_down_e": rows_first(i["L2_ffn_down_embed"].T),
        "p_up_e": rows_first(i["L2_ffn_up_embed"]),
        "m_router": rows_first(i["L3_ffn_Wr"]),
        "m_br": i["L3_ffn_br"],
        "m_weights": np.concatenate([np.concatenate([rows_first(i["L3_ffn_Wi"][e]).reshape(128, -1), rows_first(i["L3_ffn_Wg"][e]).reshape(128, -1),
                                                     rows_first(i["L3_ffn_Wo"][e]).reshape(128, -1), columns(i["L3_ffn_bi"][e]),
                                                     columns(i["L3_ffn_bg"][e])], axis=1) for e in range(E)]),
        "m_rows": np.concatenate([i["L3_ffn_bo"], i["L3_ffn_gamma"], i["L3_ffn_beta"]], axis=1),
    }
    nc = bacc.Bacc("TRN2", target_bir_lowering=False, num_devices=1)
    feeds, views = {}, {}
    for name, array in arrays.items():
        array = np.ascontiguousarray(array)
        feeds["in_" + name] = array
        views[name] = nc.dram_tensor("in_" + name, array.shape, mybir.dt.from_np(array.dtype), kind="ExternalInput").ap()
    views["out"] = nc.dram_tensor("out", (B, T, D), F32, kind="ExternalOutput").ap()
    build(nc, views)
    result = run_bass_kernel_spmd(nc, [feeds], core_ids=[0])
    return result.results[0]["out"]
```

```python
from contextlib import ExitStack

import concourse.bass as bass
import numpy as np
from concourse import mybir

ACT = mybir.ActivationFunctionType
ALU = mybir.AluOpType
F32 = mybir.dt.float32
BF16 = mybir.dt.bfloat16
F32R = mybir.dt.float32r
I32 = mybir.dt.int32
AX = mybir.AxisListType

B, T, D = 16, 112, 256
S2 = 375
KC, KN = 3, 125
H, DH = 16, 16
DC = D // 128
G, GB = 4, 4
GT = GB * T
PARTS = 3
VW = DH + 1
NEG = -1.0e30
K_PART = (0, 0, 1, 0, 2, 1)
Q_PART = (0, 1, 0, 2, 0, 1)
SROWS = DH * len(K_PART)
AROWS = SROWS + 2
E = 8
F0 = 704
F0_ROWS = (128, 128, 128, 128, 96, 96)
F0_AT = (0, 128, 256, 384, 512, 608)
F = 1024
FC = F // 128
ER = 128
PH, PK = 4, 64
NEXP = 1024
PI = NEXP // PK
BS = 256
BLOCKS = (2 * B * T + E * (BS - 1)) // BS
W_IN, W_OUT, W_B = 2 * DC * F, FC * D, 2 * FC
ATTN = 5
KV_SET = (0, 1, 3, 4)


class Region:

    def __init__(self, tensor, words):
        self.tensor, self.words, self.at = tensor, words, 0

    def clear(self):
        self.at = 0

    def take(self, parts, *dims, dtype=F32):
        count = 1
        for d in dims:
            count *= d
        words = (count + 1) // 2 if dtype == BF16 else count
        words += words % 2
        assert self.at + words <= self.words, (self.at, words)
        view = self.tensor[0:parts, self.at : self.at + words]
        self.at += words
        if dtype != F32:
            view = view.bitcast(dtype)
        view = view[:, 0:count]
        if len(dims) == 1:
            return view
        names = "abcdef"[: len(dims)]
        return view.rearrange(f"p ({' '.join(names)}) -> p {' '.join(names)}", **dict(zip(names, dims)))


def at_least(eng, sem, value):
    if not (isinstance(value, int) and value <= 0):
        eng.wait_ge(sem, value)


def batches(eng, step):
    step(0, 0, 0)
    step(1, 1, 0)
    with eng.Fori(1, B // 2) as i:
        step(i * 2, 0, i)
        step(i * 2 + 1, 1, i)


def build(nc, a):
    ctx = ExitStack()
    with ctx:
        def sb(name, shape, dt=F32):
            return ctx.enter_context(nc.sbuf_tensor(name, shape, dt))

        def sem(name):
            return ctx.enter_context(nc.semaphore(name))

        x = sb("x", [T, B, D])
        h = sb("h", [T, B, D])
        xn_t = sb("xn_t", [128, DC, B * T])
        ident = sb("ident", [128, 128])
        ident16 = sb("ident16", [T, T], BF16)
        neg16 = sb("neg16", [T, GB, T], BF16)
        gates = sb("gates", [128, 8])
        nought = sb("nought", [128, 2 * D])
        one = sb("one", [128, 1])
        idle = sb("idle", [128, 1])
        ln_raw = sb("ln_raw", [T, B, 6])
        ln_tmp = sb("ln_tmp", [T, 5, B])
        ln_mean = sb("ln_mean", [T, B])
        ln_rstd = sb("ln_rstd", [T, B])
        half = sb("half", [T, B])
        XN = 4
        xn2 = [sb(f"xn2_{r}", [T, D]) for r in range(XN)]
        ln_gain = sb("ln_gain", [128, 2, D])
        ln_scale = sb("ln_scale", [T, XN, D])
        attn_cols = sb("attn_cols", [128, ATTN, 4])
        attn_rows = sb("attn_rows", [128, 2, D])
        A_WORDS, W_WORDS, L_WORDS = 22528, 2 * (W_IN + W_OUT + W_B), 2048
        with nc.sbuf_tensor("moe_w_r", [128, 2, 2, DC, F], F32R) as moe_w_r, nc.sbuf_tensor("moe_x_r", [128, 2, 2, DC, BS], F32R) as moe_x_r:
            pass
        MOE_W_WORDS, MOE_X_WORDS = 2 * W_IN, 2 * 2 * DC * BS
        arena = Region(sb("arena", [128, A_WORDS]), A_WORDS)
        with nc.sbuf_tensor("kv_w_r", [128, 2, len(KV_SET), 2, DC, D], F32R) as kv_w_r, nc.sbuf_tensor("kv_ctx_r", [128, 2, 2, DC, S2 + 1], F32R) as kv_ctx_r:
            pass
        with nc.sbuf_tensor("lora_w_r", [128, 2, 2, DC, F], F32R) as lora_w_r, nc.sbuf_tensor("lora_x_r", [128, 2, DC, GT], F32R) as lora_x_r:
            pass
        wreg = Region(sb("wreg", [128, W_WORDS]), W_WORDS)
        wlow = Region(sb("wlow", [128, L_WORDS]), L_WORDS)
        ps = ctx.enter_context(nc.psum_tensor("ps", [128, 8, 512], F32))

        key_parts = nc.dram_tensor("key_parts", (4, B, PARTS, D, S2), BF16, kind="Internal").ap()
        values = nc.dram_tensor("values", (4, B, KN, KC * H * VW), F32, kind="Internal").ap()
        query_parts = nc.dram_tensor("query_parts", (2, PARTS, D, B * T), BF16, kind="Internal").ap()

        sent = nc.dram_tensor("sent", (BLOCKS * BS, D), F32, kind="Internal").ap()
        returned = nc.dram_tensor("returned", (BLOCKS * BS, D), F32, kind="Internal").ap()

        block = ctx.enter_context(nc.Block())
        programs = {"sync": [], "gpsimd": [], "scalar": [], "vector": [], "tensor": []}

        stage_done = sem("stage_done")
        stages = [0]

        def stage(sync=None, gpsimd=None, scalar=None, vector=None, tensor=None, meet=True):
            stages[0] += meet
            all_done = 5 * stages[0]
            for name, program in (("sync", sync), ("gpsimd", gpsimd), ("scalar", scalar), ("vector", vector), ("tensor", tensor)):
                def whole(eng, program=program):
                    if program is not None:
                        program(eng)
                    if meet:
                        eng.drain().then_inc(stage_done, 1)
                        eng.wait_ge(stage_done, all_done)
                programs[name].append(whole)

        loaded = sem("loaded")
        loads = [0]

        def expect(transfers):
            loads[0] += 16 * transfers
            return loads[0]

        in_ready = expect(3)
        const_made = sem("const_made")
        prepared = sem("prepared")
        makes = [0]

        def expect_made(count):
            makes[0] += count
            return makes[0]

        start_made = expect_made(4)
        gate_in = arena.take(128, 8)

        def start_sync(sp):
            sp.dma_start(gate_in[:, 0:4], a["g_xattn"].partition_broadcast(128)).then_inc(loaded, 16)
            sp.dma_start(gate_in[:, 4:8], a["g_ffn"].partition_broadcast(128)).then_inc(loaded, 16)
            sp.dma_start(attn_cols[:, :, :], a["attn_cols"].rearrange("l p c -> p l c")).then_inc(loaded, 16)
            sp.wait_ge(loaded, in_ready)
            sp.wait_ge(const_made, start_made)

        def start_gpsimd(pool):
            pool.memset(ident[:, :], 0.0).then_inc(const_made, 1)
            pool.memset(ident16[:, :], 0.0).then_inc(const_made, 1)
            pool.memset(neg16[:, :, :], 0.0).then_inc(const_made, 1)
            pool.memset(nought[:, :], 0.0).then_inc(const_made, 1)
            pool.memset(half[:, :], -0.5)
            pool.memset(one[:, :], 1.0)
            pool.wait_ge(const_made, start_made)
            pool.affine_select(out=ident[:, :], in_=ident[:, :], compare_op=ALU.not_equal, fill=1.0, base=0,
                               pattern=[[-1, 128]], channel_multiplier=1)
            pool.affine_select(out=ident16[:, :], in_=ident16[:, :], compare_op=ALU.not_equal, fill=1.0, base=0,
                               pattern=[[-1, T]], channel_multiplier=1)
            pool.affine_select(out=neg16[:, :, :], in_=neg16[:, :, :], compare_op=ALU.not_equal, fill=NEG, base=0,
                               pattern=[[0, GB], [-1, T]], channel_multiplier=1)

        def start_scalar(act):
            act.wait_ge(loaded, in_ready)
            act.activation(gates[:, :], gate_in, ACT.Tanh)

        stage(sync=start_sync, gpsimd=start_gpsimd, scalar=start_scalar)

        kv_ctx = [sem("kv_ctx0"), sem("kv_ctx1")]
        kv_w, kv_high, kv_lo = sem("kv_w"), sem("kv_high"), sem("kv_lo")
        kv_v = sem("kv_v")
        part_made, part_hi, part_res, part_mid, part_lo = sem("part_made"), sem("part_hi"), sem("part_res"), sem("part_mid"), sem("part_lo")
        kv_vout = sem("kv_vout")
        kv_kst, kv_vst = [sem("kv_kst0"), sem("kv_kst1")], [sem("kv_vst0"), sem("kv_vst1")]

        def context_stage():
            arena.clear()
            NKV = len(KV_SET)
            weights_ready = expect(2 * NKV)
            ones_made = expect_made(4)
            ctx_t = [arena.take(128, DC, S2 + 1) for _ in range(2)]
            parts = [arena.take(128, DC, PARTS, S2, dtype=BF16) for _ in range(2)]
            rest = [arena.take(128, DC, S2) for _ in range(2)]
            vout = [arena.take(KN, KC, H, VW) for _ in range(2)]
            bv = arena.take(128, NKV, D)
            w = arena.take(128, NKV, 2, DC, D)
            w_r = [kv_w_r[:, part] for part in range(2)]
            ctx_r = [[kv_ctx_r[:, u, part] for part in range(2)] for u in range(2)]
            PRODUCTS = ((0, 0), (0, 1), (1, 0))

            def product(pe, dst, lhs, rhs):
                for n, (i, j) in enumerate(PRODUCTS):
                    for c in range(DC):
                        mm = pe.matmul(dst, lhs(i, c), rhs(j, c), start=(n == 0 and c == 0), stop=(n == len(PRODUCTS) - 1 and c == DC - 1))
                return mm

            def sync(sp):
                sp.dma_start(ctx_t[0][:, :, 0:S2], a["ctx_t"][0]).then_inc(kv_ctx[0], 16)
                for i, s in enumerate(KV_SET):
                    sp.dma_start(w[:, i], a["attn_w"][s, :, 1:3]).then_inc(loaded, 16)
                    sp.dma_start(bv[:, i, :], a["attn_rows"][s, 0].partition_broadcast(128)).then_inc(loaded, 16)
                sp.dma_start(ctx_t[1][:, :, 0:S2], a["ctx_t"][1]).then_inc(kv_ctx[1], 16)
                sp.dma_start(x[:, :, :], a["x"].rearrange("b t d -> t b d")).then_inc(prepared, 16)

                def step(b, u, pair):
                    for i in range(NKV):
                        n = b * NKV + i
                        sp.wait_ge(part_lo, n * 2 + 2)
                        for t in range(DC):
                            sp.dma_start(key_parts[i, b, :, t * 128:(t + 1) * 128, :].rearrange("q p k -> p q k"),
                                         parts[i % 2][:, t]).then_inc(kv_kst[i % 2], 16)
                        sp.wait_ge(kv_vout, n * 2 + 2)
                        sp.dma_start(values[i, b], vout[i % 2].rearrange("p c h w -> p (c h w)")).then_inc(kv_vst[i % 2], 16)

                def more(b, u):
                    step(b, u, None)
                    sp.wait_ge(kv_lo, NKV + b + 1)
                    sp.dma_start(ctx_t[u][:, :, 0:S2], a["ctx_t"][b + 2]).then_inc(kv_ctx[u], 16)

                with sp.Fori(0, B // 2 - 1) as i:
                    more(i * 2, 0)
                    more(i * 2 + 1, 1)
                step(B - 2, 0, None)
                step(B - 1, 1, None)
                sp.wait_ge(prepared, 16)
                for q in range(2):
                    sp.wait_ge(kv_kst[q], 16 * DC * B * NKV // 2)
                    sp.wait_ge(kv_vst[q], 16 * B * NKV // 2)

            def tensor(pe):
                def step(b, u, pair):
                    pe.wait_ge(kv_lo, NKV + b + 1 if not isinstance(b, int) or b > 0 else 1)
                    for i in range(NKV):
                        n = b * NKV + i
                        if isinstance(b, int) and b == 0:
                            pe.wait_ge(kv_lo, 2 + i)
                        at_least(pe, part_res, (n - 1) * 2)
                        for t in range(DC):
                            product(pe, ps[:, 2 * (i % 2) + t, 0:S2 + 1], lambda part, c: w_r[part][:, i, 0, c, t * 128:(t + 1) * 128],
                                    lambda part, c: ctx_r[u][part][:, c, :]).then_inc(part_made, 1)
                        at_least(pe, kv_vout, (n - 1) * 2)
                        for k in range(KC):
                            mm = product(pe, ps[0:KN, 4 + 2 * (i % 2) + k // 2, (k % 2) * D:(k % 2 + 1) * D],
                                         lambda part, c: ctx_r[u][part][:, c, k * KN:(k + 1) * KN], lambda part, c: w_r[part][:, i, 1, c, :])
                            if k > 0:
                                mm.then_inc(kv_v, 1)

                batches(pe, step)

            def scalar(act):
                act.wait_ge(loaded, weights_ready)
                for i in range(NKV):
                    act.activation(w_r[0][:, i], w[:, i], ACT.Copy).then_inc(kv_w, 1)

                def step(b, u, pair):
                    for i, s in enumerate(KV_SET):
                        n = b * NKV + i
                        at_least(act, kv_kst[i % 2], (b * (NKV // 2) + i // 2) * (16 * DC))
                        for t in range(DC):
                            act.wait_ge(part_made, n * 2 + t + 1)
                            act.activation(parts[i % 2][:, t, 0, :], ps[:, 2 * (i % 2) + t, 0:S2], ACT.Identity,
                                           bias=attn_cols[:, s, 2 + t:3 + t]).then_inc(part_hi, 1)
                        for t in range(DC):
                            act.wait_ge(part_res, n * 2 + t + 1)
                            act.activation(parts[i % 2][:, t, 1, :], rest[i % 2][:, t, :], ACT.Copy).then_inc(part_mid, 1)

                batches(act, step)

            def vector(dve):
                for q in range(2):
                    dve.memset(vout[q], 1.0).then_inc(const_made, 1)
                    dve.memset(ctx_t[q][:, :, S2:], 0.0).then_inc(const_made, 1)
                dve.wait_ge(const_made, ones_made)

                def split(b, u, pair):
                    dve.wait_ge(kv_ctx[u], pair * 16 + 16)
                    at_least(dve, kv_v, (b - 1) * (NKV * 2))
                    dve.tensor_copy(ctx_r[u][0], ctx_t[u]).then_inc(kv_high, 1)
                    dve.wait_ge(kv_high, b + 1)
                    dve.tensor_tensor(ctx_r[u][1], ctx_t[u], ctx_r[u][0].bitcast(F32), ALU.subtract).then_inc(kv_lo, 1)

                split(0, 0, 0)
                for i in range(NKV):
                    dve.wait_ge(kv_w, i + 1)
                    dve.tensor_tensor(w_r[1][:, i], w[:, i], w_r[0][:, i].bitcast(F32), ALU.subtract).then_inc(kv_lo, 1)

                def step(b, u, pair):
                    for i, s in enumerate(KV_SET):
                        n = b * NKV + i
                        at_least(dve, part_lo, (n - 1) * 2)
                        for t in range(DC):
                            dve.wait_ge(part_hi, n * 2 + t + 1)
                            dve.scalar_tensor_tensor(rest[i % 2][:, t, :], ps[:, 2 * (i % 2) + t, 0:S2],
                                                     attn_cols[:, s, 2 + t:3 + t], parts[i % 2][:, t, 0, :],
                                                     ALU.add, ALU.subtract).then_inc(part_res, 1)
                        at_least(dve, kv_vst[i % 2], (b * (NKV // 2) + i // 2) * 16)
                        for k in range(2):
                            n_k = 2 - k
                            dve.wait_ge(kv_v, n * 2 + k + 1)
                            dve.tensor_tensor(vout[i % 2][:, 2 * k:2 * k + n_k, :, 0:DH],
                                              ps[0:KN, 4 + 2 * (i % 2) + k, 0:n_k * D].rearrange("p (c h e) -> p c h e", c=n_k, h=H),
                                              bv[0:KN, i, :].rearrange("p (h e) -> p h e", h=H).unsqueeze(1).broadcast_to([KN, n_k, H, DH]),
                                              ALU.add).then_inc(kv_vout, 1)
                        if i == 1 and (not isinstance(b, int) or b < B - 1):
                            split(b + 1, 1 - u, pair + u)

                step(0, 0, 0)
                step(1, 1, 0)
                with dve.Fori(1, B // 2 - 1) as i:
                    step(i * 2, 0, i)
                    step(i * 2 + 1, 1, i)
                step(B - 2, 0, B // 2 - 1)
                step(B - 1, 1, B // 2 - 1)

            def gpsimd(pool):
                def step(b, u, pair):
                    for i in range(NKV):
                        n = b * NKV + i
                        for t in range(DC):
                            pool.wait_ge(part_mid, n * 2 + t + 1)
                            pool.tensor_tensor(parts[i % 2][:, t, 2, :], rest[i % 2][:, t, :], parts[i % 2][:, t, 1, :],
                                               ALU.subtract).then_inc(part_lo, 1)

                batches(pool, step)

            stage(sync, gpsimd, scalar, vector, tensor)

        context_stage()

        ln_stat, ln_step, ln_ready = sem("ln_stat"), sem("ln_step"), sem("ln_ready")
        ln_normed, ln_scaled, ln_turned, ln_kept, ln_stored = (sem("ln_normed"), sem("ln_scaled"), sem("ln_turned"),
                                                               sem("ln_kept"), sem("ln_stored"))
        ln_evac = sem("ln_evac")
        ln_count = {"call": 0, "gain": 0, "turn": 0, "store": 0}
        ln_end = {}

        def by_four(eng, step):
            for u in range(4):
                step(u, u)
            with eng.Fori(1, B // 4) as i:
                for u in range(4):
                    step(i * 4 + u, u)

        def norm_stage(src, eps, gain=None, keep=None, turn=True, add_gate=None):
            m, mg = ln_count["call"], ln_count["gain"]
            t0, s0 = ln_count["turn"] * B, ln_count["store"] * B
            stores = keep is not None or add_gate is not None
            ln_count["call"] += 1
            ln_count["gain"] += gain is not None
            ln_count["turn"] += turn
            ln_count["store"] += stores
            rows = ln_gain
            scaled = [ln_scale[:, r, :] for r in range(XN)]
            n0 = m * B
            meet = not turn
            ln_end.update(normed=n0 + B, turned=t0 + B, stored=ln_count["store"] * B)
            g0 = mg * B
            gain_ready = expect(2) if gain is not None else 0

            def sync(sp):
                if gain is not None:
                    for r in range(2):
                        sp.dma_start(rows[:, r, :], a["ln_rows"][gain + r].partition_broadcast(128)).then_inc(loaded, 16)
                    sp.wait_ge(loaded, gain_ready)

            def vector(dve):
                with dve.Fori(0, B // 4) as i:
                    for u in range(4):
                        dve.bn_stats(ln_raw[:, i * 4 + u, :], src[:, i * 4 + u, :]).then_inc(ln_stat, 1)
                dve.wait_ge(ln_stat, n0 + B)
                k = 6 * m
                dve.tensor_tensor(ln_tmp[:, 0, :], ln_raw[:, :, 1], ln_raw[:, :, 4], ALU.add).then_inc(ln_step, 1)
                dve.tensor_tensor(ln_tmp[:, 1, :], ln_raw[:, :, 1], ln_raw[:, :, 4], ALU.subtract).then_inc(ln_step, 1)
                dve.tensor_tensor(ln_tmp[:, 2, :], ln_raw[:, :, 2], ln_raw[:, :, 5], ALU.add).then_inc(ln_step, 1)
                dve.wait_ge(ln_step, k + 3)
                dve.tensor_scalar(ln_mean[:, :], ln_tmp[:, 0, :], 0.5, None, ALU.mult).then_inc(ln_step, 1)
                dve.scalar_tensor_tensor(ln_tmp[:, 3, :], ln_tmp[:, 1, :], 0.25, ln_tmp[:, 1, :], ALU.mult, ALU.mult).then_inc(ln_step, 1)
                dve.wait_ge(ln_step, k + 5)
                dve.scalar_tensor_tensor(ln_tmp[:, 4, :], ln_tmp[:, 2, :], 1.0 / D, ln_tmp[:, 3, :], ALU.mult, ALU.add).then_inc(ln_step, 1)
                dve.wait_ge(ln_ready, 2 * (m + 1))
                if gain is not None:
                    dve.wait_ge(loaded, gain_ready)

                def step(b, u):
                    n = n0 + b
                    if turn:
                        at_least(dve, ln_turned, t0 + b - XN + 1)
                    if stores:
                        at_least(dve, ln_stored, s0 + b - XN + 1)
                    if gain is not None:
                        at_least(dve, ln_kept, g0 + b - XN + 1)
                    dve.tensor_scalar(xn2[u][:, :] if gain is None else scaled[u], src[:, b, :], ln_mean[:, bass.ds(b, 1)],
                                      ln_rstd[:, bass.ds(b, 1)], ALU.subtract, ALU.mult).then_inc(ln_normed, 1)
                    if gain is not None and u > 0:
                        shift(b - 1, u - 1)
                    if gain is not None and u == XN - 1:
                        shift(b, u)

                def shift(b, u):
                    dve.wait_ge(ln_scaled, g0 + b + 1)
                    dve.tensor_tensor(xn2[u][:, :], scaled[u], rows[0:T, 1, :], ALU.add).then_inc(ln_kept, 1)
                    if add_gate is not None:
                        dve.wait_ge(ln_kept, g0 + b + 1)
                        dve.scalar_tensor_tensor(x[:, b, :], xn2[u][:, :], gates[0:T, add_gate:add_gate + 1], x[:, b, :],
                                                 ALU.mult, ALU.add).then_inc(ln_stored, 1)

                by_four(dve, step)

            def gpsimd(pool):
                pool.wait_ge(ln_step, 6 * (m + 1))
                pool.tensor_scalar(ln_tmp[:, 0, :], ln_tmp[:, 4, :], eps, None, ALU.add).then_inc(ln_ready, 1)
                pool.wait_ge(ln_ready, 2 * m + 1)
                pool.tensor_tensor(ln_rstd[:, :], ln_tmp[:, 0, :], half[:, :], ALU.pow).then_inc(ln_ready, 1)
                if gain is not None:
                    pool.wait_ge(loaded, gain_ready)

                def step(b, u):
                    pool.wait_ge(ln_normed, n0 + b + 1)
                    pool.tensor_tensor(scaled[u], scaled[u], rows[0:T, 0, :], ALU.mult).then_inc(ln_scaled, 1)

                if gain is not None:
                    by_four(pool, step)

            def tensor(pe):
                def step(b, u):
                    n = n0 + b
                    if gain is None:
                        pe.wait_ge(ln_normed, n + 1)
                    else:
                        pe.wait_ge(ln_kept, g0 + b + 1)
                    at_least(pe, ln_evac, t0 + b - XN + 1)
                    for c in range(DC):
                        mm = pe.transpose(ps[:, u, c * T:(c + 1) * T], xn2[u][:, c * 128:(c + 1) * 128], ident[0:T, 0:T])
                    mm.then_inc(ln_turned, 1)

                by_four(pe, step)

            def scalar(act):
                def step(b, u):
                    if keep is not None:
                        if gain is None:
                            act.wait_ge(ln_normed, n0 + b + 1)
                        else:
                            act.wait_ge(ln_kept, g0 + b + 1)
                        act.activation(keep[:, b, :], xn2[u][:, :], ACT.Copy).then_inc(ln_stored, 1)
                    act.wait_ge(ln_turned, t0 + b + 1)
                    act.activation(xn_t[:, :, bass.ds(b * T, T)], ps[:, u, 0:DC * T].rearrange("p (c t) -> p c t", c=DC),
                                   ACT.Copy).then_inc(ln_evac, 1)

                by_four(act, step)

            stage(sync, gpsimd, scalar if turn else None, vector, tensor if turn else None, meet=meet)


        q_stored = sem("q_stored")
        q_count = {"tile": B * len(KV_SET) * DC, "store": 0}

        def query_stage(s, kinds, dest, gate, keys_of=None):
            arena.clear()
            wlow.clear()
            w = wlow.take(128, 4, DC, D)
            TILES = DC * kinds
            parts = arena.take(128, G, TILES, PARTS, GT, dtype=BF16)
            rest = arena.take(128, G, TILES, GT)
            add_bias = bias(dest, gate, attn_rows[0:T, 1, :])
            weights_ready = expect(3)
            q0, st0 = q_count["tile"], q_count["store"]
            turned = ln_end["turned"] - B
            q_count["tile"] += G * TILES
            q_count["store"] += G * TILES

            def sync(sp):
                sp.dma_start(w, a["attn_w"][s]).then_inc(loaded, 16)
                for r in range(2):
                    sp.dma_start(attn_rows[:, r, :], a["attn_rows"][s, r].partition_broadcast(128)).then_inc(loaded, 16)
                if keys_of is not None:
                    fetch_keys(sp, keys_of)
                with sp.Fori(0, G) as g:
                    for j in range(TILES):
                        sp.wait_ge(part_lo, q0 + g * TILES + j + 1)
                        sp.dma_start(query_parts[j // DC, :, (j % DC) * 128:(j % DC + 1) * 128, bass.ds(g * GT, GT)].rearrange("q p n -> p q n"),
                                     parts[:, bass.ds(g, 1), j, :, :].rearrange("p g q n -> p (g q) n")).then_inc(q_stored, 16)
                sp.wait_ge(q_stored, 16 * (st0 + G * TILES))

            def groups(eng, step):
                step(0)
                with eng.Fori(1, G) as g:
                    step(g)

            def tensor(pe):
                pe.wait_ge(loaded, weights_ready)

                def step(g):
                    pe.wait_ge(ln_evac, turned + (g + 1) * GB)
                    for j in range(TILES):
                        at_least(pe, part_res, q0 + g * TILES + j - 1)
                        for c in range(DC):
                            mm = pe.matmul(ps[:, XN + j % 2, 0:GT], w[:, j // DC, c, (j % DC) * 128:(j % DC + 1) * 128],
                                           xn_t[:, c, bass.ds(g * GT, GT)], start=(c == 0), stop=(c == DC - 1))
                        mm.then_inc(part_made, 1)

                groups(pe, step)

            def part(g, j, q):
                return parts[:, bass.ds(g, 1), j, q, :].rearrange("p g n -> p (g n)")

            def the_rest(g, j):
                return rest[:, bass.ds(g, 1), j, :].rearrange("p g n -> p (g n)")

            def scalar(act):
                def step(g):
                    for j in range(TILES):
                        act.wait_ge(part_made, q0 + g * TILES + j + 1)
                        act.activation(part(g, j, 0), ps[:, XN + j % 2, 0:GT], ACT.Identity, bias=attn_cols[:, s, j:j + 1]).then_inc(part_hi, 1)
                        if j > 0:
                            middle(act, g, j - 1)
                    middle(act, g, TILES - 1)

                def middle(act, g, j):
                    act.wait_ge(part_res, q0 + g * TILES + j + 1)
                    act.activation(part(g, j, 1), the_rest(g, j), ACT.Copy).then_inc(part_mid, 1)

                groups(act, step)

            def vector(dve):
                dve.wait_ge(loaded, weights_ready)

                def step(g):
                    for j in range(TILES):
                        dve.wait_ge(part_hi, q0 + g * TILES + j + 1)
                        dve.scalar_tensor_tensor(the_rest(g, j), ps[:, XN + j % 2, 0:GT], attn_cols[:, s, j:j + 1], part(g, j, 0),
                                                 ALU.add, ALU.subtract).then_inc(part_res, 1)

                groups(dve, step)
                add_bias(dve)

            def gpsimd(pool):
                def step(g):
                    for j in range(TILES):
                        pool.wait_ge(part_mid, q0 + g * TILES + j + 1)
                        pool.tensor_tensor(part(g, j, 2), the_rest(g, j), part(g, j, 1), ALU.subtract).then_inc(part_lo, 1)

                groups(pool, step)

            stage(sync, gpsimd, scalar, vector, tensor)
            return w

        bias_scaled, bias_added = sem("bias_scaled"), sem("bias_added")
        bias_count = [0]

        def bias(dest, gate, row):
            k = bias_count[0]
            bias_count[0] += 1
            scaled = arena.take(T, D)
            normed, stored = ln_end["normed"], ln_end["stored"]

            def add(dve):
                dve.tensor_scalar(scaled, row, gate, None, ALU.mult).then_inc(bias_scaled, 1)
                dve.wait_ge(bias_scaled, k + 1)
                dve.wait_ge(ln_normed, normed)
                at_least(dve, ln_stored, stored)
                for q in range(2):
                    dve.tensor_tensor(dest[:, q * 8:q * 8 + 8, :], dest[:, q * 8:q * 8 + 8, :],
                                      scaled.unsqueeze(1).broadcast_to([T, 8, D]), ALU.add).then_inc(bias_added, 1)

            return add

        def bias_done():
            return 2 * bias_count[0]

        o_copied = sem("o_copied")
        o_turned = sem("o_turned")
        o_recip, o_normed = sem("o_recip"), sem("o_normed")
        o_turned2, o_copied2 = sem("o_turned2"), sem("o_copied2")
        o_made, o_added = sem("o_made"), sem("o_added")
        MISC, SUMS = 7, 6

        class Output:

            def __init__(self, w, dest, gate):
                self.w, self.dest, self.gate = w, dest, gate
                self.sums = [arena.take(128, 4, T) for _ in range(2)]
                self.normed = [arena.take(T, D) for _ in range(2)]
                self.turned = [arena.take(128, DC, T) for _ in range(2)]
                self.recip = arena.take(T, H)
            def turn_back(self, pe, n, r):
                at_least(pe, o_added, n)
                pe.wait_ge(o_copied, n + 1)
                for j in range(4):
                    mm = pe.transpose(ps[0:T, MISC, j * 128:(j + 1) * 128], self.sums[r][:, j, :], ident[:, :])
                mm.then_inc(o_turned, 1)

            def turn(self, pe, n, r):
                pe.wait_ge(o_normed, n + 1)
                for c in range(DC):
                    mm = pe.transpose(ps[:, MISC, c * T:(c + 1) * T], self.normed[r][:, c * 128:(c + 1) * 128], ident[0:T, 0:T])
                mm.then_inc(o_turned2, 1)

            def project(self, pe, n, r):
                pe.wait_ge(o_copied2, n + 1)
                for c in range(DC):
                    mm = pe.matmul(ps[0:T, MISC, 0:D], self.turned[r][:, c, :], self.w[:, 3, c, :], start=(c == 0), stop=(c == DC - 1))
                mm.then_inc(o_made, 1)

            def copy_turned(self, act, n, r):
                act.wait_ge(o_turned2, n + 1)
                act.activation(self.turned[r], ps[:, MISC, 0:DC * T].rearrange("p (c t) -> p c t", c=DC), ACT.Copy).then_inc(o_copied2, 1)

            def copy_sums(self, act, n, r):
                act.activation(self.sums[r], ps[:, SUMS, 0:4 * T].rearrange("p (j t) -> p j t", j=4), ACT.Copy).then_inc(o_copied, 1)

            def normalise(self, dve, n, r):
                back = ps[0:T, MISC, :].rearrange("p (h w) -> p h w", w=32)
                dve.wait_ge(o_turned, n + 1)
                dve.reciprocal(self.recip, back[:, :, DH]).then_inc(o_recip, 1)
                dve.wait_ge(o_recip, n + 1)
                dve.tensor_tensor(self.normed[r].rearrange("p (h e) -> p h e", h=H), back[:, :, 0:DH],
                                  self.recip.unsqueeze(2).broadcast_to([T, H, DH]), ALU.mult).then_inc(o_normed, 1)

            def add(self, dve, n, b):
                dve.wait_ge(o_made, n + 1)
                dve.scalar_tensor_tensor(self.dest[:, b, :], ps[0:T, MISC, 0:D], self.gate, self.dest[:, b, :],
                                         ALU.mult, ALU.add).then_inc(o_added, 1)

        RING = 4
        at_loaded = [sem(f"at_loaded{r}") for r in range(RING)]
        at_maxrow = [sem(f"at_maxrow{r}") for r in range(RING)]
        at_pair, at_max = sem("at_pair"), sem("at_max")
        at_clamped, at_mturn, at_mhi, at_mmid = sem("at_clamped"), sem("at_mturn"), sem("at_mhi"), sem("at_mmid")
        at_scores, at_probs, at_pv = sem("at_scores"), sem("at_probs"), sem("at_pv")
        at_mask, at_pen0, at_pen = [sem(f"at_mask{r}") for r in range(RING)], sem("at_pen0"), sem("at_pen")
        at_count = {"call": 0, "mask": 0}
        out_count = [0]
        STEPS, PAIRS = 12, H // 2
        PAIR_AT = {0: 0, 2: 1, 3: 2, 5: 3, 6: 4, 8: 5, 9: 6, 11: 7}

        def load_keys(sp, keys, kv, b, r, j):
            sp.dma_start(keys[DH * j:DH * j + DH, :, :],
                         key_parts[kv, b, K_PART[j], :, :].rearrange("(h d) k -> d h k", d=DH)).then_inc(at_loaded[r], 16)

        def low_rings():
            wreg.clear()
            keys = [wreg.take(AROWS, H, S2, dtype=BF16) for _ in range(RING - 1)]
            return keys, [wreg.take(AROWS, H, T, dtype=BF16) for _ in range(RING - 1)]

        def fetch_keys(sp, kv):
            keys, _ = low_rings()
            for b in range(RING - 1):
                for j in range(len(K_PART)):
                    load_keys(sp, keys[b], kv, b, b, j)

        def cross_stage(kv, w, scale, dest, gate, masked=False):
            arena.clear()
            call = at_count["call"]
            n0, o0, p0 = call * B, out_count[0] * B, at_count["mask"] * B
            turn0 = call * (B // RING)
            ones_made = expect_made(RING)
            at_count["call"] += 1
            at_count["mask"] += masked
            out_count[0] += 1
            keys, queries = low_rings()
            keys.append(arena.take(AROWS, H, S2, dtype=BF16))
            queries.append(arena.take(AROWS, H, T, dtype=BF16))
            vals = [arena.take(KN, KC, H, VW) for _ in range(RING)]
            probs = [arena.take(KN, GT) for _ in range(3)]
            out = Output(w, dest, gate)
            negmax = [arena.take(T, H) for _ in range(2)]
            negmax_c = [arena.take(T, H) for _ in range(2)]
            maxrow = [arena.take(H, 2, T, dtype=BF16) for _ in range(2)]
            if masked:
                mask_in = [arena.take(T, S2, dtype=I32) for _ in range(RING)]
                pad_in = [arena.take(T, S2, dtype=I32) for _ in range(RING)]
                pen = [arena.take(T, S2, dtype=BF16) for _ in range(RING)]

            def schedule(eng, step):
                def static(b):
                    step(b, lambda d: (b + d) % RING, lambda d: turn0 + (b + d) // RING)

                static(0)
                with eng.Fori(0, 3) as i:
                    for q in range(1, RING + 1):
                        step(i * RING + q, lambda d, q=q: (q + d) % RING, lambda d, q=q: i + (turn0 + (q + d) // RING))
                for b in range(13, B):
                    static(b)

            def has(b, d):
                return not isinstance(b, int) or 0 <= b + d < B

            LOADS = 2 * len(K_PART) + 1

            def sync(sp):
                def load(b, r, which, fetched=False):
                    if masked and 0 in which:
                        sp.dma_start(mask_in[r], a["mask"][b]).then_inc(at_mask[r], 16)
                        sp.dma_start(pad_in[r], a["pad"][b].partition_broadcast(T)).then_inc(at_mask[r], 16)
                    for j in which:
                        if not fetched:
                            load_keys(sp, keys[r], kv, b, r, j)
                        sp.dma_start(queries[r][DH * j:DH * j + DH, :, :],
                                     query_parts[0, Q_PART[j], :, bass.ds(b * T, T)].rearrange("(h d) k -> d h k", d=DH)).then_inc(at_loaded[r], 16)

                def load_values(b, r):
                    sp.dma_start(vals[r].rearrange("p c h w -> p (c h w)"), values[kv, b]).then_inc(at_loaded[r], 16)

                def rows(b, r):
                    sp.wait_ge(at_mmid, n0 + b + 1)
                    for q in range(2):
                        sp.dma_start(queries[r][SROWS + q:SROWS + q + 1, :, :], maxrow[r % 2][:, q, :]).then_inc(at_maxrow[r], 16)

                for b in range(RING - 1):
                    load(b, b, range(len(K_PART)), fetched=True)
                    load_values(b, b)
                rows(0, 0)

                def step(b, place, turn):
                    if has(b, 3):
                        at_least(sp, at_scores, (n0 + b) * STEPS if has(b, -1) else 0)
                        load(b + 3, place(3), range(0, 3))
                    if has(b, 1):
                        rows(b + 1, place(1))
                    if has(b, 3):
                        load(b + 3, place(3), range(3, len(K_PART)))
                        at_least(sp, at_pv, (n0 + b) * STEPS if has(b, -1) else 0)
                        load_values(b + 3, place(3))

                schedule(sp, step)

            def gpsimd(pool):
                for r in range(2):
                    pool.memset(keys[r][SROWS:AROWS, :, :], 1.0).then_inc(const_made, 1)

            def tensor(pe):
                def pair(b, r, p):
                    k = (n0 + b) * PAIRS + p
                    at_least(pe, at_max, k - 1)
                    for e in range(2):
                        hd = 2 * p + e
                        mm = pe.matmul(ps[0:T, 2 * (p % 2) + e, 0:S2], queries[r][0:SROWS, hd, :], keys[r][0:SROWS, hd, :],
                                       start=True, stop=not masked)
                        if masked:
                            mm = pe.matmul(ps[0:T, 2 * (p % 2) + e, 0:S2], neg16[:, 0, :], pen[r], start=False, stop=True)
                    mm.then_inc(at_pair, 1)

                def maxima(b, r):
                    pe.wait_ge(at_clamped, n0 + b + 1)
                    pe.transpose(ps[0:H, MISC, 0:T], negmax_c[r % 2], ident[0:T, 0:T]).then_inc(at_mturn, 1)

                def scores(b, r, k):
                    m = (n0 + b) * STEPS + k
                    at_least(pe, at_probs, m - 1)
                    bank, c = 4 + k % 2, k % KC
                    if masked:
                        pe.matmul(ps[0:KN, bank, 0:GT], pen[r][:, c * KN:(c + 1) * KN], neg16[:, :, :], start=True, stop=False)
                    for g in range(4):
                        hd = 4 * (k // KC) + g
                        mm = pe.matmul(ps[0:KN, bank, g * T:(g + 1) * T], keys[r][:, hd, c * KN:(c + 1) * KN], queries[r][:, hd, :],
                                       start=not masked, stop=not masked or g == 3)
                    mm.then_inc(at_scores, 1)

                def weigh(b, r, k):
                    m = (n0 + b) * STEPS + k
                    pe.wait_ge(at_probs, m + 1)
                    j, c = k // KC, k % KC
                    for g in range(4):
                        mm = pe.matmul(ps[32 * g:32 * g + VW, SUMS, j * T:(j + 1) * T], vals[r][:, c, 4 * j + g, :],
                                       probs[k % 3][:, g * T:(g + 1) * T], start=(c == 0), stop=(c == KC - 1))
                    mm.then_inc(at_pv, 1)

                def arrived(b, r, turn):
                    pe.wait_ge(at_loaded[r], (turn + 1) * (16 * LOADS))
                    if masked:
                        pe.wait_ge(at_pen, p0 + b + 1)

                for b in range(2):
                    arrived(b, b, turn0)
                    for p in range(PAIRS):
                        pair(b, b, p)
                    if b == 0:
                        maxima(0, 0)

                def step(b, place, turn):
                    here, prev = place(0), place(-1)
                    last = o0 + b - 1
                    pe.wait_ge(at_maxrow[here], (turn(0) + 1) * 32)
                    for k in range(STEPS):
                        scores(b, here, k)
                        if k >= 2:
                            if k == 2:
                                at_least(pe, o_copied, o0 + b)
                            weigh(b, here, k - 2)
                        elif has(b, -1):
                            weigh(b - 1, prev, STEPS - 2 + k)
                        if k in PAIR_AT and has(b, 2):
                            if k == 0:
                                arrived(b + 2, place(2), turn(2))
                            pair(b + 2, place(2), PAIR_AT[k])
                        if k == 1 and has(b, 1):
                            at_least(pe, o_added, last if has(b, -1) else o0)
                            maxima(b + 1, place(1))
                        if has(b, -1):
                            if k == 4:
                                at_least(pe, at_mmid, n0 + b + 2 if has(b, 1) else n0 + b + 1)
                                out.turn_back(pe, last, prev % 2)
                            if k == 6:
                                out.turn(pe, last, prev % 2)
                            if k == 8:
                                out.project(pe, last, prev % 2)

                pe.wait_ge(const_made, ones_made)
                schedule(pe, step)
                for k in range(STEPS - 2, STEPS):
                    weigh(B - 1, (B - 1) % RING, k)
                last = o0 + B - 1
                out.turn_back(pe, last, (B - 1) % 2)
                out.turn(pe, last, (B - 1) % 2)
                out.project(pe, last, (B - 1) % 2)

            def scalar(act):
                act.activation(idle[:, :], one[:, :], ACT.Exp)

                for r in range(2, RING):
                    act.activation(keys[r][SROWS:AROWS, :, :], one[SROWS:AROWS, :].unsqueeze(2).broadcast_to([2, H, S2]), ACT.Copy).then_inc(const_made, 1)

                def sums(b, r):
                    act.wait_ge(at_pv, (n0 + b + 1) * STEPS)
                    out.copy_sums(act, o0 + b, r % 2)

                def step(b, place, turn):
                    for k in range(STEPS):
                        m = (n0 + b) * STEPS + k
                        at_least(act, at_pv, m - 2)
                        act.wait_ge(at_scores, m + 1)
                        act.activation(probs[k % 3], ps[0:KN, 4 + k % 2, 0:GT], ACT.Exp, scale=scale).then_inc(at_probs, 1)
                        if k == 1 and has(b, -1):
                            sums(b - 1, place(-1))
                        if k == 7 and has(b, -1):
                            out.copy_turned(act, o0 + b - 1, place(-1) % 2)

                schedule(act, step)
                sums(B - 1, (B - 1) % RING)
                out.copy_turned(act, o0 + B - 1, (B - 1) % 2)

            def vector(dve):
                dve.memset(ps[:, SUMS, :], 0.0)

                def reduce_pair(b, r, p):
                    k = (n0 + b) * PAIRS + p
                    dve.wait_ge(at_pair, k + 1)
                    dve.tensor_reduce(negmax[r % 2][:, 2 * p:2 * p + 2], ps[0:T, 2 * (p % 2):2 * (p % 2) + 2, 0:S2], AX.X, ALU.max,
                                      negate=True).then_inc(at_max, 1)

                def clamp(b, r):
                    dve.wait_ge(at_max, (n0 + b + 1) * PAIRS)
                    dve.tensor_scalar(negmax_c[r % 2], negmax[r % 2], 0.1 * -NEG, None, ALU.min).then_inc(at_clamped, 1)

                def split_rows(b, r):
                    n = n0 + b
                    dve.wait_ge(at_mturn, n + 1)
                    at_least(dve, at_scores, (n - 1) * STEPS)
                    dve.tensor_copy(maxrow[r % 2][:, 0, :], ps[0:H, MISC, 0:T]).then_inc(at_mhi, 1)
                    dve.wait_ge(at_mhi, n + 1)
                    dve.tensor_tensor(maxrow[r % 2][:, 1, :], ps[0:H, MISC, 0:T], maxrow[r % 2][:, 0, :], ALU.subtract).then_inc(at_mmid, 1)

                def penalty(b, r, turn):
                    dve.wait_ge(at_mask[r], (turn - turn0 + 1) * 32)
                    at_least(dve, at_pv, (n0 + b - 3) * STEPS)
                    dve.tensor_scalar(mask_in[r].bitcast(F32), mask_in[r], 0, None, ALU.is_equal).then_inc(at_pen0, 1)
                    dve.wait_ge(at_pen0, p0 + b + 1)
                    dve.scalar_tensor_tensor(pen[r], pad_in[r], 0, mask_in[r].bitcast(F32), ALU.is_equal, ALU.add).then_inc(at_pen, 1)

                if masked:
                    for b in range(RING - 1):
                        penalty(b, b, turn0)
                for p in range(PAIRS):
                    reduce_pair(0, 0, p)
                clamp(0, 0)
                split_rows(0, 0)
                for p in range(PAIRS):
                    reduce_pair(1, 1, p)

                def step(b, place, turn):
                    last, prev = o0 + b - 1, place(-1)
                    if has(b, 1):
                        clamp(b + 1, place(1))
                    for p in range(PAIRS):
                        if has(b, 2):
                            reduce_pair(b + 2, place(2), p)
                        if p == 0 and has(b, 1):
                            split_rows(b + 1, place(1))
                        if p == 2 and has(b, -1):
                            out.normalise(dve, last, prev % 2)
                        if p == 5 and has(b, -1):
                            out.add(dve, last, b - 1)
                    if masked and has(b, 3):
                        penalty(b + 3, place(3), turn(3))

                schedule(dve, step)
                out.normalise(dve, o0 + B - 1, (B - 1) % 2)
                out.add(dve, o0 + B - 1, B - 1)

            stage(sync, gpsimd, scalar, vector, tensor)

        se_inv = sem("se_inv")
        se_loaded = [sem("se_loaded0"), sem("se_loaded1")]
        se_group, se_v, se_vout = sem("se_group"), sem("se_v"), sem("se_vout")
        se_scores, se_masked, se_max, se_shifted = sem("se_scores"), sem("se_masked"), sem("se_max"), sem("se_shifted")
        se_probs, se_pturn, se_pcopied, se_pv = sem("se_probs"), sem("se_pturn"), sem("se_pcopied"), sem("se_pv")

        def self_stage(s, w, scale, dest, gate):
            arena.clear()
            wreg.clear()
            masks_ready = expect(2)
            ones_made = expect_made(3)
            o0 = out_count[0] * B
            out_count[0] += 1
            keys = [wreg.take(SROWS, H, T, dtype=BF16) for _ in range(2)]
            queries = [wreg.take(SROWS, H, T, dtype=BF16) for _ in range(2)]
            group_t = wreg.take(128, DC, GT)
            am = wreg.take(T, T)
            pm = arena.take(T, B, T)
            out = Output(w, dest, gate)
            vals = [arena.take(T, H, VW) for _ in range(2)]
            masked = [arena.take(T, 4, T) for _ in range(4)]
            probs = [arena.take(T, 4, T) for _ in range(2)]
            probs_t = [arena.take(T, 4, T) for _ in range(2)]
            negmax = arena.take(T, H)
            LOADS = 2 * len(K_PART)
            Q4 = 4

            def sync(sp):
                sp.dma_start(am, a["am"][0, 0]).then_inc(loaded, 16)
                sp.dma_start(pm, a["pm"].rearrange("b o u k -> (o u) b k").squeeze(0).partition_broadcast(T)).then_inc(loaded, 16)

                def load(b, u):
                    for j in range(len(K_PART)):
                        for kind, dst, part in ((1, keys, K_PART[j]), (0, queries, Q_PART[j])):
                            sp.dma_start(dst[u][DH * j:DH * j + DH, :, :],
                                         query_parts[kind, part, :, bass.ds(b * T, T)].rearrange("(h d) k -> d h k", d=DH)).then_inc(se_loaded[u], 16)

                load(0, 0)
                load(1, 1)
                with sp.Fori(1, B // 2) as i:
                    for u in range(2):
                        sp.wait_ge(se_scores, (i * 2 + u - 1) * 4)
                        load(i * 2 + u, u)
                sp.wait_ge(loaded, masks_ready)

            def gpsimd(pool):
                pool.wait_ge(loaded, masks_ready)
                pool.tensor_tensor(pm, pm, am.unsqueeze(1).broadcast_to([T, B, T]), ALU.mult).then_inc(se_inv, 1)
                pool.wait_ge(se_inv, 1)
                pool.tensor_scalar(pm, pm, -1.0, 1.0, ALU.mult, ALU.add).then_inc(se_inv, 1)
                pool.wait_ge(se_inv, 2)
                pool.tensor_scalar(pm, pm, -1.0e9, None, ALU.mult).then_inc(se_inv, 1)

            def tensor(pe):
                def scores(b, u, k):
                    m = b * 4 + k
                    at_least(pe, se_masked, m - 1)
                    for g in range(Q4):
                        hd = 4 * k + g
                        mm = pe.matmul(ps[0:T, k % 2, g * T:(g + 1) * T], queries[u][:, hd, :], keys[u][:, hd, :], start=True, stop=True)
                    mm.then_inc(se_scores, 1)

                def turn(b, k):
                    m = b * 4 + k
                    pe.wait_ge(se_probs, m + 1)
                    at_least(pe, se_pcopied, m - 1)
                    for g in range(Q4):
                        mm = pe.transpose(ps[0:T, 2 + k % 2, g * T:(g + 1) * T], probs[k % 2][:, g, :], ident[0:T, 0:T])
                    mm.then_inc(se_pturn, 1)

                def weigh(b, u, k):
                    m = b * 4 + k
                    pe.wait_ge(se_pcopied, m + 1)
                    if k == 0:
                        pe.wait_ge(se_vout, b + 1)
                        at_least(pe, o_copied, o0 + b)
                    for g in range(Q4):
                        mm = pe.matmul(ps[32 * g:32 * g + VW, SUMS, k * T:(k + 1) * T], vals[u][:, 4 * k + g, :],
                                       probs_t[k % 2][:, g, :], start=True, stop=True)
                    mm.then_inc(se_pv, 1)

                pe.wait_ge(const_made, ones_made)
                pe.wait_ge(se_loaded[0], 16 * LOADS)
                for k in range(2):
                    scores(0, 0, k)

                def step(g):
                    for q in range(GB):
                        u, b = q % 2, g * GB + q
                        last = o0 + b - 1
                        for k in range(4):
                            if k == 0:
                                if q == 0:
                                    pe.wait_ge(se_group, g + 1)
                                for c in range(DC):
                                    mm = pe.matmul(ps[0:T, 4, 0:D], group_t[:, c, q * T:(q + 1) * T], w[:, 2, c, :], start=(c == 0), stop=(c == DC - 1))
                                mm.then_inc(se_v, 1)
                            if k < 2:
                                scores(b, u, k + 2)
                            elif has(b, 1):
                                if k == 2:
                                    pe.wait_ge(se_loaded[1 - u], (g * 2 + (q + 1) // 2 + 1) * (16 * LOADS))
                                scores(b + 1, 1 - u, k - 2)
                            if k == 0 and has(b, -2):
                                out.turn(pe, last - 1, u)
                            if k == 1 and has(b, -2):
                                out.project(pe, last - 1, u)
                            if k == 2 and has(b, -1):
                                out.turn_back(pe, last, 1 - u)
                            turn(b, k)
                            if k > 0:
                                weigh(b, u, k - 1)
                            elif has(b, -1):
                                weigh(b - 1, 1 - u, 3)

                over_groups(pe, step)
                out.turn(pe, o0 + B - 2, 0)
                out.project(pe, o0 + B - 2, 0)
                weigh(B - 1, 1, 3)
                out.turn_back(pe, o0 + B - 1, 1)
                out.turn(pe, o0 + B - 1, 1)
                out.project(pe, o0 + B - 1, 1)

            def scalar(act):
                act.activation(idle[:, :], one[:, :], ACT.Exp)

                def sums(b, u):
                    act.wait_ge(se_pv, b * 4 + 4)
                    out.copy_sums(act, o0 + b, u)

                def copy(b, k):
                    m = b * 4 + k
                    act.wait_ge(se_pturn, m + 1)
                    at_least(act, se_pv, m - 1)
                    act.activation(probs_t[k % 2], ps[0:T, 2 + k % 2, 0:GT].rearrange("p (g t) -> p g t", g=4), ACT.Copy).then_inc(se_pcopied, 1)

                def step(g):
                    for q in range(GB):
                        u, b = q % 2, g * GB + q
                        for k in range(4):
                            m = b * 4 + k
                            act.wait_ge(se_shifted, m + 1)
                            at_least(act, se_pturn, m - 1)
                            act.activation(probs[k % 2], masked[k], ACT.Exp).then_inc(se_probs, 1)
                            if k > 0:
                                copy(b, k - 1)
                            elif has(b, -1):
                                copy(b - 1, 3)
                            if k == 1 and has(b, -1):
                                sums(b - 1, 1 - u)
                            if k == 0 and has(b, -2):
                                out.copy_turned(act, o0 + b - 2, u)

                over_groups(act, step)
                out.copy_turned(act, o0 + B - 2, 0)
                copy(B - 1, 3)
                sums(B - 1, 1)
                out.copy_turned(act, o0 + B - 1, 1)

            def has(b, d):
                return not isinstance(b, int) or 0 <= b + d < B

            def over_groups(eng, step):
                step(0)
                with eng.Fori(1, G - 1) as g:
                    step(g)
                step(G - 1)

            def vector(dve):
                dve.memset(ps[:, SUMS, :], 0.0).then_inc(const_made, 1)
                for u in range(2):
                    dve.memset(vals[u], 1.0).then_inc(const_made, 1)
                dve.wait_ge(se_inv, 3)

                def step(g):
                    at_least(dve, se_v, g * GB)
                    dve.tensor_copy(group_t, xn_t[:, :, bass.ds(g * GT, GT)]).then_inc(se_group, 1)
                    for q in range(GB):
                        u, b = q % 2, g * GB + q
                        n = o0 + b
                        for k in range(4):
                            m = b * 4 + k
                            dve.wait_ge(se_masked, m + 1)
                            dve.tensor_reduce(negmax[:, 4 * k:4 * k + 4], masked[k], AX.X, ALU.max).then_inc(se_max, 1)
                            if k < 3:
                                mask(b, k + 1)
                            elif has(b, 1):
                                mask(b + 1, 0)
                            dve.wait_ge(se_max, m + 1)
                            dve.tensor_tensor(masked[k], masked[k], negmax[:, 4 * k:4 * k + 4].unsqueeze(2).broadcast_to([T, 4, T]),
                                              ALU.subtract).then_inc(se_shifted, 1)
                            if k == 1:
                                dve.wait_ge(se_v, b + 1)
                                at_least(dve, se_pv, (b - 1) * 4)
                                dve.tensor_tensor(vals[u][:, :, 0:DH], ps[0:T, 4, 0:D].rearrange("p (h e) -> p h e", h=H),
                                                  attn_rows[0:T, 0, :].rearrange("p (h e) -> p h e", h=H), ALU.add).then_inc(se_vout, 1)
                            if k == 2 and has(b, -2):
                                out.add(dve, n - 2, b - 2)
                            if k == 3 and has(b, -1):
                                out.normalise(dve, n - 1, 1 - u)

                def mask(b, k):
                    m = b * 4 + k
                    dve.wait_ge(se_scores, m + 1)
                    at_least(dve, se_probs, m - 3)
                    dve.scalar_tensor_tensor(masked[k], ps[0:T, k % 2, 0:GT].rearrange("p (g t) -> p g t", g=4), scale,
                                             pm[:, bass.ds(b, 1), :].broadcast_to([T, 4, T]), ALU.mult, ALU.add).then_inc(se_masked, 1)

                mask(0, 0)
                over_groups(dve, step)
                out.add(dve, o0 + B - 2, B - 2)
                out.normalise(dve, o0 + B - 1, 1)
                out.add(dve, o0 + B - 1, B - 1)

            stage(sync, gpsimd, scalar, vector, tensor)

        def groups(eng, step):
            step(0)
            with eng.Fori(1, G) as g:
                step(g)

        expert_w = [sem("expert_w0"), sem("expert_w1")]
        ffn_h, e0_gate, ffn_act, ffn_out, e0_kept = sem("ffn_h"), sem("e0_gate"), sem("ffn_act"), sem("ffn_out"), sem("e0_kept")
        e0_turned, ffn_added = sem("e0_turned"), sem("ffn_added")

        def position_experts_stage(gate):
            arena.clear()
            wreg.clear()
            TE = T // E
            turned = ln_end["turned"]
            NT = B * TE
            NF = len(F0_ROWS)
            w1 = [wreg.take(128, DC, F0) for _ in range(2)]
            w3 = [wreg.take(128, DC, F0) for _ in range(2)]
            w2 = [wreg.take(128, NF, D) for _ in range(2)]
            hid = [arena.take(128, NF, NT) for _ in range(2)]
            silu = [arena.take(128, NT) for _ in range(2)]
            out_t = arena.take(128, DC, B * T)
            stage_in = [arena.take(128, DC, NT) for _ in range(2)]
            rows = F0_ROWS

            def experts(eng, step):
                step(0, 0, 0)
                step(1, 1, 0)
                with eng.Fori(1, E // 2) as i:
                    step(i * 2, 0, i)
                    step(i * 2 + 1, 1, i)

            def sync(sp):
                def step(e, u, i):
                    at_least(sp, ffn_out, (e - 1) * DC)
                    sp.dma_start(w1[u], a["e0_w1"][e]).then_inc(expert_w[u], 16)
                    sp.dma_start(w3[u], a["e0_w3"][e]).then_inc(expert_w[u], 16)
                    sp.dma_start(w2[u][:, 0:4, :], a["e0_w2"][e]).then_inc(expert_w[u], 16)
                    sp.dma_start(w2[u][0:96, 4:6, :], a["e0_w2r"][e]).then_inc(expert_w[u], 16)

                experts(sp, step)
                for u in range(2):
                    sp.wait_ge(expert_w[u], 64 * E // 2)

            def tensor(pe):
                pe.wait_ge(ln_evac, turned)

                def step(e, u, i):
                    pe.wait_ge(expert_w[u], (i + 1) * 64)
                    for f in range(NF):
                        k = e * NF + f
                        at_least(pe, ffn_act, k - 1)
                        for q, w in ((0, w1[u]), (1, w3[u])):
                            for c in range(DC):
                                mm = pe.matmul(ps[0:rows[f], f % 2, q * NT:(q + 1) * NT], w[:, c, F0_AT[f]:F0_AT[f] + rows[f]],
                                               xn_t[:, c, :].rearrange("p (b t) -> p b t", t=T)[:, :, bass.ds(e * TE, TE)],
                                               start=(c == 0), stop=(c == DC - 1))
                        mm.then_inc(ffn_h, 1)
                    for c in range(DC):
                        at_least(pe, e0_kept, e * DC + c - 1)
                        for f in range(NF):
                            if c == 0:
                                pe.wait_ge(ffn_act, e * NF + f + 1)
                            mm = pe.matmul(ps[:, 2 + c, 0:NT], w2[u][0:rows[f], f, c * 128:(c + 1) * 128], hid[u][0:rows[f], f, :],
                                           start=(f == 0), stop=(f == NF - 1))
                        mm.then_inc(ffn_out, 1)

                experts(pe, step)
                for b in range(B):
                    at_least(pe, ffn_added, b - 1)
                    if b == 0:
                        pe.wait_ge(e0_kept, E * DC)
                    for c in range(DC):
                        mm = pe.transpose(ps[0:T, 4 + b % 2, c * 128:(c + 1) * 128], out_t[:, c, b * T:(b + 1) * T], ident[:, :])
                    mm.then_inc(e0_turned, 1)

            def scalar(act):
                act.activation(idle[:, :], one[:, :], ACT.Silu)

                def step(e, u, i):
                    for f in range(NF):
                        k = e * NF + f
                        act.wait_ge(ffn_h, k + 1)
                        at_least(act, ffn_act, k - 1)
                        act.activation(silu[f % 2][0:rows[f], :], ps[0:rows[f], f % 2, 0:NT], ACT.Silu).then_inc(e0_gate, 1)
                    for c in range(DC):
                        act.wait_ge(ffn_out, e * DC + c + 1)
                        act.activation(out_t[:, c, :].rearrange("p (b t) -> p b t", t=T)[:, :, bass.ds(e * TE, TE)],
                                       ps[:, 2 + c, 0:NT].rearrange("p (b t) -> p b t", t=TE), ACT.Copy).then_inc(e0_kept, 1)

                experts(act, step)

            def vector(dve):
                def step(e, u, i):
                    for f in range(NF):
                        k = e * NF + f
                        dve.wait_ge(e0_gate, k + 1)
                        if f == 0:
                            at_least(dve, ffn_out, (e - 1) * DC)
                        dve.tensor_tensor(hid[u][0:rows[f], f, :], silu[f % 2][0:rows[f], :], ps[0:rows[f], f % 2, NT:2 * NT],
                                          ALU.mult).then_inc(ffn_act, 1)

                experts(dve, step)
                for b in range(B):
                    dve.wait_ge(e0_turned, b + 1)
                    dve.scalar_tensor_tensor(x[:, b, :], ps[0:T, 4 + b % 2, 0:D], gates[0:T, gate:gate + 1], x[:, b, :],
                                             ALU.mult, ALU.add).then_inc(ffn_added, 1)

            stage(sync, None, scalar, vector, tensor)

        rt_logits, rt_step, rt_exp = sem("rt_logits"), sem("rt_step"), sem("rt_exp")
        rt_count = {"call": 0, "step": 0}

        class TopTwo:

            def __init__(self, router, bias=None):
                self.n = rt_count["call"]
                self.ranks_made = expect_made(E)
                rt_count["call"] += 1
                self.router, self.bias = router, bias
                self.turned = ln_end["turned"]
                self.logits, self.rank, self.equal = (arena.take(T, B, E) for _ in range(3))
                self.best, self.found, self.second, self.gap, self.grown = (arena.take(T, B) for _ in range(5))
                self.onehot = [arena.take(T, B, E) for _ in range(2)]
                self.weight = [arena.take(T, B) for _ in range(2)]
                self.steps = rt_count["step"]

            def make_ranks(self, pool):
                for e in range(E):
                    pool.memset(self.rank[:, :, e], float(E - e)).then_inc(const_made, 1)

            def logits_pe(self, pe):
                pe.wait_ge(ln_evac, self.turned)
                for b in range(B):
                    for c in range(DC):
                        mm = pe.matmul(ps[0:T, 0, b * E:(b + 1) * E], xn_t[:, c, b * T:(b + 1) * T], self.router[:, c, :],
                                       start=(c == 0), stop=(c == DC - 1))
                mm.then_inc(rt_logits, 1)

            def exp_act(self, act):
                act.wait_ge(rt_step, self.gap_step)
                act.activation(self.grown, self.gap, ACT.Exp).then_inc(rt_exp, 1)

            def plan(self):
                self.gap_step = self.steps + 14
                rt_count["step"] = self.steps + 17

            def choose(self, dve):
                def link(ins):
                    self.steps += 1
                    ins.then_inc(rt_step, 1)
                    dve.wait_ge(rt_step, self.steps)

                def over(v):
                    return v.unsqueeze(2).broadcast_to([T, B, E])

                dve.wait_ge(const_made, self.ranks_made)
                dve.wait_ge(rt_logits, self.n + 1)
                logits = ps[0:T, 0, 0:B * E].rearrange("p (b e) -> p b e", e=E)
                if self.bias is None:
                    link(dve.tensor_copy(self.logits, logits))
                else:
                    link(dve.tensor_tensor(self.logits, logits, self.bias.unsqueeze(1).broadcast_to([T, B, E]), ALU.add))
                for k, top in ((0, self.best), (1, self.second)):
                    link(dve.tensor_reduce(top, self.logits, AX.X, ALU.max))
                    link(dve.tensor_tensor(self.equal, self.logits, over(top), ALU.is_equal))
                    link(dve.tensor_tensor(self.equal, self.equal, self.rank, ALU.mult))
                    link(dve.tensor_reduce(self.found, self.equal, AX.X, ALU.max))
                    link(dve.tensor_tensor(self.onehot[k], self.equal, over(self.found), ALU.is_equal))
                    if k == 0:
                        link(dve.scalar_tensor_tensor(self.logits, self.onehot[0], NEG, self.logits, ALU.mult, ALU.add))
                    else:
                        link(dve.tensor_tensor(self.gap, self.second, self.best, ALU.subtract))
                link(dve.tensor_copy(self.found, self.gap))
                dve.wait_ge(rt_exp, self.n + 1)
                link(dve.tensor_scalar(self.found, self.grown, 1.0, None, ALU.add))
                link(dve.reciprocal(self.weight[0], self.found))
                link(dve.tensor_tensor(self.weight[1], self.grown, self.weight[0], ALU.mult))

        e1_mask, e1_maskt, e1_maskc = sem("e1_mask"), sem("e1_maskt"), sem("e1_maskc")
        e1_weights, e1_scaled, e1_both = sem("e1_weights"), sem("e1_scaled"), sem("e1_both")
        e1_low, e1_lowc, e1_lowm, e1_hid = sem("e1_low"), sem("e1_lowc"), sem("e1_lowm"), sem("e1_hid")
        e1_gate, e1_act, e1_z, e1_zm, e1_out, e1_added = (sem("e1_gate"), sem("e1_act"), sem("e1_z"), sem("e1_zm"),
                                                          sem("e1_out"), sem("e1_added"))

        def lora_experts_stage(gate):
            arena.clear()
            wreg.clear()
            wlow.clear()
            LORA_SCALE = 2.0
            w_r = [[lora_w_r[:, part, q] for q in range(2)] for part in range(2)]
            x_r = [lora_x_r[:, part] for part in range(2)]
            PRODUCTS = ((0, 0), (0, 1), (1, 0))
            wreg.take(128, 2 * 2 * DC * F + 2 * DC * GT)
            wd = wreg.take(128, FC, D)
            b2 = wreg.take(128, D)
            router = wreg.take(128, DC, E)
            a1, a2 = wlow.take(128, DC, ER), wlow.take(128, FC, ER)
            a3 = arena.take(128, DC, ER)
            b1, b3 = arena.take(128, F), arena.take(128, F)
            top = TopTwo(router)
            top.plan()
            MASKS = 4
            wide = [wlow.take(T, E, ER // E, dtype=BF16) for _ in range(MASKS)]
            weight_g = arena.take(128, 2, GT)
            wide_w = [wlow.take(T, 128) for _ in range(MASKS)]
            MASK_BANK = (2, 6)
            weight_t = arena.take(128, 2, B * T)
            mask_t = arena.take(128, 2, B * T, dtype=BF16)
            weight = arena.take(T, 2, B)
            low = arena.take(128, 2, GT)
            lowm = [[arena.take(128, GT) for _ in range(2)] for _ in range(2)]
            act_t = [arena.take(128, FC, GT) for _ in range(2)]
            w_raw = [t.rearrange("p f t -> p (f t)")[:, 0:DC * F].rearrange("p (c f) -> p c f", c=DC) for t in act_t]
            silu = [arena.take(128, GT) for _ in range(2)]
            scaled = [arena.take(128, GT) for _ in range(2)]
            zm = [arena.take(128, GT) for _ in range(3)]
            weights_ready = expect(10)
            order = [(0, 0)]
            for f in range(1, FC):
                order += [(f, 0), (f - 1, 1)]
            order.append((FC - 1, 1))
            when = {fk: n for n, fk in enumerate(order)}

            def sync(sp):
                for dst, name in ((router, "e1_router"), (a1, "e1_a1"), (a3, "e1_a3"), (w_raw[0], "e1_gate"), (w_raw[1], "e1_up"), (b1, "e1_b1"),
                                  (b3, "e1_b3"), (wd, "e1_down"), (a2, "e1_a2"), (b2, "e1_b2")):
                    sp.dma_start(dst, a[name]).then_inc(loaded, 16)
                sp.wait_ge(loaded, weights_ready)
                rows_of = 2 * 128
                sp.dma_start(sent.rearrange("(j p q) d -> p j (q d)", p=128, q=2),
                             nought[:, :].unsqueeze(1).broadcast_to([128, BLOCKS * BS // rows_of, 2 * D])).then_inc(prepared, 16)

            def gpsimd(pool):
                top.make_ranks(pool)

                def step(g):
                    pool.wait_ge(e1_weights, 3 * g + 3)
                    for n, (f, k) in enumerate(order):
                        m = g * (FC * 2) + n
                        pool.wait_ge(e1_gate, m + 1)
                        at_least(pool, e1_act, m - 1)
                        pool.tensor_tensor(scaled[n % 2], silu[n % 2], weight_g[:, k, :], ALU.mult).then_inc(e1_scaled, 1)

                groups(pool, step)

            def tensor(pe):
                pe.wait_ge(loaded, weights_ready)
                top.logits_pe(pe)
                for b in range(B):
                    for k in range(2):
                        m = b * 2 + k
                        pe.wait_ge(e1_mask, m + 1)
                        if b % GB == 0 and b >= 2 * GB:
                            pe.wait_ge(e1_maskc, (b // GB - 1) * 4)
                        bank = MASK_BANK[b // GB % 2]
                        cols = slice((b % GB) * T, (b % GB + 1) * T)
                        pe.matmul(ps[:, bank + k, cols], wide[m % MASKS].rearrange("p e r -> p (e r)"), ident16[:, :], start=True, stop=True)
                        pe.transpose(ps[:, (bank + 2 + k) % 8, cols], wide_w[m % MASKS], ident[0:T, 0:T]).then_inc(e1_maskt, 1)
                pe.wait_ge(e1_maskc, 4 * G)

                def hidden(g, f, k):
                    for q, bq in enumerate((b1, b3)):
                        dst = ps[:, 2 + 2 * (f % 3) + q, 0:GT]
                        if k == 0:
                            for n, (wp, xp) in enumerate(PRODUCTS):
                                for c in range(DC):
                                    pe.matmul(dst, w_r[wp][q][:, c, f * 128:(f + 1) * 128], x_r[xp][:, c, :], start=(n == 0 and c == 0), stop=False)
                        mm = pe.matmul(dst, bq[:, f * 128:(f + 1) * 128], lowm[q][k], start=False, stop=True, skip_group_check=k == 1)
                    mm.then_inc(e1_hid, 1)

                def step(g):
                    if not isinstance(g, int) or g > 0:
                        pe.wait_ge(e1_zm, g * 3 + 2)
                    for q, w in ((0, a1), (1, a3)):
                        for c in range(DC):
                            mm = pe.matmul(ps[:, q, 0:GT], w[:, c, :], xn_t[:, c, bass.ds(g * GT, GT)], start=(c == 0), stop=(c == DC - 1))
                        mm.then_inc(e1_low, 1)
                    at_least(pe, e1_added, g * GB)
                    pe.wait_ge(e1_weights, 3 * g + 2)
                    pe.wait_ge(e1_lowm, (g + 1) * 6)
                    for f in range(FC + 1):
                        if f < FC:
                            if f >= 3:
                                pe.wait_ge(e1_act, g * (FC * 2) + when[f - 3, 1] + 1)
                            hidden(g, f, 0)
                        if f > 0:
                            pe.wait_ge(e1_act, g * (FC * 2) + when[f - 1, 0] + 1)
                            hidden(g, f - 1, 1)
                    for k in range(2):
                        for f in range(FC):
                            pe.wait_ge(e1_act, g * (FC * 2) + when[f, k] + 1)
                            mm = pe.matmul(ps[:, k, 0:GT], a2[:, f, :], act_t[k][:, f, :], start=(f == 0), stop=(f == FC - 1))
                        mm.then_inc(e1_z, 1)
                    pe.wait_ge(e1_both, (g + 1) * FC)
                    for q in range(GB):
                        dst = ps[0:T, 2 + q, 0:D]
                        for f in range(FC):
                            pe.matmul(dst, act_t[0][:, f, q * T:(q + 1) * T], wd[:, f, :], start=(f == 0), stop=False)
                        pe.wait_ge(e1_zm, g * 3 + 5)
                        pe.matmul(dst, zm[2][:, q * T:(q + 1) * T], b2, start=False, stop=True).then_inc(e1_out, 1)

                groups(pe, step)

            def scalar(act):
                act.wait_ge(loaded, weights_ready)
                for q in range(2):
                    act.activation(w_r[0][q], w_raw[q], ACT.Copy).then_inc(e1_lowc, 1)
                top.exp_act(act)
                act.activation(idle[:, :], one[:, :], ACT.Silu)
                for g in range(G):
                    for k in range(2):
                        act.wait_ge(e1_maskt, (g * GB + GB - 1) * 2 + k + 1)
                        act.activation(mask_t[:, k, g * GT:(g + 1) * GT], ps[:, MASK_BANK[g % 2] + k, 0:GT], ACT.Copy).then_inc(e1_maskc, 1)
                        act.activation(weight_t[:, k, g * GT:(g + 1) * GT], ps[:, (MASK_BANK[g % 2] + 2 + k) % 8, 0:GT], ACT.Copy).then_inc(e1_maskc, 1)

                def step(g):
                    for q in range(2):
                        act.wait_ge(e1_low, g * 2 + q + 1)
                        at_least(act, e1_lowm, g * 6)
                        act.activation(low[:, q, :], ps[:, q, 0:GT], ACT.Copy).then_inc(e1_lowc, 1)
                    for n, (f, k) in enumerate(order):
                        m = g * (FC * 2) + n
                        act.wait_ge(e1_hid, m + 1)
                        at_least(act, e1_scaled, m - 1)
                        act.activation(silu[n % 2], ps[:, 2 + 2 * (f % 3), 0:GT], ACT.Silu).then_inc(e1_gate, 1)

                groups(act, step)

            def vector(dve):
                def split(g):
                    dve.tensor_copy(x_r[0], xn_t[:, :, bass.ds(g * GT, GT)]).then_inc(e1_weights, 1)
                    dve.wait_ge(e1_weights, 3 * g + 1)
                    dve.tensor_tensor(x_r[1], xn_t[:, :, bass.ds(g * GT, GT)], x_r[0].bitcast(F32), ALU.subtract).then_inc(e1_weights, 1)

                dve.wait_ge(loaded, weights_ready)
                for q in range(2):
                    dve.wait_ge(e1_lowc, q + 1)
                    dve.tensor_tensor(w_r[1][q], w_raw[q], w_r[0][q].bitcast(F32), ALU.subtract)
                dve.wait_ge(ln_evac, top.turned)
                split(0)
                top.choose(dve)
                for k in range(2):
                    dve.tensor_scalar(weight[:, k, :], top.weight[k], gates[0:T, gate:gate + 1], None, ALU.mult).then_inc(e1_zm, 1)
                dve.wait_ge(e1_zm, 2)
                for b in range(B):
                    for k in range(2):
                        m = b * 2 + k
                        at_least(dve, e1_maskt, m - MASKS + 1)
                        dve.tensor_scalar(wide[m % MASKS], top.onehot[k][:, b, :].unsqueeze(2).broadcast_to([T, E, ER // E]), LORA_SCALE, None, ALU.mult)
                        dve.tensor_copy(wide_w[m % MASKS], weight[:, k, b:b + 1].broadcast_to([T, 128])).then_inc(e1_mask, 1)

                def step(g):
                    cols = bass.ds(g * GT, GT)
                    at_least(dve, e1_z, g * 2)
                    if isinstance(g, int) and g == 0:
                        dve.wait_ge(e1_maskc, 4 * G)
                    dve.tensor_copy(weight_g, weight_t[:, :, cols]).then_inc(e1_weights, 1)
                    for q in range(2):
                        dve.wait_ge(e1_lowc, 2 + g * 2 + q + 1)
                        for k in range(2):
                            dve.tensor_tensor(lowm[q][k], low[:, q, :], mask_t[:, k, cols], ALU.mult).then_inc(e1_lowm, 1)
                        dve.wait_ge(e1_lowm, g * 6 + q * 3 + 2)
                        dve.tensor_tensor(lowm[q][1], lowm[q][1], lowm[q][0], ALU.subtract).then_inc(e1_lowm, 1)
                    at_least(dve, e1_out, g * GB)
                    for n, (f, k) in enumerate(order):
                        dve.wait_ge(e1_scaled, g * (FC * 2) + n + 1)
                        dve.tensor_tensor(act_t[k][:, f, :], scaled[n % 2], ps[:, 3 + 2 * (f % 3), 0:GT], ALU.mult).then_inc(e1_act, 1)
                    if not isinstance(g, int) or g < G - 1:
                        split(g + 1)
                    for k in range(2):
                        dve.wait_ge(e1_z, g * 2 + k + 1)
                        dve.tensor_tensor(zm[k], ps[:, k, 0:GT], mask_t[:, k, cols], ALU.mult).then_inc(e1_zm, 1)
                        if k == 0:
                            dve.wait_ge(e1_act, (g + 1) * (FC * 2))
                            for f in range(FC):
                                dve.tensor_tensor(act_t[0][:, f, :], act_t[0][:, f, :], act_t[1][:, f, :], ALU.add).then_inc(e1_both, 1)
                    dve.wait_ge(e1_zm, g * 3 + 4)
                    dve.tensor_tensor(zm[2], zm[0], zm[1], ALU.add).then_inc(e1_zm, 1)
                    for q in range(GB):
                        b = g * GB + q
                        dve.wait_ge(e1_out, b + 1)
                        dve.tensor_tensor(x[:, b, :], ps[0:T, 2 + q, 0:D], x[:, b, :], ALU.add).then_inc(e1_added, 1)

                step(0)
                with dve.Fori(1, G - 1) as g:
                    step(g)
                step(G - 1)

            stage(sync, gpsimd, scalar, vector, tensor)


        def relu_stage():
            arena.clear()
            wreg.clear()
            w1, w2 = wreg.take(128, DC, F), wreg.take(128, FC, D)
            b1 = wreg.take(128, FC)
            weights_ready = expect(4)
            hid = [arena.take(128, FC, GT) for _ in range(2)]
            row = arena.take(128, D)
            add_bias = bias(h, one[0:T, :], row[0:T, :])
            biased = bias_done()
            turned = ln_end["turned"]
            h0, out0, added0 = E * len(F0_ROWS), E * DC, B

            def sync(sp):
                sp.dma_start(row, a["r_b2"].partition_broadcast(128)).then_inc(loaded, 16)
                for dst, name in ((w1, "r_w1"), (b1, "r_b1"), (w2, "r_w2")):
                    sp.dma_start(dst, a[name]).then_inc(loaded, 16)
                sp.wait_ge(loaded, weights_ready)

            def pairs(eng, step):
                step(0, 0)
                step(1, 1)
                with eng.Fori(1, G // 2) as i:
                    step(i * 2, 0)
                    step(i * 2 + 1, 1)

            def tensor(pe):
                pe.wait_ge(loaded, weights_ready)
                pe.wait_ge(ln_evac, turned)

                def step(g, u):
                    for f in range(FC):
                        n = g * FC + f
                        pe.wait_ge(ffn_act, h0 + n - 1)
                        for c in range(DC):
                            mm = pe.matmul(ps[:, f % 2, 0:GT], w1[:, c, f * 128:(f + 1) * 128], xn_t[:, c, bass.ds(g * GT, GT)],
                                           start=(c == 0), stop=(c == DC - 1))
                        mm.then_inc(ffn_h, 1)
                    pe.wait_ge(ffn_act, h0 + (g + 1) * FC)
                    for q in range(GB):
                        pe.wait_ge(ffn_added, added0 + g * GB + q - 1)
                        for f in range(FC):
                            mm = pe.matmul(ps[0:T, 2 + q % 2, 0:D], hid[u][:, f, q * T:(q + 1) * T], w2[:, f, :], start=(f == 0), stop=(f == FC - 1))
                        mm.then_inc(ffn_out, 1)

                pairs(pe, step)

            def scalar(act):
                act.wait_ge(loaded, weights_ready)

                def step(g, u):
                    act.wait_ge(ffn_out, out0 + (g - 1) * GB)
                    for f in range(FC):
                        act.wait_ge(ffn_h, h0 + g * FC + f + 1)
                        act.activation(hid[u][:, f, :], ps[:, f % 2, 0:GT], ACT.Relu, bias=b1[:, f:f + 1]).then_inc(ffn_act, 1)

                pairs(act, step)

            def vector(dve):
                dve.wait_ge(loaded, weights_ready)
                add_bias(dve)
                dve.wait_ge(bias_added, biased)

                def step(g, u):
                    for q in range(GB):
                        b = g * GB + q
                        dve.wait_ge(ffn_out, out0 + b + 1)
                        dve.tensor_tensor(h[:, b, :], h[:, b, :], ps[0:T, 2 + q % 2, 0:D], ALU.add).then_inc(ffn_added, 1)

                pairs(dve, step)

            stage(sync, None, scalar, vector, tensor)

        pk_group, pk_q, pk_qc = sem("pk_group"), sem("pk_q"), sem("pk_qc")
        pk_h, pk_gate, pk_act = sem("pk_h"), sem("pk_gate"), sem("pk_act")
        pk_emb, pk_silu, pk_sim, pk_simc = sem("pk_emb"), sem("pk_silu"), sem("pk_sim"), sem("pk_simc")
        pk_step, pk_exp, pk_sum, pk_dexp, pk_kept = (sem("pk_step"), sem("pk_exp"), sem("pk_sum"),
                                                              sem("pk_dexp"), sem("pk_kept"))
        pk_top = sem("pk_top")
        pk_mixed, pk_turned, pk_turnc, pk_out, pk_added = (sem("pk_mixed"), sem("pk_turned"), sem("pk_turnc"), sem("pk_out"), sem("pk_added"))

        def product_key_stage(gate):
            arena.clear()
            wreg.clear()
            wlow.clear()
            wg, wu = wreg.take(128, DC, F), wreg.take(128, DC, F)
            wd = wreg.take(128, FC, D)
            wq = wreg.take(128, DC, 2 * PH * PK)
            keys = wreg.take(128, 4, 2 * PK)
            de, ue = wreg.take(128, DC, NEXP), wreg.take(128, NEXP // 128, D)
            bcols = wreg.take(128, 2, FC)
            group_t = arena.take(128, DC, GT)
            q_t = wlow.take(128, 4, GT)
            hid = arena.take(128, FC, GT)
            silu = [arena.take(128, GT) for _ in range(2)]
            act_e = [h[:, 4 * q:4 * q + 4, :].rearrange("p b d -> p (b d)") for q in range(GB)]
            sims = [arena.take(T, 2 * PH, PK) for _ in range(GB)]
            sums = [arena.take(T, PI, PK) for _ in range(PH)]
            exps = [arena.take(T, PI, PK) for _ in range(2)]
            mix = [arena.take(T, NEXP) for _ in range(2)]
            mix_t = arena.take(128, NEXP // 128, T)
            K = 8
            best = arena.take(T, GB, 2 * PH, K)
            index = arena.take(T, GB, PH, K, dtype=mybir.dt.uint32)
            beyond = arena.take(T, GB * PH * K)
            grid, shifted, chosen = (arena.take(T, GB, PH, K * K) for _ in range(3))
            top = arena.take(T, GB, PH, K)
            negmax, total, share, clamped = (arena.take(T, GB, PH) for _ in range(4))
            rowsum = arena.take(T, GB * PH * K)
            last = arena.take(T, GB)
            spare = arena.take(T, 2)
            EMB_BANK = (4, 0, 2, 4)
            EXPS = GB + 1
            SHIFTED = 6 * GB
            WEIGHTED = SHIFTED + 10
            LINKS = WEIGHTED + GB
            weights_ready = expect(10)
            row = arena.take(128, D)
            add_bias = bias(x, gates[0:T, gate:gate + 1], row[0:T, :])
            biased = bias_done()
            turned = ln_end["turned"]
            keys_cleared = expect_made(1)

            def sync(sp):
                sp.dma_start(row, a["p_bd"].partition_broadcast(128)).then_inc(loaded, 16)
                for dst, name in ((wq, "p_q"), (wg, "p_gate"), (wu, "p_up"), (bcols, "p_bcols"), (de, "p_down_e"), (wd, "p_down"), (ue, "p_up_e")):
                    sp.dma_start(dst, a[name]).then_inc(loaded, 16)
                sp.wait_ge(const_made, keys_cleared)
                for q in range(2):
                    sp.dma_start(keys[64 * q:64 * q + 64, :, 64 * q:64 * q + 64], a["p_keys"][64 * q:64 * q + 64]).then_inc(loaded, 16)
                sp.wait_ge(loaded, weights_ready)

            def tensor(pe):
                pe.wait_ge(loaded, weights_ready)

                def queries(g):
                    pe.wait_ge(pk_group, g + 1)
                    for c in range(4):
                        if c < 2:
                            at_least(pe, pk_act, g * FC)
                            at_least(pe, pk_silu, (g - 1) * GB + 2)
                        else:
                            pe.wait_ge(pk_qc, g * 4 + c - 1)
                        for d in range(DC):
                            mm = pe.matmul(ps[:, c % 2, 0:GT], wq[:, d, c * 128:(c + 1) * 128], group_t[:, d, :], start=(d == 0), stop=(d == DC - 1))
                        mm.then_inc(pk_q, 1)

                def similarities(g):
                    pe.wait_ge(pk_qc, (g + 1) * 4)
                    at_least(pe, pk_silu, g * GB)
                    for q in range(GB):
                        at_least(pe, pk_simc, g * GB + q - 1)
                        for c in range(4):
                            mm = pe.matmul(ps[0:T, 4 + q % 2, c * 128:(c + 1) * 128], q_t[:, c, q * T:(q + 1) * T], keys[:, c, :], start=True, stop=True)
                        mm.then_inc(pk_sim, 1)

                def out(g, q):
                    n = g * GB + q
                    bank = 6 + q % 2
                    at_least(pe, pk_added, n - 1)
                    for f in range(FC):
                        pe.matmul(ps[0:T, bank, 0:D], hid[:, f, q * T:(q + 1) * T], wd[:, f, :], start=(f == 0), stop=False)
                    pe.wait_ge(pk_mixed, n + 1)
                    if q == 0:
                        pe.wait_ge(pk_silu, n + 3)
                    at_least(pe, pk_turnc, n * 2)
                    for k in range(NEXP // 128):
                        mm = pe.transpose(ps[:, 2 + k // 4, (k % 4) * T:(k % 4 + 1) * T], act_e[q][:, k * 128:(k + 1) * 128], ident[0:T, 0:T])
                    mm.then_inc(pk_turned, 1)
                    pe.wait_ge(pk_turnc, n * 2 + 2)
                    for k in range(NEXP // 128):
                        mm = pe.matmul(ps[0:T, bank, 0:D], mix_t[:, k, :], ue[:, k, :], start=False, stop=(k == NEXP // 128 - 1))
                    mm.then_inc(pk_out, 1)

                def embeddings(g, q):
                    if q == 1 or q == 2:
                        pe.wait_ge(pk_act, g * FC + FC - 2 + q)
                    elif q == 3:
                        pe.wait_ge(pk_silu, g * GB + 1)
                    for e in range(2):
                        for d in range(DC):
                            mm = pe.matmul(ps[0:T, EMB_BANK[q] + e, :], group_t[:, d, q * T:(q + 1) * T], de[:, d, e * 512:(e + 1) * 512],
                                           start=(d == 0), stop=(d == DC - 1))
                    mm.then_inc(pk_emb, 1)

                def step(g):
                    at_least(pe, pk_turnc, g * GB * 2)
                    for f in range(FC):
                        at_least(pe, pk_act, g * FC + f - 1)
                        for q, w in ((0, wg), (1, wu)):
                            for d in range(DC):
                                mm = pe.matmul(ps[:, 2 * (f % 2) + q, 0:GT], w[:, d, f * 128:(f + 1) * 128], group_t[:, d, :],
                                               start=(d == 0), stop=(d == DC - 1))
                        mm.then_inc(pk_h, 1)
                    pe.wait_ge(pk_simc, (g + 1) * GB)
                    for q in range(GB):
                        embeddings(g, q)
                    pe.wait_ge(pk_act, (g + 1) * FC)
                    more = not isinstance(g, int) or g < G - 1
                    for q in range(GB):
                        if q == GB - 1 and more:
                            similarities(g + 1)
                        out(g, q)
                        if q == 1 and more:
                            queries(g + 1)

                queries(0)
                similarities(0)
                over_groups(pe, step)

            def over_groups(eng, step):
                step(0)
                with eng.Fori(1, G - 1) as g:
                    step(g)
                step(G - 1)

            def scalar(act):
                act.wait_ge(loaded, weights_ready)

                def turned(n):
                    act.wait_ge(pk_turned, n + 1)
                    at_least(act, pk_out, n)
                    for k in range(2):
                        act.activation(mix_t[:, 4 * k:4 * k + 4, :], ps[:, 2 + k, 0:4 * T].rearrange("p (k t) -> p k t", k=4),
                                       ACT.Copy).then_inc(pk_turnc, 1)

                def queries(g):
                    at_least(act, pk_sim, g * GB)
                    for c in range(4):
                        act.wait_ge(pk_q, g * 4 + c + 1)
                        act.activation(q_t[:, c, :], ps[:, c % 2, 0:GT], ACT.Copy).then_inc(pk_qc, 1)

                def similarities(g):
                    for q in range(GB):
                        n = g * GB + q
                        act.wait_ge(pk_sim, n + 1)
                        at_least(act, pk_sum, (n - GB + 1) * PH)
                        act.activation(sims[q], ps[0:T, 4 + q % 2, :].rearrange("p (h k) -> p h k", k=PK), ACT.Copy).then_inc(pk_simc, 1)

                def embeddings(g, q):
                    n = g * GB + q
                    act.wait_ge(pk_emb, n + 1)
                    at_least(act, pk_turned, n - GB + 1)
                    act.activation(act_e[q].rearrange("p (e k) -> p e k", e=2), ps[0:T, EMB_BANK[q]:EMB_BANK[q] + 2, :],
                                   ACT.Tanh, scale=0.5).then_inc(pk_exp, 1)

                def step(g):
                    more = not isinstance(g, int) or g < G - 1
                    act.activation(idle[:, :], one[:, :], ACT.Silu)
                    for f in range(FC):
                        n = g * FC + f
                        act.wait_ge(pk_h, n + 1)
                        at_least(act, pk_act, n - 1)
                        act.activation(silu[f % 2], ps[:, 2 * (f % 2), 0:GT], ACT.Silu, bias=bcols[:, 0, f:f + 1]).then_inc(pk_gate, 1)
                    act.activation(idle[:, :], one[:, :], ACT.Exp)
                    embeddings(g, 0)
                    act.wait_ge(pk_step, g * LINKS + SHIFTED)
                    act.activation(shifted, shifted, ACT.Exp).then_inc(pk_exp, 1)
                    for q in range(GB):
                        n = g * GB + q
                        for hd in range(PH):
                            m = n * PH + hd
                            act.wait_ge(pk_sum, m + 1)
                            at_least(act, pk_kept, m - 1)
                            act.activation(exps[hd % 2], sums[hd], ACT.Exp, bias=negmax[:, q, hd:hd + 1]).then_inc(pk_dexp, 1)
                            if q < 2 and hd == 1:
                                embeddings(g, 1 + 2 * q)
                            if q > 0 and hd == 2:
                                turned(n - 1)
                            if q == 3 and hd == 1 and more:
                                queries(g + 1)
                        if q == 0:
                            embeddings(g, 2)
                    if more:
                        similarities(g + 1)
                    turned(g * GB + GB - 1)

                queries(0)
                similarities(0)
                over_groups(act, step)

            def gpsimd(pool):
                pool.memset(keys, 0.0).then_inc(const_made, 1)

                def step(g):
                    for q in range(GB):
                        n = g * GB + q
                        pool.wait_ge(pk_simc, n + 1)
                        for hd in range(PH):
                            m = n * PH + hd
                            at_least(pool, pk_kept, m - PH + 1)
                            pool.tensor_tensor(sums[hd], sims[q][:, hd, 0:PI].unsqueeze(2).broadcast_to([T, PI, PK]),
                                               sims[q][:, PH + hd, :].unsqueeze(1).broadcast_to([T, PI, PK]), ALU.add).then_inc(pk_sum, 1)
                        if q > 0:
                            activate(g, q - 1)
                    activate(g, GB - 1)

                def activate(g, q):
                    pool.wait_ge(pk_silu, g * GB + q + 1)
                    pool.wait_ge(pk_step, g * LINKS + WEIGHTED + q + 1)
                    pool.tensor_tensor(act_e[q], mix[q % 2], act_e[q], ALU.mult).then_inc(pk_mixed, 1)

                over_groups(pool, step)

            def vector(dve):
                dve.wait_ge(loaded, weights_ready)
                add_bias(dve)
                dve.wait_ge(bias_added, biased)

                def stream(g):
                    at_least(dve, pk_emb, g * GB)
                    dve.tensor_copy(group_t, xn_t[:, :, bass.ds(g * GT, GT)]).then_inc(pk_group, 1)

                dve.wait_ge(ln_evac, turned)
                stream(0)

                def add(n, q):
                    dve.wait_ge(pk_out, n + 1)
                    dve.scalar_tensor_tensor(x[:, n, :], ps[0:T, 6 + q % 2, 0:D], gates[0:T, gate:gate + 1], x[:, n, :],
                                             ALU.mult, ALU.add).then_inc(pk_added, 1)

                def step(g):
                    done = [0]

                    def link(ins):
                        done[0] += 1
                        ins.then_inc(pk_step, 1)
                        dve.wait_ge(pk_step, g * LINKS + done[0])

                    def hold():
                        dve.memset(spare, 0.0)

                    def over(v):
                        return v.broadcast_to([T, PH, K * K])

                    def select(q):
                        dve.wait_ge(pk_simc, g * GB + q + 1)
                        hold()
                        for s in range(2 * PH):
                            ins = dve.max(best[:, q, s, :], sims[q][:, s, :])
                        link(ins)
                        link(dve.tensor_tensor(grid[:, q].rearrange("p h (i j) -> p h i j", i=K),
                                               best[:, q, 0:PH, :].unsqueeze(3).broadcast_to([T, PH, K, K]),
                                               best[:, q, PH:2 * PH, :].unsqueeze(2).broadcast_to([T, PH, K, K]), ALU.add))
                        hold()
                        for s in range(PH):
                            dve.max_index(index[:, q, s, :], best[:, q, s, :], sims[q][:, s, :])
                        for s in range(PH):
                            ins = dve.max(top[:, q, s, :], grid[:, q, s, :])
                        link(ins)

                    def shift(q):
                        if q == 0:
                            at_least(dve, pk_dexp, g * GB * PH)
                        link(dve.tensor_scalar(negmax[:, q, :], top[:, q, :, 0], -1.0, None, ALU.mult))
                        link(dve.tensor_tensor(shifted[:, q], grid[:, q], over(top[:, q, :, 0:1]), ALU.subtract))
                        link(dve.tensor_tensor(chosen[:, q], grid[:, q], over(top[:, q, :, K - 1:K]), ALU.is_ge))

                    def hidden(f):
                        if f == 0:
                            at_least(dve, pk_out, g * GB)
                        dve.wait_ge(pk_gate, g * FC + f + 1)
                        dve.scalar_tensor_tensor(hid[:, f, :], ps[:, 2 * (f % 2) + 1, 0:GT], bcols[:, 1, f:f + 1], silu[f % 2],
                                                 ALU.add, ALU.mult).then_inc(pk_act, 1)

                    def shares():
                        dve.wait_ge(pk_exp, g * EXPS + 2)
                        flat = "p q h k -> p (q h k)"
                        link(dve.tensor_tensor(chosen.rearrange(flat), chosen.rearrange(flat), shifted.rearrange(flat), ALU.mult))
                        link(dve.tensor_scalar(beyond, index.rearrange(flat), float(PI), None, ALU.is_ge))
                        link(dve.tensor_reduce(rowsum, chosen.rearrange("p q h (i j) -> p (q h i) j", j=K), AX.X, ALU.add))
                        link(dve.tensor_reduce(total.rearrange("p q h -> p (q h)"), rowsum.rearrange("p (r i) -> p r i", i=K), AX.X, ALU.add))
                        link(dve.reciprocal(share.rearrange("p q h -> p (q h)"), total.rearrange("p q h -> p (q h)")))
                        link(dve.tensor_tensor(rowsum, rowsum, beyond, ALU.mult))
                        link(dve.tensor_reduce(clamped.rearrange("p q h -> p (q h)"), rowsum.rearrange("p (r i) -> p r i", i=K), AX.X, ALU.add))
                        link(dve.tensor_scalar(share, share, 0.5, None, ALU.mult))
                        link(dve.tensor_tensor(clamped, clamped, share, ALU.mult))
                        link(dve.tensor_reduce(last, clamped, AX.X, ALU.add))

                    def activations(q):
                        dve.wait_ge(pk_exp, g * EXPS + (2 + q if q else 1))
                        act_q = act_e[q].rearrange("p (e k) -> p e k", e=2)
                        dve.scalar_tensor_tensor(act_q, act_q, 1.0, ps[0:T, EMB_BANK[q]:EMB_BANK[q] + 2, :], ALU.add, ALU.mult).then_inc(pk_silu, 1)

                    def weigh(q):
                        n = g * GB + q
                        at_least(dve, pk_mixed, n - 1)
                        for hd in range(PH):
                            m = n * PH + hd
                            dve.wait_ge(pk_dexp, m + 1)
                            dve.scalar_tensor_tensor(exps[hd % 2], sums[hd], top[:, q, hd, K - 1:K], exps[hd % 2], ALU.is_ge, ALU.mult).then_inc(pk_top, 1)
                            dve.wait_ge(pk_top, m + 1)
                            flat_e = exps[hd % 2].rearrange("p i j -> p (i j)")
                            if hd == 2 and q >= 2:
                                add(n - 2, q - 2)
                            if hd == 2 and q < 2:
                                activations(1 + 2 * q)
                            if hd == 0:
                                dve.tensor_scalar(mix[q % 2], flat_e, share[:, q, 0:1], None, ALU.mult).then_inc(pk_kept, 1)
                            else:
                                dve.wait_ge(pk_kept, m)
                                dve.scalar_tensor_tensor(mix[q % 2], flat_e, share[:, q, hd:hd + 1], mix[q % 2], ALU.mult, ALU.add).then_inc(pk_kept, 1)
                        dve.wait_ge(pk_kept, (n + 1) * PH)
                        link(dve.tensor_tensor(mix[q % 2][:, NEXP - 1:NEXP], mix[q % 2][:, NEXP - 1:NEXP], last[:, q:q + 1], ALU.add))

                    select(0)
                    if not isinstance(g, int) or g > 0:
                        ends(g - 1)
                    hidden(0)
                    shift(0)
                    hidden(1)
                    select(1)
                    hidden(2)
                    shift(1)
                    hidden(3)
                    select(2)
                    hidden(4)
                    shift(2)
                    for f in range(5, FC):
                        hidden(f)
                    select(3)
                    shift(3)
                    assert done[0] == SHIFTED
                    activations(0)
                    shares()
                    for q in range(GB):
                        weigh(q)
                        if q == 0:
                            activations(2)
                        if q == 1 and (not isinstance(g, int) or g < G - 1):
                            stream(g + 1)
                    assert done[0] == LINKS

                def ends(g):
                    for q in (GB - 2, GB - 1):
                        add(g * GB + q, q)

                over_groups(dve, step)
                ends(G - 1)

            stage(sync, gpsimd, scalar, vector, tensor)

        m_prefix, m_index = sem("m_prefix"), sem("m_index")
        m_w_in, m_w_out = [sem("m_w_in0"), sem("m_w_in1")], [sem("m_w_out0"), sem("m_w_out1")]
        m_high, m_low = sem("m_high"), sem("m_low")
        m_sent, m_x, m_rows = sem("m_sent"), [sem("m_x0"), sem("m_x1")], [sem("m_rows0"), sem("m_rows1")]
        m_xt, m_xtc, m_biased = sem("m_xt"), sem("m_xtc"), sem("m_biased")
        m_h, m_gate, m_act, m_out, m_res = sem("m_h"), sem("m_gate"), sem("m_act"), sem("m_out"), sem("m_res")
        m_norm, m_aggr, m_rstd, m_y = sem("m_norm"), sem("m_aggr"), sem("m_rstd"), sem("m_y")
        m_stored, m_got, m_added = [sem("m_stored0"), sem("m_stored1")], [sem("m_got0"), sem("m_got1")], sem("m_added")

        def routed_experts_stage(gate):
            arena.clear()
            arena.take(128, MOE_W_WORDS + MOE_X_WORDS)
            wreg.clear()
            wlow.clear()
            EPS = 1e-12
            kept = ln_end["stored"]
            inputs_ready = expect(2)
            HALVES = BS // 128
            TOP_BLOCKS = -(-(B * T) // BS)
            w_in = [wreg.take(128, 2, DC, F) for _ in range(2)]
            w_out_b = [wreg.take(128, W_OUT + W_B) for _ in range(2)]
            w_out = [w[:, 0:W_OUT].rearrange("p (f d) -> p f d", f=FC) for w in w_out_b]
            bcols = [w[:, W_OUT:].rearrange("p (q f) -> p q f", q=2) for w in w_out_b]
            w_r = [moe_w_r[:, part] for part in range(2)]
            x_r = [[moe_x_r[:, u, part] for part in range(2)] for u in range(2)]
            router = wlow.take(128, DC, E)
            br = arena.take(T, E)
            top = TopTwo(router, br)
            top.plan()
            chosen = rt_count["step"]
            routing_made = expect_made(4)
            coef = arena.take(T, 2, B)
            before = arena.take(T, T)
            ones = arena.take(T, 128)
            thresholds = arena.take(128, E, TOP_BLOCKS)
            block_no = arena.take(128, BLOCKS, E)
            lane = arena.take(128, 2)
            lane_i = arena.take(128, 2, dtype=I32)
            both = arena.take(T, B, E)
            run = arena.take(128, B + 1, E)
            filled = arena.take(128, E, TOP_BLOCKS)
            blocks_of = arena.take(128, E)
            first = arena.take(128, E)
            started = arena.take(128, BLOCKS, E)
            expert = arena.take(128, BLOCKS)
            w_index = arena.take(128, BLOCKS, dtype=mybir.dt.uint32)
            row_index = arena.take(128, BLOCKS, dtype=mybir.dt.uint32)
            place = arena.take(T, B, E)
            picked = arena.take(T, B, E)
            slot = [arena.take(T, B, dtype=mybir.dt.uint32) for _ in range(2)]
            half_b = [arena.take(128, FC) for _ in range(2)]
            rows = [arena.take(128, 3 * D) for _ in range(2)]
            free = Region(xn_t.rearrange("p c t -> p (c t)"), DC * B * T)
            x_in = [free.take(128, HALVES, D) for _ in range(2)]
            y = [free.take(128, HALVES, D) for _ in range(2)]
            biased = [free.take(128, HALVES, D) for _ in range(2)]
            res = free.take(128, HALVES, D)
            gelu = [arena.take(128, BS) for _ in range(2)]
            tanh = [arena.take(128, BS) for _ in range(2)]
            hid = [arena.take(128, FC, BS) for _ in range(2)]
            stats = arena.take(128, HALVES, 6)
            moments = arena.take(128, HALVES, 2)
            eps = arena.take(128, HALVES)
            rstd = arena.take(128, HALVES)
            exponent = arena.take(128, HALVES)
            spare = arena.take(128, 2)
            PRODUCTS = ((0, 0), (0, 1), (1, 0))
            RING = 4
            fetched = [(m_got[0], 0), (m_got[1], 0)] + [(m_rows[u], 16 * ((BLOCKS + 1 - u) // 2)) for u in range(2)]
            got = [(wlow if r < RING // 2 else arena).take(T, 2 * D) for r in range(RING)]
            SENDS = 2 * B

            def over_blocks(eng, step):
                step(0, 0, 0)
                step(1, 1, 0)
                with eng.Fori(1, BLOCKS // 2) as i:
                    step(i * 2, 0, i)
                    step(i * 2 + 1, 1, i)
                step(BLOCKS - 1, (BLOCKS - 1) % 2, BLOCKS // 2)

            def sync(sp):
                for dst, src in ((router, a["m_router"]), (br, a["m_br"].partition_broadcast(T))):
                    sp.dma_start(dst, src).then_inc(loaded, 16)

                def load(j, u):
                    sp.dma_start(x_in[u], sent[bass.ds(j * BS, BS), :].rearrange("(q p) d -> p q d", p=128)).then_inc(m_x[u], 16)

                def store(j, u):
                    sp.wait_ge(m_y, (j + 1) * HALVES)
                    sp.dma_start(returned[bass.ds(j * BS, BS), :].rearrange("(q p) d -> p q d", p=128), y[u]).then_inc(m_stored[u], 16)

                sp.wait_ge(m_sent, 16 * SENDS)
                load(0, 0)
                load(1, 1)
                with sp.Fori(0, (BLOCKS - 1) // 2 - 1) as i:
                    for u in range(2):
                        store(i * 2 + u, u)
                        load(i * 2 + u + 2, u)
                last = BLOCKS - 3
                store(last, last % 2)
                load(last + 2, last % 2)
                store(last + 1, (last + 1) % 2)
                store(last + 2, last % 2)
                for q in range(2):
                    these = slice(q * B // 2, (q + 1) * B // 2)
                    sp.wait_ge(m_added, (q + 1) * B)
                    sp.dma_start(a["out"][these].rearrange("b t d -> t b d"), x[:, these, :]).then_inc(stored, 16)
                sp.wait_ge(stored, 32)

            def gpsimd(pool):
                top.make_ranks(pool)
                pool.memset(before, 1.0).then_inc(const_made, 1)
                pool.memset(ones, 1.0)
                pool.memset(eps, EPS)
                pool.memset(exponent, -0.5)
                for k in range(TOP_BLOCKS):
                    pool.memset(thresholds[:, :, k], float(k * BS))
                for k in range(BLOCKS):
                    pool.memset(block_no[:, k, :], float(k))
                pool.iota(lane_i, pattern=[[0, 2]], base=-128, channel_multiplier=1).then_inc(const_made, 1)
                pool.wait_ge(const_made, routing_made - 2)
                pool.tensor_copy(lane, lane_i).then_inc(const_made, 1)
                pool.affine_select(out=before, in_=before, compare_op=ALU.is_gt, fill=0.0, base=0, pattern=[[1, T]],
                                   channel_multiplier=-1).then_inc(const_made, 1)

                def gather_in(j):
                    pool.indirect_dma_start(w_in[j % 2].rearrange("p q c f -> p (q c f)"), None, a["m_w_in"],
                                            bass.IndirectOffsetOnAxis(ap=w_index[:, j:j + 1], axis=0)).then_inc(m_w_in[j % 2], 16)

                def gather_out(j):
                    pool.indirect_dma_start(w_out_b[j % 2], None, a["m_w_out"], bass.IndirectOffsetOnAxis(ap=w_index[:, j:j + 1], axis=0)
                                            ).then_inc(m_w_out[j % 2], 16)

                def gather_rows(j):
                    pool.indirect_dma_start(rows[j % 2], None, a["m_rows"], bass.IndirectOffsetOnAxis(ap=row_index[:, j:j + 1], axis=0)
                                            ).then_inc(m_rows[j % 2], 16)

                pool.wait_ge(m_index, 1)
                for j in range(2):
                    gather_in(j)
                    gather_out(j)
                    gather_rows(j)
                pool.wait_ge(m_index, 3)
                pool.wait_ge(prepared, 32)
                pool.wait_ge(ln_stored, kept)
                for k in range(2):
                    for b in range(B):
                        pool.indirect_dma_start(sent, bass.IndirectOffsetOnAxis(ap=slot[k][:, b:b + 1], axis=0), h[:, b, :], None
                                                ).then_inc(m_sent, 16)
                def split_low(j, tiles):
                    for f in tiles:
                        pool.wait_ge(m_high, j * FC + f + 1)
                        cols = slice(f * 128, (f + 1) * 128)
                        pool.tensor_tensor(w_r[1][:, :, :, cols], w_in[j % 2][:, :, :, cols], w_r[0][:, :, :, cols].bitcast(F32),
                                           ALU.subtract).then_inc(m_low, 1)

                def rstds(j):
                    pool.wait_ge(m_aggr, (j + 1) * HALVES)
                    at_least(pool, m_y, j * HALVES)
                    pool.tensor_tensor(rstd, moments[:, :, 1], eps, ALU.add).then_inc(m_rstd, 1)
                    pool.wait_ge(m_rstd, 2 * j + 1)
                    pool.tensor_tensor(rstd, rstd, exponent, ALU.pow).then_inc(m_rstd, 1)

                pool.wait_ge(m_low, FC)
                for j in range(BLOCKS):
                    follows = 0 < j < BLOCKS - 1
                    if follows:
                        pool.wait_ge(m_out, j)
                        gather_out(j + 1)
                    if j > 0:
                        rstds(j - 1)
                    if j + 1 < BLOCKS:
                        split_low(j + 1, range(2))
                    if follows:
                        pool.wait_ge(m_y, j * HALVES)
                        gather_rows(j + 1)
                    if j + 1 < BLOCKS:
                        split_low(j + 1, range(2, FC))
                    if j == 0:
                        gather_in(2)
                    if j + 3 < BLOCKS:
                        pool.wait_ge(m_low, (j + 2) * FC)
                        gather_in(j + 3)
                rstds(BLOCKS - 1)
                for u in range(2):
                    pool.wait_ge(m_stored[u], 16 * ((BLOCKS + 1 - u) // 2))
                for b in range(B):
                    at_least(pool, m_added, 2 * (b - RING + 1))
                    for k in range(2):
                        pool.indirect_dma_start(got[b % RING][:, k * D:(k + 1) * D], None, returned,
                                                bass.IndirectOffsetOnAxis(ap=slot[k][:, b:b + 1], axis=0)).then_inc(fetched[b % RING][0], 16)

            def tensor(pe):
                pe.wait_ge(loaded, inputs_ready)
                top.logits_pe(pe)
                pe.wait_ge(const_made, routing_made)
                pe.wait_ge(rt_step, chosen + 1)
                pe.matmul(ps[0:T, 1, 0:B * E], before, both.rearrange("p b e -> p (b e)"), start=True, stop=True)
                pe.matmul(ps[:, 2, 0:B * E], ones, both.rearrange("p b e -> p (b e)"), start=True, stop=True).then_inc(m_prefix, 1)

                def turn(j, u, i):
                    pe.wait_ge(m_x[u], (i + 1) * 16)
                    at_least(pe, m_xtc, 2 * j)
                    for q in range(HALVES):
                        for c in range(DC):
                            mm = pe.transpose(ps[:, 4, c * BS + q * 128:c * BS + (q + 1) * 128], x_in[u][:, q, c * 128:(c + 1) * 128], ident[:, :])
                    mm.then_inc(m_xt, 1)

                turn(0, 0, 0)

                def step(j, u, i):
                    pe.wait_ge(m_xtc, 2 * j + 2)
                    if isinstance(j, int) and j == 0:
                        pe.wait_ge(m_low, FC)
                    for f in range(FC):
                        if not isinstance(j, int) or j > 0:
                            pe.wait_ge(m_low, j * FC + f + 1)
                        at_least(pe, m_act, j * FC + f - 3)
                        for q in range(2):
                            for n, (wp, xp) in enumerate(PRODUCTS):
                                for c in range(DC):
                                    mm = pe.matmul(ps[:, f % 4, q * BS:(q + 1) * BS], w_r[wp][:, q, c, f * 128:(f + 1) * 128], x_r[u][xp][:, c, :],
                                                   start=(n == 0 and c == 0), stop=(n == len(PRODUCTS) - 1 and c == DC - 1))
                        mm.then_inc(m_h, 1)
                    if not isinstance(j, int) or j < BLOCKS - 1:
                        turn(j + 1, 1 - u, i + u)
                    at_least(pe, m_res, (j - 1) * HALVES)
                    pe.wait_ge(m_w_out[u], (i + 1) * 16)
                    for q in range(HALVES):
                        for f in range(FC):
                            if q == 0:
                                pe.wait_ge(m_act, j * FC + f + 1)
                            mm = pe.matmul(ps[:, 5 + u, q * D:(q + 1) * D], hid[u][:, f, q * 128:(q + 1) * 128], w_out[u][:, f, :],
                                           start=(f == 0), stop=(f == FC - 1))
                    mm.then_inc(m_out, 1)

                over_blocks(pe, step)

            def scalar(act):
                top.exp_act(act)
                act.activation(idle[:, :], one[:, :], ACT.Gelu)

                def copy(j, u):
                    act.wait_ge(m_xt, j + 1)
                    at_least(act, m_h, (j - 1) * FC)
                    act.activation(x_r[u][0], ps[:, 4, 0:DC * BS].rearrange("p (c s) -> p c s", c=DC), ACT.Copy).then_inc(m_xtc, 1)

                def split_high(v, f):
                    cols = slice(f * 128, (f + 1) * 128)
                    act.activation(w_r[0][:, :, :, cols], w_in[v][:, :, :, cols], ACT.Copy).then_inc(m_high, 1)

                act.wait_ge(m_w_in[0], 16)
                for f in range(FC):
                    split_high(0, f)
                copy(0, 0)

                def step(j, u, i):
                    follows = not isinstance(j, int) or j < BLOCKS - 1
                    act.wait_ge(m_w_out[u], (i + 1) * 16)
                    if follows:
                        act.wait_ge(m_w_in[1 - u], (i + u + 1) * 16)
                    act.wait_ge(m_biased, 2 * j + 1)
                    for f in range(FC):
                        n = j * FC + f
                        act.wait_ge(m_h, n + 1)
                        at_least(act, m_act, n - 1)
                        act.activation(gelu[f % 2], ps[:, f % 4, 0:BS], ACT.Gelu, bias=bcols[u][:, 0, f:f + 1])
                        act.activation(tanh[f % 2], ps[:, f % 4, BS:2 * BS], ACT.Tanh, scale=0.5, bias=half_b[u][:, f:f + 1]).then_inc(m_gate, 1)
                        if follows:
                            split_high(1 - u, f)
                    if follows:
                        copy(j + 1, 1 - u)

                over_blocks(act, step)

            def vector(dve):
                dve.wait_ge(loaded, inputs_ready)
                top.choose(dve)
                for k in range(2):
                    dve.tensor_scalar(coef[:, k, :], top.weight[k], gates[0:T, gate:gate + 1], None, ALU.mult)
                steps = [chosen]

                def link(ins):
                    steps[0] += 1
                    ins.then_inc(rt_step, 1)
                    dve.wait_ge(rt_step, steps[0])

                link(dve.tensor_tensor(both, top.onehot[0], top.onehot[1], ALU.add))
                dve.wait_ge(const_made, routing_made)
                dve.wait_ge(m_prefix, 1)
                counts = ps[:, 2, 0:B * E].rearrange("p (b e) -> p b e", e=E)
                dve.memset(first[:, 0:1], 0.0)
                link(dve.memset(run[:, 0, :], 0.0))
                for b in range(B):
                    link(dve.tensor_tensor(run[:, b + 1, :], run[:, b, :], counts[:, b, :], ALU.add))
                link(dve.tensor_tensor(filled, run[:, B, :].unsqueeze(2).broadcast_to([128, E, TOP_BLOCKS]), thresholds, ALU.is_gt))
                link(dve.tensor_reduce(blocks_of, filled, AX.X, ALU.add))
                for e in range(1, E):
                    link(dve.tensor_tensor(first[:, e:e + 1], first[:, e - 1:e], blocks_of[:, e - 1:e], ALU.add))
                link(dve.tensor_tensor(started, block_no, first.unsqueeze(1).broadcast_to([128, BLOCKS, E]), ALU.is_ge))
                link(dve.tensor_reduce(expert, started, AX.X, ALU.add))
                dve.tensor_scalar(row_index, expert, 1.0, None, ALU.subtract)
                dve.tensor_scalar(w_index, expert, 128.0, lane[:, 0:1], ALU.mult, ALU.add).then_inc(m_index, 1)
                link(dve.tensor_tensor(place, ps[0:T, 1, 0:B * E].rearrange("p (b e) -> p b e", e=E), run[0:T, 0:B, :], ALU.add))
                link(dve.scalar_tensor_tensor(place, first[0:T, :].unsqueeze(1).broadcast_to([T, B, E]), float(BS), place, ALU.mult, ALU.add))
                for k in range(2):
                    link(dve.tensor_tensor(picked, top.onehot[k], place, ALU.mult))
                    link(dve.tensor_reduce(top.found, picked, AX.X, ALU.add))
                    dve.tensor_copy(slot[k], top.found).then_inc(m_index, 1)
                    dve.wait_ge(m_index, k + 2)

                for f in range(FC):
                    dve.wait_ge(m_high, f + 1)
                    cols = slice(f * 128, (f + 1) * 128)
                    dve.tensor_tensor(w_r[1][:, :, :, cols], w_in[0][:, :, :, cols], w_r[0][:, :, :, cols].bitcast(F32), ALU.subtract).then_inc(m_low, 1)

                def rows_low(j, u):
                    dve.wait_ge(m_xtc, 2 * j + 1)
                    dve.tensor_tensor(x_r[u][1], ps[:, 4, 0:DC * BS].rearrange("p (c s) -> p c s", c=DC), x_r[u][0].bitcast(F32),
                                      ALU.subtract).then_inc(m_xtc, 1)

                def halve(u, i):
                    dve.wait_ge(m_w_out[u], (i + 1) * 16)
                    dve.tensor_scalar(half_b[u], bcols[u][:, 1, :], 0.5, None, ALU.mult).then_inc(m_biased, 1)

                halve(0, 0)
                rows_low(0, 0)

                def step(j, u, i):
                    dve.wait_ge(m_rows[u], (i + 1) * 16)
                    dve.wait_ge(m_x[u], (i + 1) * 16)
                    dve.tensor_tensor(biased[u], x_in[u], rows[u][:, 0:D].unsqueeze(1).broadcast_to([128, HALVES, D]), ALU.add).then_inc(m_biased, 1)
                    at_least(dve, m_out, j - 1)
                    for f in range(FC):
                        dve.wait_ge(m_gate, j * FC + f + 1)
                        dve.scalar_tensor_tensor(hid[u][:, f, :], tanh[f % 2], 1.0, gelu[f % 2], ALU.add, ALU.mult).then_inc(m_act, 1)
                    if not isinstance(j, int) or j < BLOCKS - 1:
                        rows_low(j + 1, 1 - u)
                        halve(1 - u, i + u)
                    dve.wait_ge(m_out, j + 1)
                    dve.wait_ge(m_biased, 2 * j + 2)
                    for q in range(HALVES):
                        dve.scalar_tensor_tensor(res[:, q, :], ps[:, 5 + u, q * D:(q + 1) * D], 0.5, biased[u][:, q, :],
                                                 ALU.mult, ALU.add).then_inc(m_res, 1)
                    for q in range(HALVES):
                        dve.wait_ge(m_res, j * HALVES + q + 1)
                        dve.bn_stats(stats[:, q, :], res[:, q, :]).then_inc(m_norm, 1)
                    dve.wait_ge(m_norm, (2 * j + 1) * HALVES)
                    dve.memset(spare, 0.0)
                    for q in range(HALVES):
                        dve.bn_aggr(moments[:, q, :], stats[:, q, :]).then_inc(m_aggr, 1)
                    dve.wait_ge(m_aggr, (j + 1) * HALVES)
                    for q in range(HALVES):
                        dve.scalar_tensor_tensor(res[:, q, :], res[:, q, :], moments[:, q, 0:1], rows[u][:, D:2 * D],
                                                 ALU.subtract, ALU.mult).then_inc(m_norm, 1)
                    dve.wait_ge(m_norm, (2 * j + 2) * HALVES)
                    dve.wait_ge(m_rstd, 2 * j + 2)
                    at_least(dve, m_stored[u], i * 16)
                    for q in range(HALVES):
                        dve.scalar_tensor_tensor(y[u][:, q, :], res[:, q, :], rstd[:, q:q + 1], rows[u][:, 2 * D:3 * D],
                                                 ALU.mult, ALU.add).then_inc(m_y, 1)

                over_blocks(dve, step)
                for b in range(B):
                    fetch, before_it = fetched[b % RING]
                    dve.wait_ge(fetch, before_it + 32 * (b // RING + 1))
                    for k in range(2):
                        at_least(dve, m_added, 2 * b + k)
                        dve.scalar_tensor_tensor(x[:, b, :], got[b % RING][:, k * D:(k + 1) * D], coef[:, k, b:b + 1], x[:, b, :],
                                                 ALU.mult, ALU.add).then_inc(m_added, 1)

            stage(sync, gpsimd, scalar, vector, tensor)

        stored = sem("stored")

        def chain():
            norm_stage(x, 1e-5)
            w = query_stage(0, 1, x, gates[0:T, 0:1], keys_of=0)
            cross_stage(0, w, 0.25, x, gates[0:T, 0:1])
            norm_stage(x, 1e-5)
            position_experts_stage(4)
            norm_stage(x, 1e-5)
            w = query_stage(1, 1, x, gates[0:T, 1:2], keys_of=1)
            cross_stage(1, w, 0.25, x, gates[0:T, 1:2])
            norm_stage(x, 1e-5)
            lora_experts_stage(5)
            norm_stage(x, 1e-5, keep=h)
            w = query_stage(2, 2, h, one[0:T, :])
            self_stage(2, w, 0.25, h, one[0:T, :])
            norm_stage(h, 1e-6, gain=0, keep=h)
            w = query_stage(3, 1, h, one[0:T, :], keys_of=2)
            cross_stage(2, w, 0.25, h, one[0:T, :])
            norm_stage(h, 1e-6, gain=2, keep=h)
            relu_stage()
            norm_stage(h, 1e-6, gain=4, turn=False, add_gate=2)
            norm_stage(x, 1e-5)
            product_key_stage(6)
            norm_stage(x, 1e-5)
            w = query_stage(4, 1, x, gates[0:T, 3:4], keys_of=3)
            cross_stage(3, w, float(np.log(D) / np.sqrt(DH)), x, gates[0:T, 3:4], masked=True)
            norm_stage(x, 1e-5, keep=h)
            routed_experts_stage(7)

        chain()

        @block.sync
        def _(sp):
            for program in programs["sync"]:
                program(sp)

        @block.gpsimd
        def _(pool):
            for program in programs["gpsimd"]:
                program(pool)

        @block.scalar
        def _(act):
            for program in programs["scalar"]:
                program(act)

        @block.vector
        def _(dve):
            for program in programs["vector"]:
                program(dve)

        @block.tensor
        def _(pe):
            for program in programs["tensor"]:
                program(pe)


def kernel(**inputs):
    import concourse.bacc as bacc
    from concourse.bass_utils import run_bass_kernel_spmd

    i = {k: np.asarray(v) for k, v in inputs.items()}

    def rows_first(w):
        return w.reshape(-1, 128, w.shape[-1]).transpose(1, 0, 2)

    def columns(v):
        return v.reshape(-1, 128).T

    def attn_set(names, turned):
        return np.stack([rows_first(i[n].T if turned else i[n]) for n in names], axis=1)

    sets = []
    for layer, names, turned in (("L0_xattn_", ("Wq", "Wk", "Wv", "Wo"), True), ("L1_xattn_", ("Wq", "Wk", "Wv", "Wo"), True),
                                 ("L2_xattn_", ("wq1", "wk1", "wv1", "wo1"), False), ("L2_xattn_", ("wq2", "wk2", "wv2", "wo2"), False),
                                 ("L3_xattn_", ("Wq", "Wk", "Wv", "Wo"), True)):
        sets.append(([layer + n for n in names], [layer + "b" + n[1:] for n in names], turned))
    arrays = {
        "x": i["x"],
        "g_xattn": i["g_xattn"],
        "g_ffn": i["g_ffn"],
        "ctx_t": i["ctx_1024"].transpose(0, 2, 1).reshape(B, DC, 128, S2).transpose(0, 2, 1, 3),
        "attn_w": np.stack([attn_set(w, turned) for w, _, turned in sets]),
        "attn_cols": np.stack([np.concatenate([columns(i[b[0]]), columns(i[b[1]])], axis=1) for _, b, _ in sets]),
        "attn_rows": np.stack([np.stack([i[b[2]], i[b[3]]]) for _, b, _ in sets]),
        "am": i["mask_1x1xSxS_fk0"],
        "pm": i["mask_Bx1x1xS_ff1"],
        "mask": i["mask_Bx1xSxS2_if1"].reshape(B, T, S2),
        "pad": i["mask_BxS2_if1"],
        "ln_rows": np.stack([i["L2_xattn_" + n] for n in ("g1", "be1", "g2", "be2", "g3", "be3")]),
        "e0_w1": i["L0_ffn_w1"].reshape(E, DC, 128, F0).transpose(0, 2, 1, 3),
        "e0_w3": i["L0_ffn_w3"].reshape(E, DC, 128, F0).transpose(0, 2, 1, 3),
        "e0_w2": i["L0_ffn_w2"][:, 0:512].reshape(E, 4, 128, D).transpose(0, 2, 1, 3),
        "e0_w2r": i["L0_ffn_w2"][:, 512:].reshape(E, 2, 96, D).transpose(0, 2, 1, 3),
        "e1_router": rows_first(i["L1_ffn_gate_w"].T),
        "e1_gate": rows_first(i["L1_ffn_w_gate"].T),
        "e1_up": rows_first(i["L1_ffn_w_up"].T),
        "e1_down": rows_first(i["L1_ffn_w_down"].T),
        "e1_a1": rows_first(i["L1_ffn_A1"].reshape(ER, D).T),
        "e1_a3": rows_first(i["L1_ffn_A3"].reshape(ER, D).T),
        "e1_b1": i["L1_ffn_B1"].transpose(0, 2, 1).reshape(ER, F),
        "e1_b3": i["L1_ffn_B3"].transpose(0, 2, 1).reshape(ER, F),
        "e1_a2": rows_first(i["L1_ffn_A2"].reshape(ER, F).T),
        "e1_b2": i["L1_ffn_B2"].transpose(0, 2, 1).reshape(ER, D),
        "r_w1": rows_first(i["L2_xattn_w_ff1"]),
        "r_b1": columns(i["L2_xattn_b_ff1"]),
        "r_w2": rows_first(i["L2_xattn_w_ff2"]),
        "r_b2": i["L2_xattn_b_ff2"],
        "p_gate": rows_first(i["L2_ffn_Wg"]),
        "p_up": rows_first(i["L2_ffn_Wu"]),
        "p_down": rows_first(i["L2_ffn_Wd"]),
        "p_bcols": np.stack([columns(i["L2_ffn_bg"]), columns(i["L2_ffn_bu"])], axis=1),
        "p_bd": i["L2_ffn_bd"],
        "p_q": rows_first(i["L2_ffn_Wq"]),
        "p_keys": i["L2_ffn_keys"].transpose(2, 0, 3, 1).reshape(4, 128, PK).transpose(1, 0, 2),
        "p_down_e": rows_first(i["L2_ffn_down_embed"].T),
        "p_up_e": rows_first(i["L2_ffn_up_embed"]),
        "m_router": rows_first(i["L3_ffn_Wr"]),
        "m_br": i["L3_ffn_br"],
        "m_w_in": np.concatenate([np.concatenate([rows_first(i["L3_ffn_Wi"][e]).reshape(128, -1), rows_first(i["L3_ffn_Wg"][e]).reshape(128, -1)],
                                                 axis=1) for e in range(E)]),
        "m_w_out": np.concatenate([np.concatenate([rows_first(i["L3_ffn_Wo"][e]).reshape(128, -1), columns(i["L3_ffn_bi"][e]),
                                                   columns(i["L3_ffn_bg"][e])], axis=1) for e in range(E)]),
        "m_rows": np.concatenate([i["L3_ffn_bo"], i["L3_ffn_gamma"], i["L3_ffn_beta"]], axis=1),
    }
    nc = bacc.Bacc("TRN2", target_bir_lowering=False, num_devices=1)
    feeds, views = {}, {}
    for name, array in arrays.items():
        array = np.ascontiguousarray(array)
        feeds["in_" + name] = array
        views[name] = nc.dram_tensor("in_" + name, array.shape, mybir.dt.from_np(array.dtype), kind="ExternalInput").ap()
    views["out"] = nc.dram_tensor("out", (B, T, D), F32, kind="ExternalOutput").ap()
    build(nc, views)
    result = run_bass_kernel_spmd(nc, [feeds], core_ids=[0])
    return result.results[0]["out"]
```
